# Optimizing a Trainium2 kernel written in Bass

```python
import numpy as np
import jax
import jax.numpy as jnp

def _softmax(x, axis=-1):
    return jax.nn.softmax(x, axis=axis)

def _gelu(x):
    return jax.nn.gelu(x, approximate=True)

def _silu(x):
    return jax.nn.silu(x)

def _sigmoid(x):
    return jax.nn.sigmoid(x)

def _layernorm(x, axis=-1, eps=1e-05):
    m = jnp.mean(x, axis=axis, keepdims=True)
    v = jnp.var(x, axis=axis, keepdims=True)
    return (x - m) / jnp.sqrt(v + eps)

def _scatter_add(tgt, idx, src, axis=0):
    return tgt.at[idx].add(src)

def _segment_sum(src, seg, n):
    return jax.ops.segment_sum(src, seg, n)
kernel_name = 'mk_hybrid_d1_jaxref_r8_3d8558'

def setup_inputs(seed: int=0):
    np.random.seed(seed)
    _w = jnp.asarray

    def _L0_attn_a_setup():
        import jax, jax.numpy as jnp
        import numpy as np
        INFTY_APPROX = 1e+30
        ROTARY_BASE = 10000.0
        D_HEAD = 128

        def rope(x):
            *_, length, width = x.shape
            half = width // 2
            positions = jnp.arange(length)[:, None].astype(x.dtype)
            dims = jnp.arange(half).astype(x.dtype)
            ang_freqs = jnp.power(ROTARY_BASE, -dims / half)[None, :]
            radians = positions * ang_freqs
            cos = jnp.cos(radians)[None, None].astype(x.dtype)
            sin = jnp.sin(radians)[None, None].astype(x.dtype)
            even, odd = jnp.split(x, 2, axis=-1)
            r_even = even * cos - odd * sin
            r_odd = even * sin + odd * cos
            return jnp.concatenate([r_even, r_odd], axis=-1)
        key = jax.random.key(seed)
        ks = jax.random.split(key, 5)
        B, T, M, D = (4, 256, 128, D_HEAD)
        H = M // D
        x = jax.random.normal(ks[0], (B, T, M), dtype=jnp.float32)
        scale = M ** (-0.5)
        wq = jax.random.normal(ks[1], (H, M, D), dtype=jnp.float32) * scale
        wk = jax.random.normal(ks[2], (H, M, D), dtype=jnp.float32) * scale
        wv = jax.random.normal(ks[3], (H, M, D), dtype=jnp.float32) * scale
        wo = jax.random.normal(ks[4], (H, D, M), dtype=jnp.float32) * scale
        return {'x': x, 'wq': wq, 'wk': wk, 'wv': wv, 'wo': wo}
    _L0_attn_a_in = _L0_attn_a_setup()

    def _L0_attn_b_setup():
        import jax, jax.numpy as jnp
        import numpy as np
        B, S, HID = (2, 256, 128)
        H, D = (16, 64)
        KD = H * D
        RMS_EPS = 1e-05
        L2_EPS = 1e-12

        def _l2norm(t):
            n = jnp.sqrt(jnp.sum(t * t, axis=-1, keepdims=True))
            return t / jnp.clip(n, L2_EPS)
        key = jax.random.key(seed)
        ks = jax.random.split(key, 9)
        w = lambda k, shape: jax.random.normal(k, shape, jnp.float32) * 0.02
        return {'x': jax.random.normal(ks[0], (B, S, HID), jnp.float32), 'Wq': w(ks[1], (HID, KD)), 'Wk': w(ks[2], (HID, KD)), 'Wv': w(ks[3], (HID, KD)), 'Wf': w(ks[4], (HID, KD)), 'Wb': w(ks[5], (HID, H)), 'A_log': jnp.log(jnp.full((H,), 8.0, jnp.float32)), 'dt_bias': jnp.zeros((KD,), jnp.float32), 'Wg': w(ks[6], (HID, KD)), 'bg': jnp.zeros((KD,), jnp.float32), 'Wo': w(ks[7], (KD, HID)), 'norm_w': jnp.ones((D,), jnp.float32)}
    _L0_attn_b_in = _L0_attn_b_setup()

    def _L0_ffn_setup():
        import jax, jax.numpy as jnp
        import numpy as np
        DIM = 128

        def _reference_tuple_inner(x, W_r, W_k, W_v, mu_r, mu_k):
            B, T, C = x.shape
            x_prev = jnp.concatenate([jnp.zeros((B, 1, C), x.dtype), x[:, :-1, :]], axis=1)
            xr = mu_r * x + (1.0 - mu_r) * x_prev
            xk = mu_k * x + (1.0 - mu_k) * x_prev
            r = jax.nn.sigmoid(jnp.einsum('btc,dc->btd', xr, W_r))
            k = jnp.einsum('btc,dc->btd', xk, W_k)
            k_act = jnp.square(jax.nn.relu(k))
            out = r * jnp.einsum('btc,dc->btd', k_act, W_v)
            new_state = x[:, -1, :]
            return (out, new_state)
        key = jax.random.key(seed)
        ks = jax.random.split(key, 6)
        B, T, C = (8, 256, DIM)
        x = jax.random.normal(ks[0], (B, T, C), dtype=jnp.float32)
        s = 1.0 / np.sqrt(C)
        W_r = jax.random.uniform(ks[1], (C, C), jnp.float32, -s, s)
        W_k = jax.random.uniform(ks[2], (C, C), jnp.float32, -s, s)
        W_v = jax.random.uniform(ks[3], (C, C), jnp.float32, -s, s)
        mu_r = jax.random.uniform(ks[4], (C,), jnp.float32)
        mu_k = jax.random.uniform(ks[5], (C,), jnp.float32)
        return {'x': x, 'W_r': W_r, 'W_k': W_k, 'W_v': W_v, 'mu_r': mu_r, 'mu_k': mu_k}
    _L0_ffn_in = _L0_ffn_setup()
    _d = {'L0_attn_a_x': _L0_attn_a_in['x'], 'L0_attn_a_wq': _L0_attn_a_in['wq'], 'L0_attn_a_wk': _L0_attn_a_in['wk'], 'L0_attn_a_wv': _L0_attn_a_in['wv'], 'L0_attn_a_wo': _L0_attn_a_in['wo'], 'L0_attn_b_Wq': _L0_attn_b_in['Wq'], 'L0_attn_b_Wk': _L0_attn_b_in['Wk'], 'L0_attn_b_Wv': _L0_attn_b_in['Wv'], 'L0_attn_b_Wf': _L0_attn_b_in['Wf'], 'L0_attn_b_Wb': _L0_attn_b_in['Wb'], 'L0_attn_b_A_log': _L0_attn_b_in['A_log'], 'L0_attn_b_dt_bias': _L0_attn_b_in['dt_bias'], 'L0_attn_b_Wg': _L0_attn_b_in['Wg'], 'L0_attn_b_bg': _L0_attn_b_in['bg'], 'L0_attn_b_Wo': _L0_attn_b_in['Wo'], 'L0_attn_b_norm_w': _L0_attn_b_in['norm_w'], 'L0_ffn_W_r': _L0_ffn_in['W_r'], 'L0_ffn_W_k': _L0_ffn_in['W_k'], 'L0_ffn_W_v': _L0_ffn_in['W_v'], 'L0_ffn_mu_r': _L0_ffn_in['mu_r'], 'L0_ffn_mu_k': _L0_ffn_in['mu_k']}
    _x0 = _d['L0_attn_a_x']
    _d['L0_attn_a_x'] = jax.random.normal(jax.random.fold_in(jax.random.key(seed), 1), (2, 2048, 128), dtype=_x0.dtype)
    del _x0
    return _d

def reference(L0_attn_a_x, L0_attn_a_wq, L0_attn_a_wk, L0_attn_a_wv, L0_attn_a_wo, L0_attn_b_Wq, L0_attn_b_Wk, L0_attn_b_Wv, L0_attn_b_Wf, L0_attn_b_Wb, L0_attn_b_A_log, L0_attn_b_dt_bias, L0_attn_b_Wg, L0_attn_b_bg, L0_attn_b_Wo, L0_attn_b_norm_w, L0_ffn_W_r, L0_ffn_W_k, L0_ffn_W_v, L0_ffn_mu_r, L0_ffn_mu_k):

    def _L0_attn_a_ref(x, wq, wk, wv, wo):
        import jax, jax.numpy as jnp
        import numpy as np
        INFTY_APPROX = 1e+30
        ROTARY_BASE = 10000.0
        D_HEAD = 128

        def rope(x):
            *_, length, width = x.shape
            half = width // 2
            positions = jnp.arange(length)[:, None].astype(x.dtype)
            dims = jnp.arange(half).astype(x.dtype)
            ang_freqs = jnp.power(ROTARY_BASE, -dims / half)[None, :]
            radians = positions * ang_freqs
            cos = jnp.cos(radians)[None, None].astype(x.dtype)
            sin = jnp.sin(radians)[None, None].astype(x.dtype)
            even, odd = jnp.split(x, 2, axis=-1)
            r_even = even * cos - odd * sin
            r_odd = even * sin + odd * cos
            return jnp.concatenate([r_even, r_odd], axis=-1)
        q = jnp.einsum('bim,hmd->bhid', x, wq)
        k = jnp.einsum('bim,hmd->bhid', x, wk)
        v = jnp.einsum('bim,hmd->bhid', x, wv)
        q = rope(q)
        k = rope(k)
        mult = jnp.asarray(D_HEAD ** (-0.5), dtype=x.dtype)
        s = jnp.einsum('bhid,bhjd->bhij', q * mult, k * mult)
        T = s.shape[-1]
        i = jnp.arange(T)[:, None]
        j = jnp.arange(T)[None, :]
        mask = (i < j).astype(s.dtype)[None, None]
        s = s - jnp.asarray(INFTY_APPROX, dtype=s.dtype) * mask
        p = jax.nn.softmax(s, axis=-1)
        o = jnp.einsum('bhij,bhjd->bhid', p, v)
        r = jnp.einsum('bhid,hdm->bim', o, wo)
        return r

    def _L0_attn_b_ref(x, Wq, Wk, Wv, Wf, Wb, A_log, dt_bias, Wg, bg, Wo, norm_w):
        import jax, jax.numpy as jnp
        import numpy as np
        B, S, HID = (2, 256, 128)
        H, D = (16, 64)
        KD = H * D
        RMS_EPS = 1e-05
        L2_EPS = 1e-12

        def _l2norm(t):
            n = jnp.sqrt(jnp.sum(t * t, axis=-1, keepdims=True))
            return t / jnp.clip(n, L2_EPS)
        b, s, _ = x.shape
        h = A_log.shape[0]
        d = norm_w.shape[0]
        q = jax.nn.silu(x @ Wq).reshape(b, s, h, d)
        k = jax.nn.silu(x @ Wk).reshape(b, s, h, d)
        v = jax.nn.silu(x @ Wv).reshape(b, s, h, d)
        g = (x @ Wf).reshape(b, s, h, d)
        beta = jax.nn.sigmoid(x @ Wb)
        q = _l2norm(q)
        k = _l2norm(k)
        g = jax.nn.sigmoid(g - dt_bias.reshape(h, d))
        A = jnp.exp(-jnp.exp(A_log))
        qs = jnp.moveaxis(q, 1, 0)
        kss = jnp.moveaxis(k, 1, 0)
        vs = jnp.moveaxis(v, 1, 0)
        gs = jnp.moveaxis(g, 1, 0)
        bs = jnp.moveaxis(beta, 1, 0)
        state0 = jnp.zeros((b, h, d, d), x.dtype)

        def step(state, inp):
            q_t, k_t, v_t, g_t, b_t = inp
            o_t = jnp.einsum('bhd,bhde->bhe', q_t, state) * g_t
            state = A[None, :, None, None] * state + b_t[..., None, None] * (k_t[..., :, None] * v_t[..., None, :])
            return (state, o_t)
        _, o = jax.lax.scan(step, state0, (qs, kss, vs, gs, bs))
        o = jnp.moveaxis(o, 0, 1)
        o = o * jax.lax.rsqrt(jnp.mean(o * o, axis=-1, keepdims=True) + RMS_EPS) * norm_w
        gate = jax.nn.sigmoid(x @ Wg + bg).reshape(b, s, h, d)
        o = (o * gate).reshape(b, s, h * d)
        return o @ Wo

    def _L0_ffn_ref(x, W_r, W_k, W_v, mu_r, mu_k):
        import jax, jax.numpy as jnp
        import numpy as np
        DIM = 128

        def _reference_tuple_inner(x, W_r, W_k, W_v, mu_r, mu_k):
            B, T, C = x.shape
            x_prev = jnp.concatenate([jnp.zeros((B, 1, C), x.dtype), x[:, :-1, :]], axis=1)
            xr = mu_r * x + (1.0 - mu_r) * x_prev
            xk = mu_k * x + (1.0 - mu_k) * x_prev
            r = jax.nn.sigmoid(jnp.einsum('btc,dc->btd', xr, W_r))
            k = jnp.einsum('btc,dc->btd', xk, W_k)
            k_act = jnp.square(jax.nn.relu(k))
            out = r * jnp.einsum('btc,dc->btd', k_act, W_v)
            new_state = x[:, -1, :]
            return (out, new_state)
        return _reference_tuple_inner(x, W_r, W_k, W_v, mu_r, mu_k)[0]
    x = L0_attn_a_x
    x = x + _L0_attn_a_ref(_layernorm(x, axis=-1), L0_attn_a_wq, L0_attn_a_wk, L0_attn_a_wv, L0_attn_a_wo)
    x = x + _L0_ffn_ref(_layernorm(x, axis=-1), L0_ffn_W_r, L0_ffn_W_k, L0_ffn_W_v, L0_ffn_mu_r, L0_ffn_mu_k)
    x = x + _L0_attn_b_ref(_layernorm(x, axis=-1), L0_attn_b_Wq, L0_attn_b_Wk, L0_attn_b_Wv, L0_attn_b_Wf, L0_attn_b_Wb, L0_attn_b_A_log, L0_attn_b_dt_bias, L0_attn_b_Wg, L0_attn_b_bg, L0_attn_b_Wo, L0_attn_b_norm_w)
    x = x + _L0_ffn_ref(_layernorm(x, axis=-1), L0_ffn_W_r, L0_ffn_W_k, L0_ffn_W_v, L0_ffn_mu_r, L0_ffn_mu_k)
    return x

_drawn_inputs = setup_inputs


def setup_inputs(seed=0):
    import zlib

    import numpy as np

    out = dict(_drawn_inputs(seed))
    spreads = {'L0_attn_b_A_log': (2.079441547393799, 0.6),
     'L0_attn_b_dt_bias': (0.0, 0.779),
     'L0_attn_b_bg': (0.0, 0.799),
     'L0_attn_b_norm_w': (1.0, 0.2)}
    factors = {'L0_attn_a_wq': 7.947,
     'L0_attn_a_wk': 7.675,
     'L0_attn_b_Wb': 4.985,
     'L0_ffn_mu_r': 3.171,
     'L0_attn_b_Wf': 3.359,
     'L0_attn_b_Wg': 3.281}
    for name, (base, spread) in spreads.items():
        noise = np.random.default_rng([zlib.crc32(name.encode()), seed]).standard_normal(out[name].shape)
        drawn = base * np.exp(spread * noise) if base else spread * noise
        out[name] = jnp.asarray(drawn.astype(out[name].dtype))
    for name, factor in factors.items():
        out[name] = (out[name] * factor).astype(out[name].dtype)
    return out
```

```python
from contextlib import ExitStack

import numpy as np

import concourse.bass as bass
from concourse import mybir

F32 = mybir.dt.float32
F32R = mybir.dt.float32r
ALU = mybir.AluOpType
ACT = mybir.ActivationFunctionType
AX = mybir.AxisListType

P = 128
B, T, C = 2, 2048, 128
NT = T // P
GT = 4
G = GT * P
NG = T // G
H, D = 16, 64
HD = H * D
NP = H // 2
ROTARY_BASE = 10000.0
LN_EPS = 1e-5
RMS_EPS = 1e-5
L2_EPS = 1e-12
NEG = -1e30
HALVES = HD // G

C_IDENT, C_LAG, C_STRICT, C_NEG, C_TPOS = (k * P for k in range(5))
C_LEFT = 5 * P
C_WIDTH = 5 * P + 1


def bank_sems(sem, name, n):
    return [sem(f"{name}{k}") for k in range(n)]


def qkv_phase(nc, io, X, const, qk_hi, qk_lo, V):
    ctx = ExitStack()
    with ctx:
        sb = lambda name, shape, dt=F32: ctx.enter_context(nc.sbuf_tensor("qkv_" + name, shape, dt))
        sem = lambda name: ctx.enter_context(nc.semaphore("qkv_" + name))
        ident = const[:, C_IDENT:C_IDENT + P]
        cos = sb("cos", [P, T])
        sin = sb("sin", [P, T])
        w = sb("w", [P, 5, P])
        w_hi = sb("w_hi", [P, 4, P], F32R)
        w_lo = sb("w_lo", [P, 4, P], F32R)
        stats = sb("stats", [P, 2, GT, 6])
        mv = sb("mv", [P, 2, GT, 2])
        rstd = sb("rstd", [P, 2, GT])
        mhalf = sb("mhalf", [P, GT])
        eps = sb("eps", [P, GT])
        held = sb("held", [P, 1])
        xn = sb("xn", [P, 2, G])
        xT = sb("xT", [P, 2, G])
        x_hi = sb("x_hi", [P, 2, G], F32R)
        x_lo = sb("x_lo", [P, 2, G], F32R)
        by_cos = sb("by_cos", [P, 2, G])
        by_sin = sb("by_sin", [P, 2, G])
        rot = sb("rot", [P, 2, G])
        xt_ps = ctx.enter_context(nc.psum_tensor("qkv_xt_ps", [P, G], F32))
        pr_ps = [ctx.enter_context(nc.psum_tensor(f"qkv_pr_ps{k}", [P, G], F32)) for k in range(4)]
        v_ps = ctx.enter_context(nc.psum_tensor("qkv_v_ps", [P, G], F32))

        loaded_x, loaded_w, loaded_const, loaded_rope = (sem(n) for n in ("loaded_x", "loaded_w", "loaded_const", "loaded_rope"))
        weights_split = sem("weights_split")
        w_hi_ready = sem("w_hi_ready")
        mhalf_set = sem("mhalf_set")
        stats_ready, moments_ready, rstd_step, xn_ready = (sem(n) for n in ("stats_ready", "moments_ready", "rstd_step", "xn_ready"))
        xt_full, xt_copied, xlo_ready = (sem(n) for n in ("xt_full", "xt_copied", "xlo_ready"))
        pr_full = bank_sems(sem, "pr_full", 4)
        pr_read = bank_sems(sem, "pr_read", 4)
        rot_ready, rot_hi = bank_sems(sem, "rot_ready", 2), bank_sems(sem, "rot_hi", 2)
        rot_lo = sem("rot_lo")
        v_full, v_read = sem("v_full"), sem("v_read")

        block = ctx.enter_context(nc.Block())

        def tile_of(i, b, j):
            return b * NT + i * GT + j

        @block.sync
        def _(eng):
            eng.dma_start(const[:, :], io["const"]).then_inc(loaded_const, 16)
            for i in range(NG):
                for b in range(B):
                    src = io["x"][b, i * G:(i + 1) * G, :].rearrange("(t p) c -> p t c", p=P)
                    t0 = tile_of(i, b, 0)
                    eng.dma_start(X[:, t0:t0 + GT, :], src).then_inc(loaded_x, 16)
                    if i == 0 and b == 0:
                        eng.dma_start(w[:, :, :], io["w_qkv"]).then_inc(loaded_w, 16)
                        eng.dma_start(cos[:, :], io["cos"]).then_inc(loaded_rope, 16)
                        eng.dma_start(sin[:, :], io["sin"]).then_inc(loaded_rope, 16)
                    eng.wait_ge(loaded_x, 16 * (2 * i + b + 1))

        @block.gpsimd
        def _(eng):
            eng.memset(mhalf[:, :], -0.5).then_inc(mhalf_set, 1)
            eng.memset(eps[:, :], LN_EPS).then_inc(mhalf_set, 1)
            eng.wait_ge(loaded_w, 16)
            eng.wait_ge(w_hi_ready, 1)
            eng.tensor_tensor(w_lo[:, :, :], w[:, 0:4, :], w_hi[:, :, :].bitcast(F32), ALU.subtract).then_inc(weights_split, 1)
            eng.wait_ge(mhalf_set, 2)

            def rstds(g, b):
                eng.wait_ge(moments_ready, GT * (g + 1))
                eng.tensor_tensor(rstd[:, b, :], mv[:, b, :, 1], eps[:, :], ALU.add).then_inc(rstd_step, 1)
                eng.wait_ge(rstd_step, 2 * g + 1)
                eng.tensor_tensor(rstd[:, b, :], rstd[:, b, :], mhalf[:, :], ALU.pow).then_inc(rstd_step, 1)

            def rotated(i, b, r):
                g = 2 * i + b
                eng.wait_ge(pr_read[2 * r], g + 1)
                eng.wait_ge(pr_read[2 * r + 1], g + 1)
                eng.tensor_tensor(rot[:, r, :], by_cos[:, r, :], by_sin[:, r, :], ALU.add).then_inc(rot_ready[r], 1)
                eng.wait_ge(rot_hi[r], g + 1)
                at = (r * B + b) * T + i * G
                eng.tensor_tensor(qk_lo[:, bass.ds(at, G)], rot[:, r, :],
                                  qk_hi[:, bass.ds(at, G)].bitcast(F32), ALU.subtract).then_inc(rot_lo, 1)

            rstds(0, 0)
            with eng.Fori(0, NG - 1) as i:
                rstds(2 * i + 1, 1)
                rotated(i, 0, 0)
                rotated(i, 0, 1)
                rstds(2 * i + 2, 0)
                rotated(i, 1, 0)
                rotated(i, 1, 1)
            rstds(2 * NG - 1, 1)
            for b in range(B):
                for r in range(2):
                    rotated(NG - 1, b, r)

        @block.vector
        def _(eng):
            def moments(i, b):
                g = 2 * i + b
                eng.wait_ge(loaded_x, 16 * (g + 1))
                for j in range(GT):
                    eng.bn_stats(stats[:, b, j, :], X[:, bass.ds(tile_of(i, b, j), 1), :]).then_inc(stats_ready, 1)
                eng.wait_ge(stats_ready, GT * g + GT)
                eng.memset(held[:, :], 0.0)
                for j in range(GT):
                    eng.bn_aggr(mv[:, b, j, :], stats[:, b, j, :]).then_inc(moments_ready, 1)

            def normalize(i, b):
                g = 2 * i + b
                eng.wait_ge(rstd_step, 2 * g + 2)
                for j in range(GT):
                    eng.tensor_scalar(xn[:, b, j * P:(j + 1) * P], X[:, bass.ds(tile_of(i, b, j), 1), :],
                                      mv[:, b, j, 0:1], rstd[:, b, j:j + 1], ALU.subtract, ALU.mult).then_inc(xn_ready, 1)

            def low_x(g, b):
                eng.wait_ge(xt_copied, 2 * g + 2)
                eng.tensor_tensor(x_lo[:, b, :], xT[:, b, :], x_hi[:, b, :].bitcast(F32), ALU.subtract).then_inc(xlo_ready, 1)

            def products(i, b, r, first=False):
                g = 2 * i + b
                if not first:
                    eng.wait_ge(rot_ready[r], g)
                for k, (prod, table) in enumerate(((by_cos, cos), (by_sin, sin))):
                    eng.wait_ge(pr_full[2 * r + k], g + 1)
                    eng.tensor_tensor(prod[:, r, :], pr_ps[2 * r + k][:, :], table[:, bass.ds(i * G, G)],
                                      ALU.mult).then_inc(pr_read[2 * r + k], 1)

            moments(0, 0)
            normalize(0, 0)
            eng.wait_ge(loaded_rope, 32)

            def group(i, b, nxt, first=False):
                if nxt:
                    moments(*nxt)
                low_x(2 * i + b, b)
                products(i, b, 0, first)
                if nxt:
                    normalize(*nxt)
                products(i, b, 1, first)

            group(0, 0, (0, 1), first=True)
            group(0, 1, (1, 0))
            with eng.Fori(1, NG - 1) as i:
                group(i, 0, (i, 1))
                group(i, 1, (i + 1, 0))
            group(NG - 1, 0, (NG - 1, 1))
            group(NG - 1, 1, None)

        @block.scalar
        def _(eng):
            eng.wait_ge(loaded_w, 16)
            eng.activation(w_hi[:, :, :], w[:, 0:4, :], ACT.Copy).then_inc(w_hi_ready, 1)

            def copy_x(g, b):
                eng.wait_ge(xt_full, g + 1)
                eng.activation(xT[:, b, :], xt_ps[:, :], ACT.Copy).then_inc(xt_copied, 1)
                eng.activation(x_hi[:, b, :], xt_ps[:, :], ACT.Copy).then_inc(xt_copied, 1)

            def high_part(i, b, r):
                eng.wait_ge(rot_ready[r], 2 * i + b + 1)
                at = (r * B + b) * T + i * G
                eng.activation(qk_hi[:, bass.ds(at, G)], rot[:, r, :], ACT.Copy).then_inc(rot_hi[r], 1)

            def group(i, b, nxt):
                g = 2 * i + b
                eng.wait_ge(v_full, g + 1)
                eng.activation(V[:, bass.ds(tile_of(i, b, 0), GT), :], v_ps[:, :].rearrange("p (t c) -> p t c", t=GT),
                               ACT.Copy).then_inc(v_read, 1)
                high_part(i, b, 0)
                if nxt:
                    copy_x(*nxt)
                high_part(i, b, 1)

            copy_x(0, 0)
            with eng.Fori(0, NG - 1) as i:
                group(i, 0, (2 * i + 1, 1))
                group(i, 1, (2 * i + 2, 0))
            group(NG - 1, 0, (2 * NG - 1, 1))
            group(NG - 1, 1, None)

        @block.tensor
        def _(eng):
            eng.wait_ge(loaded_const, 16)

            def turn_x(g, b, first=False):
                if not first:
                    eng.wait_ge(xt_copied, 2 * g)
                for j in range(GT):
                    eng.wait_ge(xn_ready, GT * g + j + 1)
                    mm = eng.transpose(xt_ps[:, j * P:(j + 1) * P], xn[:, b, j * P:(j + 1) * P], ident)
                mm.then_inc(xt_full, 1)

            def values(g, b, first=False):
                eng.wait_ge(xt_copied, 2 * g + 2)
                if not first:
                    eng.wait_ge(v_read, g)
                for j in range(GT):
                    mm = eng.matmul(v_ps[:, j * P:(j + 1) * P], xT[:, b, j * P:(j + 1) * P], w[:, 4, :], start=True, stop=True)
                mm.then_inc(v_full, 1)

            def project(g, b, r, first=False):
                eng.wait_ge(xlo_ready, g + 1)
                for k in (2 * r, 2 * r + 1):
                    if not first:
                        eng.wait_ge(pr_read[k], g)
                    eng.matmul(pr_ps[k][:, :], w_hi[:, k, :], x_hi[:, b, :], start=True, stop=False)
                    eng.matmul(pr_ps[k][:, :], w_lo[:, k, :], x_hi[:, b, :], start=False, stop=False)
                    eng.matmul(pr_ps[k][:, :], w_hi[:, k, :], x_lo[:, b, :], start=False, stop=True).then_inc(pr_full[k], 1)

            def group(g, b, nxt, first=False):
                values(g, b, first)
                project(g, b, 0, first)
                if nxt:
                    turn_x(*nxt)
                project(g, b, 1, first)

            turn_x(0, 0, first=True)
            eng.wait_ge(w_hi_ready, 1)
            eng.wait_ge(weights_split, 1)
            group(0, 0, (1, 1), first=True)
            group(1, 1, (2, 0))
            with eng.Fori(1, NG - 1) as i:
                group(2 * i, 0, (2 * i + 1, 1))
                group(2 * i + 1, 1, (2 * i + 2, 0))
            group(2 * NG - 2, 0, (2 * NG - 1, 1))
            group(2 * NG - 1, 1, None)


def attention_phase(nc, io, X, const, qk_hi, qk_lo, V, w5_hi, w5_lo):
    ctx = ExitStack()
    with ctx:
        sb = lambda name, shape, dt=F32: ctx.enter_context(nc.sbuf_tensor("at_" + name, shape, dt))
        sem = lambda name: ctx.enter_context(nc.semaphore("at_" + name))
        ident = const[:, C_IDENT:C_IDENT + P]
        causal = const[:, C_NEG:C_NEG + P]
        wo = sb("wo", [P, P])
        w5_raw = sb("w5_raw", [P, 2, HD])
        q_hi = sb("q_hi", [P, 2, P], F32R)
        q_lo = sb("q_lo", [P, 2, P], F32R)
        top = sb("top", [P, 2, GT])
        ntop = sb("ntop", [P, 2, 2])
        probs = sb("probs", [P, 2, T])
        probsT = sb("probsT", [P, 2, G])
        psums = sb("psums", [P, 2, GT])
        total = sb("total", [P, 2, 2])
        o_n = sb("o_n", [P, 2, P])
        oT = sb("oT", [P, 2, P])
        s_ps = ctx.enter_context(nc.psum_tensor("at_s_ps", [P, T], F32))
        t_ps = [ctx.enter_context(nc.psum_tensor(f"at_t_ps{k}", [P, G], F32)) for k in range(2)]
        o_ps = [ctx.enter_context(nc.psum_tensor(f"at_o_ps{k}", [P, G], F32)) for k in range(2)]

        wo_loaded = sem("wo_loaded")
        w5_loaded = bank_sems(sem, "w5_loaded", 2)
        w5_hi_done, w5_lo_done = sem("w5_hi_done"), sem("w5_lo_done")
        q_here = sem("q_here")
        s_full = bank_sems(sem, "s_full", NG)
        masked, top_ready, ntop_step = sem("masked"), sem("top_ready"), sem("ntop_step")
        exp_ready = sem("exp_ready")
        t_full = bank_sems(sem, "t_full", 2)
        t_read = bank_sems(sem, "t_read", 2)
        pv_used = sem("pv_used")
        o_full, total_step, o_ready = sem("o_full"), sem("total_step"), sem("o_ready")
        x_ready = sem("x_ready")

        block = ctx.enter_context(nc.Block())

        def blocks(n):
            return n // GT + 1

        BLK = [sum(blocks(m) for m in range(n)) for n in range(NT + 1)]
        BANK = [[sum(1 for m in range(n) if blocks(m) > k) for n in range(NT + 1)] for k in range(NG)]

        CREDIT = 1

        jobs = []
        for n in range(NT + 2):
            if n < NT:
                jobs += [("probs", n, j) for j in range(blocks(n))]
            if 1 <= n <= NT:
                jobs.append(("oT", n - 1, 0))
            if n >= 2:
                jobs.append(("wo", n - 2, 0))
        NJ = len(jobs)
        assert NJ % 2 == 0
        JOB = {job: k for k, job in enumerate(jobs)}

        def ring(b, job):
            k = JOB[job]
            return k % 2, b * (NJ // 2) + k // 2

        @block.sync
        def _(eng):
            eng.dma_start(wo[:, :], io["wo"]).then_inc(wo_loaded, 16)
            for k in range(5):
                if k >= 2:
                    eng.wait_ge(w5_lo_done, k - 1)
                eng.dma_start(w5_raw[:, k % 2, :], io["w5"][:, k * HD:(k + 1) * HD]).then_inc(w5_loaded[k % 2], 16)

        @block.gpsimd
        def _(eng):
            def bring_q(b, n):
                if n >= 2:
                    j = blocks(n - 2) - 1
                    eng.wait_ge(s_full[j], b * BANK[j][NT] + BANK[j][n - 2] + 1 + CREDIT)
                else:
                    eng.wait_ge(s_full[NG - 1], b * BANK[NG - 1][NT] + CREDIT)
                at = b * T + n * P
                eng.tensor_copy(q_hi[:, n % 2, :], qk_hi[:, bass.ds(at, P)]).then_inc(q_here, 1)
                eng.tensor_copy(q_lo[:, n % 2, :], qk_lo[:, bass.ds(at, P)]).then_inc(q_here, 1)

            def split_w5(k):
                eng.wait_ge(w5_loaded[k % 2], 16 * (k // 2 + 1))
                part = slice(k * HD, (k + 1) * HD)
                eng.tensor_copy(w5_hi[:, part], w5_raw[:, k % 2, :]).then_inc(w5_hi_done, 1)
                eng.wait_ge(w5_hi_done, k + 1)
                eng.tensor_tensor(w5_lo[:, part], w5_raw[:, k % 2, :], w5_hi[:, part].bitcast(F32),
                                  ALU.subtract).then_inc(w5_lo_done, 1)

            with eng.Fori(0, B) as b:
                for n in range(NT):
                    bring_q(b, n)
            for k in range(5):
                split_w5(k)

        @block.tensor
        def _(eng):
            eng.wait_ge(wo_loaded, 16)
            eng.sem_inc(o_full, CREDIT)
            for j in range(NG):
                eng.sem_inc(s_full[j], CREDIT)

            def scores(b, n):
                N = b * NT + n
                eng.wait_ge(q_here, 2 * N + 2)
                for j in range(blocks(n)):
                    used = BLK[n - 1] + j + 1 if n >= 1 and j < blocks(n - 1) else 0
                    eng.wait_ge(exp_ready, b * BLK[NT] + used + CREDIT)
                    width = G if j < n // GT else max(2 * P, (n % GT + 1) * P)
                    at = (B + b) * T + j * G
                    out = s_ps[:, j * G:j * G + width]
                    k_hi, k_lo = qk_hi[:, bass.ds(at, width)], qk_lo[:, bass.ds(at, width)]
                    eng.matmul(out, q_hi[:, n % 2, :], k_hi, start=True, stop=False)
                    eng.matmul(out, q_lo[:, n % 2, :], k_hi, start=False, stop=False)
                    eng.matmul(out, q_hi[:, n % 2, :], k_lo, start=False, stop=True).then_inc(s_full[j], 1)

            def wait_bank(b, job):
                k, before = ring(b, job)
                eng.wait_ge(t_read[k], before + CREDIT)
                return t_ps[k], t_full[k]

            def transposes(b, n, j):
                N = b * NT + n
                eng.wait_ge(exp_ready, b * BLK[NT] + BLK[n] + j + 1 + CREDIT)
                bank, full = wait_bank(b, ("probs", n, j))
                for t in range(min(GT, n + 1 - j * GT)):
                    mm = eng.transpose(bank[:, t * P:(t + 1) * P], probs[:, n % 2, (j * GT + t) * P:(j * GT + t + 1) * P], ident)
                mm.then_inc(full, 1)

            def values(b, n, j):
                N = b * NT + n
                k, before = ring(b, ("probs", n, j))
                eng.wait_ge(t_read[k], before + 1 + CREDIT)
                if j == 0:
                    if n >= 2:
                        eng.wait_ge(o_ready, N - 1 + CREDIT)
                    else:
                        eng.wait_ge(o_ready, b * NT + CREDIT)
                for t in range(min(GT, n + 1 - j * GT)):
                    kt = j * GT + t
                    mm = eng.matmul(o_ps[n % 2][:, 0:P], probsT[:, (BLK[n] + j) % 2, t * P:(t + 1) * P],
                                    V[:, bass.ds(b * NT + kt, 1), :], start=(kt == 0), stop=(kt == n))
                    if kt == n:
                        mm.then_inc(o_full, 1)
                    elif t == GT - 1:
                        mm.then_inc(pv_used, 1)

            def turn_o(b, n):
                eng.wait_ge(o_ready, b * NT + n + 1 + CREDIT)
                bank, full = wait_bank(b, ("oT", n, 0))
                eng.transpose(bank[:, 0:P], o_n[:, n % 2, :], ident).then_inc(full, 1)

            def project_o(b, n):
                k, before = ring(b, ("oT", n, 0))
                eng.wait_ge(t_read[k], before + 1 + CREDIT)
                bank, full = wait_bank(b, ("wo", n, 0))
                eng.matmul(bank[:, 0:P], oT[:, n % 2, :], wo[:, :], start=True, stop=True).then_inc(full, 1)

            with eng.Fori(0, B) as b:
                scores(b, 0)
                for n in range(NT + 2):
                    if n + 1 < NT:
                        scores(b, n + 1)
                    if n < NT:
                        transposes(b, n, 0)
                        for j in range(1, blocks(n)):
                            transposes(b, n, j)
                            values(b, n, j - 1)
                    if 1 <= n <= NT:
                        turn_o(b, n - 1)
                    if n < NT:
                        values(b, n, blocks(n) - 1)
                    if n >= 2:
                        project_o(b, n - 2)

        @block.vector
        def _(eng):
            def maxima(b, n):
                N = b * NT + n
                last = n // GT
                for j in range(blocks(n)):
                    eng.wait_ge(s_full[j], b * BANK[j][NT] + BANK[j][n] + 1 + CREDIT)
                    if j == last:
                        diag = s_ps[:, n * P:(n + 1) * P]
                        eng.tensor_tensor(diag, diag, causal, ALU.add).then_inc(masked, 1)
                        eng.wait_ge(masked, N + 1)
                    end = min((j + 1) * G, (n + 1) * P)
                    eng.tensor_reduce(top[:, n % 2, j:j + 1], s_ps[:, j * G:end], AX.X, ALU.max).then_inc(top_ready, 1)
                eng.wait_ge(top_ready, b * BLK[NT] + BLK[n + 1])
                eng.tensor_reduce(ntop[:, n % 2, 0:1], top[:, n % 2, 0:blocks(n)], AX.X, ALU.max, negate=True).then_inc(ntop_step, 1)
                eng.wait_ge(ntop_step, 2 * N + 1)
                eng.tensor_scalar(ntop[:, n % 2, 1:2], ntop[:, n % 2, 0:1], 1.0 / C, None, ALU.mult).then_inc(ntop_step, 1)

            def copy_probs(b, n, j):
                k, before = ring(b, ("probs", n, j))
                eng.wait_ge(t_full[k], before + 1)
                width = min(G, (n + 1) * P - j * G)
                m = BLK[n] + j
                if m >= 2:
                    pn, pj = JOBS_OF[m - 2]
                    if pj == blocks(pn) - 1:
                        eng.wait_ge(o_full, b * NT + pn + 1 + CREDIT)
                    else:
                        eng.wait_ge(pv_used, b * INNER[NT] + INNER[pn] + pj + 1)
                else:
                    eng.wait_ge(o_full, b * NT + CREDIT)
                eng.tensor_copy(probsT[:, m % 2, 0:width], t_ps[k][:, 0:width]).then_inc(t_read[k], 1)

            def sum_rows(b, n):
                N = b * NT + n
                eng.wait_ge(exp_ready, b * BLK[NT] + BLK[n + 1] + CREDIT)
                eng.tensor_reduce(total[:, n % 2, 0:1], psums[:, n % 2, 0:blocks(n)], AX.X, ALU.add).then_inc(total_step, 1)
                eng.wait_ge(total_step, 2 * N + 1)
                eng.reciprocal(total[:, n % 2, 1:2], total[:, n % 2, 0:1]).then_inc(total_step, 1)

            def copy_oT(b, n):
                k, before = ring(b, ("oT", n, 0))
                eng.wait_ge(t_full[k], before + 1)
                eng.tensor_copy(oT[:, n % 2, :], t_ps[k][:, 0:P]).then_inc(t_read[k], 1)

            def residual(b, n):
                k, before = ring(b, ("wo", n, 0))
                eng.wait_ge(t_full[k], before + 1)
                xt = X[:, bass.ds(b * NT + n, 1), :]
                eng.tensor_tensor(xt, t_ps[k][:, 0:P].rearrange("p (t c) -> p t c", t=1), xt, ALU.add).then_inc(t_read[k], 1)

            JOBS_OF = [(n, j) for n in range(NT) for j in range(blocks(n))]
            INNER = [sum(blocks(m) - 1 for m in range(n)) for n in range(NT + 1)]
            for k in range(2):
                eng.sem_inc(t_read[k], CREDIT)
            with eng.Fori(0, B) as b:
                maxima(b, 0)
                for n in range(NT + 2):
                    if n + 1 < NT:
                        maxima(b, n + 1)
                    if n < NT:
                        sum_rows(b, n)
                        for j in range(blocks(n)):
                            copy_probs(b, n, j)
                    if 1 <= n <= NT:
                        copy_oT(b, n - 1)
                    if n >= 2:
                        residual(b, n - 2)

        @block.scalar
        def _(eng):
            def exponentials(b, n):
                N = b * NT + n
                eng.wait_ge(ntop_step, 2 * N + 2)
                if n >= 2:
                    k, before = ring(b, ("probs", n - 2, blocks(n - 2) - 1))
                    eng.wait_ge(t_full[k], before + 1)
                else:
                    eng.wait_ge(o_full, b * NT + CREDIT)
                for j in range(blocks(n)):
                    end = min((j + 1) * G, (n + 1) * P)
                    eng.activation(probs[:, n % 2, j * G:end], s_ps[:, j * G:end], ACT.Exp, bias=ntop[:, n % 2, 1:2],
                                   scale=1.0 / C, accum_out=psums[:, n % 2, j:j + 1]).then_inc(exp_ready, 1)

            def scale_o(b, n):
                N = b * NT + n
                eng.wait_ge(o_full, N + 1 + CREDIT)
                eng.wait_ge(total_step, 2 * N + 2)
                eng.activation(o_n[:, n % 2, :], o_ps[n % 2][:, 0:P], ACT.Copy, scale=total[:, n % 2, 1:2]).then_inc(o_ready, 1)

            eng.sem_inc(exp_ready, CREDIT)
            eng.sem_inc(o_ready, CREDIT)
            with eng.Fori(0, B) as b:
                exponentials(b, 0)
                for n in range(NT):
                    if n + 1 < NT:
                        exponentials(b, n + 1)
                    scale_o(b, n)


def ffn_phase(nc, io, X, const, name, out=None):
    ctx = ExitStack()
    with ctx:
        sb = lambda what, shape, dt=F32: ctx.enter_context(nc.sbuf_tensor(name + what, shape, dt))
        sem = lambda what: ctx.enter_context(nc.semaphore(name + what))
        psum = lambda what: ctx.enter_context(nc.psum_tensor(name + what, [P, G], F32))
        ident = const[:, C_IDENT:C_IDENT + P]
        w = sb("w", [P, 3, P])
        wk_hi = sb("wk_hi", [P, P], F32R)
        wk_lo = sb("wk_lo", [P, P], F32R)
        mu = sb("mu", [P, 2])
        rest = sb("rest", [P, 2])
        mhalf = sb("mhalf", [P, GT])
        eps = sb("eps", [P, GT])
        held = sb("held", [P, 1])
        stats = sb("stats", [P, 2, GT, 6])
        mv = sb("mv", [P, 2, GT, 2])
        rstd = sb("rstd", [P, 2, GT])
        xn = sb("xn", [P, 2, G])
        xT = sb("xT", [P, B * (T + 1)])
        prev = sb("prev", [P, 2, 2, G])
        xr = sb("xr", [P, 2, G])
        xk = sb("xk", [P, 2, G])
        xk_hi = sb("xk_hi", [P, 2, G], F32R)
        xk_lo = sb("xk_lo", [P, 2, G], F32R)
        k_pos = sb("k_pos", [P, 2, G])
        k_act = sb("k_act", [P, 2, G])
        r_tanh = sb("r_tanh", [P, 2, G])
        gated = sb("gated", [P, 2, G])
        xt_ps = [psum(f"xt_ps{b}") for b in range(2)]
        k_ps = [psum(f"k_ps{b}") for b in range(2)]
        r_ps = [psum(f"r_ps{b}") for b in range(2)]
        o_ps = [psum(f"o_ps{b}") for b in range(2)]

        (loaded_w, loaded_mu, set_up, rest_set, wk_hi_ready, wk_lo_ready, stats_ready, moments_ready, rstd_step,
         xn_ready, xt_full, xt_ready, prev_ready, xr_ready, xk_ready, xk_hi_ready, xk_lo_ready, k_full, k_pos_ready,
         k_act_ready, r_full, r_ready, o_full, gated_ready, x_ready, stored) = (sem(n) for n in (
             "loaded_w", "loaded_mu", "set_up", "rest_set", "wk_hi_ready", "wk_lo_ready", "stats_ready", "moments_ready",
             "rstd_step", "xn_ready", "xt_full", "xt_ready", "prev_ready", "xr_ready", "xk_ready", "xk_hi_ready",
             "xk_lo_ready", "k_full", "k_pos_ready", "k_act_ready", "r_full", "r_ready", "o_full", "gated_ready",
             "x_ready", "stored"))
        block = ctx.enter_context(nc.Block())


        @block.sync
        def _(eng):
            eng.dma_start(w[:, :, :], io["w_ffn"]).then_inc(loaded_w, 16)
            eng.dma_start(mu[:, :], io["mu"]).then_inc(loaded_mu, 16)
            if out is not None:
                for i in range(NG):
                    for b in range(B):
                        g = 2 * i + b
                        eng.wait_ge(x_ready, g + 1)
                        t0 = b * NT + i * GT
                        eng.dma_start(out[b, i * G:(i + 1) * G, :].rearrange("(t p) c -> p t c", p=P),
                                      X[:, t0:t0 + GT, :]).then_inc(stored, 16)
                eng.wait_ge(stored, 16 * B * NG)

        @block.gpsimd
        def _(eng):
            eng.memset(mhalf[:, :], -0.5).then_inc(set_up, 1)
            eng.memset(eps[:, :], LN_EPS).then_inc(set_up, 1)
            for b in range(B):
                eng.memset(xT[:, b * (T + 1):b * (T + 1) + 1], 0.0).then_inc(set_up, 1)
            eng.wait_ge(wk_hi_ready, 1)
            eng.tensor_tensor(wk_lo[:, :], w[:, 1, :], wk_hi[:, :].bitcast(F32), ALU.subtract).then_inc(wk_lo_ready, 1)
            eng.wait_ge(set_up, 4)

            def rstds(g, b):
                eng.wait_ge(moments_ready, GT * (g + 1))
                eng.tensor_tensor(rstd[:, b, :], mv[:, b, :, 1], eps[:, :], ALU.add).then_inc(rstd_step, 1)
                eng.wait_ge(rstd_step, 2 * g + 1)
                eng.tensor_tensor(rstd[:, b, :], rstd[:, b, :], mhalf[:, :], ALU.pow).then_inc(rstd_step, 1)

            def low_part(g, b):
                eng.wait_ge(xk_hi_ready, g + 1)
                eng.tensor_tensor(xk_lo[:, b, :], xk[:, b, :], xk_hi[:, b, :].bitcast(F32), ALU.subtract).then_inc(xk_lo_ready, 1)

            def square(g, b):
                eng.wait_ge(k_pos_ready, g + 1)
                eng.tensor_tensor(k_act[:, b, :], k_pos[:, b, :], k_pos[:, b, :], ALU.mult).then_inc(k_act_ready, 1)

            rstds(0, 0)
            low_part(0, 0)
            rstds(1, 1)
            square(0, 0)
            with eng.Fori(0, NG - 1) as i:
                low_part(2 * i + 1, 1)
                rstds(2 * i + 2, 0)
                square(2 * i + 1, 1)
                low_part(2 * i + 2, 0)
                rstds(2 * i + 3, 1)
                square(2 * i + 2, 0)
            low_part(2 * NG - 1, 1)
            square(2 * NG - 1, 1)

        @block.vector
        def _(eng):
            eng.wait_ge(loaded_mu, 16)
            eng.tensor_scalar(rest[:, :], mu[:, :], -1.0, 1.0, ALU.mult, ALU.add).then_inc(rest_set, 1)

            def moments(i, b):
                g = 2 * i + b
                for j in range(GT):
                    eng.bn_stats(stats[:, b, j, :], X[:, bass.ds(b * NT + i * GT + j, 1), :]).then_inc(stats_ready, 1)
                eng.wait_ge(stats_ready, GT * g + GT)
                eng.memset(held[:, :], 0.0)
                for j in range(GT):
                    eng.bn_aggr(mv[:, b, j, :], stats[:, b, j, :]).then_inc(moments_ready, 1)

            def normalize(i, b):
                g = 2 * i + b
                eng.wait_ge(rstd_step, 2 * g + 2)
                for j in range(GT):
                    eng.tensor_scalar(xn[:, b, j * P:(j + 1) * P], X[:, bass.ds(b * NT + i * GT + j, 1), :],
                                      mv[:, b, j, 0:1], rstd[:, b, j:j + 1], ALU.subtract, ALU.mult).then_inc(xn_ready, 1)

            def mix(i, b):
                g = 2 * i + b
                here = xT[:, bass.ds(b * (T + 1) + i * G + 1, G)]
                eng.wait_ge(prev_ready, 2 * g + 1)
                eng.scalar_tensor_tensor(xk[:, b, :], here, mu[:, 1:2], prev[:, b, 1, :], ALU.mult, ALU.add).then_inc(xk_ready, 1)
                eng.wait_ge(prev_ready, 2 * g + 2)
                eng.scalar_tensor_tensor(xr[:, b, :], here, mu[:, 0:1], prev[:, b, 0, :], ALU.mult, ALU.add).then_inc(xr_ready, 1)

            def output(i, b):
                g = 2 * i + b
                xs = X[:, bass.ds(b * NT + i * GT, GT), :]
                eng.wait_ge(r_ready, g + 1)
                eng.wait_ge(o_full, g + 1)
                eng.scalar_tensor_tensor(gated[:, b, :], r_tanh[:, b, :], 1.0, o_ps[b][:, :], ALU.add, ALU.mult).then_inc(gated_ready, 1)
                eng.wait_ge(gated_ready, g + 1)
                eng.scalar_tensor_tensor(xs, gated[:, b, :].rearrange("p (t c) -> p t c", t=GT), 0.5, xs,
                                         ALU.mult, ALU.add).then_inc(x_ready, 1)

            moments(0, 0)
            normalize(0, 0)
            moments(0, 1)
            mix(0, 0)
            normalize(0, 1)
            with eng.Fori(0, NG - 1) as i:
                moments(i + 1, 0)
                mix(i, 1)
                normalize(i + 1, 0)
                output(i, 0)
                moments(i + 1, 1)
                mix(i + 1, 0)
                normalize(i + 1, 1)
                output(i, 1)
            mix(NG - 1, 1)
            output(NG - 1, 0)
            output(NG - 1, 1)

        @block.scalar
        def _(eng):
            eng.wait_ge(loaded_w, 16)
            eng.activation(wk_hi[:, :], w[:, 1, :], ACT.Copy).then_inc(wk_hi_ready, 1)
            eng.wait_ge(rest_set, 1)
            eng.wait_ge(set_up, 4)

            def front(i, b):
                g = 2 * i + b
                at = b * (T + 1) + i * G
                eng.wait_ge(xt_full, g + 1)
                eng.activation(xT[:, bass.ds(at + 1, G)], xt_ps[b][:, :], ACT.Copy).then_inc(xt_ready, 1)
                eng.wait_ge(xt_ready, g + 1)
                for r in (1, 0):
                    eng.activation(prev[:, b, r, :], xT[:, bass.ds(at, G)], ACT.Copy, scale=rest[:, r:r + 1]).then_inc(prev_ready, 1)
                eng.wait_ge(xk_ready, g + 1)
                eng.activation(xk_hi[:, b, :], xk[:, b, :], ACT.Copy).then_inc(xk_hi_ready, 1)

            def back(i, b):
                g = 2 * i + b
                eng.wait_ge(k_full, g + 1)
                eng.activation(k_pos[:, b, :], k_ps[b][:, :], ACT.Relu).then_inc(k_pos_ready, 1)
                eng.wait_ge(r_full, g + 1)
                eng.activation(r_tanh[:, b, :], r_ps[b][:, :], ACT.Tanh, scale=0.5).then_inc(r_ready, 1)

            front(0, 0)
            with eng.Fori(0, NG - 1) as i:
                back(i, 0)
                front(i, 1)
                back(i, 1)
                front(i + 1, 0)
            back(NG - 1, 0)
            front(NG - 1, 1)
            back(NG - 1, 1)

        @block.tensor
        def _(eng):
            eng.wait_ge(loaded_w, 16)
            eng.wait_ge(wk_lo_ready, 1)

            def turn(g, b, first=False):
                if not first:
                    eng.wait_ge(xt_ready, g - 1)
                for j in range(GT):
                    eng.wait_ge(xn_ready, GT * g + j + 1)
                    mm = eng.transpose(xt_ps[b][:, j * P:(j + 1) * P], xn[:, b, j * P:(j + 1) * P], ident)
                mm.then_inc(xt_full, 1)

            def keys(g, b, first=False):
                eng.wait_ge(xk_lo_ready, g + 1)
                if not first:
                    eng.wait_ge(k_pos_ready, g - 1)
                eng.matmul(k_ps[b][:, :], wk_hi[:, :], xk_hi[:, b, :], start=True, stop=False)
                eng.matmul(k_ps[b][:, :], wk_lo[:, :], xk_hi[:, b, :], start=False, stop=False)
                eng.matmul(k_ps[b][:, :], wk_hi[:, :], xk_lo[:, b, :], start=False, stop=True).then_inc(k_full, 1)

            def receptance(g, b, first=False):
                eng.wait_ge(xr_ready, g + 1)
                if not first:
                    eng.wait_ge(r_ready, g - 1)
                for j in range(GT):
                    mm = eng.matmul(r_ps[b][:, j * P:(j + 1) * P], xr[:, b, j * P:(j + 1) * P], w[:, 0, :], start=True, stop=True)
                mm.then_inc(r_full, 1)

            def values(g, b, first=False):
                eng.wait_ge(k_act_ready, g + 1)
                if not first:
                    eng.wait_ge(gated_ready, g - 1)
                for j in range(GT):
                    mm = eng.matmul(o_ps[b][:, j * P:(j + 1) * P], k_act[:, b, j * P:(j + 1) * P], w[:, 2, :], start=True, stop=True)
                mm.then_inc(o_full, 1)

            turn(0, 0, True)
            keys(0, 0, True)
            turn(1, 1, True)
            receptance(0, 0, True)
            keys(1, 1, True)
            values(0, 0, True)
            turn(2, 0)
            receptance(1, 1, True)
            keys(2, 0)
            values(1, 1, True)
            with eng.Fori(1, NG - 1) as i:
                g = 2 * i
                turn(g + 1, 1)
                receptance(g, 0)
                keys(g + 1, 1)
                values(g, 0)
                turn(g + 2, 0)
                receptance(g + 1, 1)
                keys(g + 2, 0)
                values(g + 1, 1)
            g = 2 * (NG - 1)
            turn(g + 1, 1)
            receptance(g, 0)
            keys(g + 1, 1)
            values(g, 0)
            receptance(g + 1, 1)
            values(g + 1, 1)


class Tile:

    def __init__(self, i, off):
        self.i, self.off = i, off
        self.m = 2 * i + off
        self.b = off % 2
        self.x = (off % 2) * NT + i + off // 2

    def later(self, k):
        return Tile(self.i, self.off + k)

    def count(self, per_tile, k=0):
        return 2 * per_tile * self.i + per_tile * self.off + k


PROJ = [("q", 0), ("f", 0), ("k", 0), ("f", 1), ("q", 1), ("g", 0), ("k", 1), ("g", 1), ("v", 0), ("v", 1)]
TURN = {job: k for k, job in enumerate(
    [("qT", 0), ("kT", 0), ("qT", 1), ("kT", 1), ("qk", 0), ("qk", 1), ("qk", 2), ("qk", 3), ("oT", 0), ("oT", 1)])}
NTURN = len(TURN)


def linear_phase(nc, io, X, const, w5_hi, w5_lo):
    ctx = ExitStack()
    with ctx:
        sb = lambda what, shape, dt=F32: ctx.enter_context(nc.sbuf_tensor("la_" + what, shape, dt))
        sem = lambda what: ctx.enter_context(nc.semaphore("la_" + what))
        psum = lambda what: ctx.enter_context(nc.psum_tensor("la_" + what, [P, G], F32))
        ident = const[:, C_IDENT:C_IDENT + P]

        w_beta = sb("w_beta", [P, H])
        w_out = sb("w_out", [P, NP, P])
        norm_w = sb("norm_w", [P, 1])
        bias_f = sb("bias_f", [P, HD])
        bias_g = sb("bias_g", [P, HD])
        rate = sb("rate", [P, H])
        rate_col = sb("rate_col", [P, NP])
        decay = sb("decay", [P, H, P])
        decay_q = sb("decay_q", [P, NP, P])
        decay_k = sb("decay_k", [P, H])
        decay_s = sb("decay_s", [P, NP])
        mhalf = sb("mhalf", [P, H])
        ones = sb("ones", [P, H])
        eps = sb("eps", [P, 1])
        held = sb("held", [P, 1])
        state = sb("state", [P, 2, NP, P])
        faded = sb("faded", [P, 2, NP, P])

        stats = sb("stats", [P, 2, 6])
        mv = sb("mv", [P, 2, 2])
        rstd = sb("rstd", [P, 2])
        xn = sb("xn", [P, 2, P])
        xT = sb("xT", [P, 2, P])
        x_hi = sb("x_hi", [P, 2, P], F32R)
        x_lo = sb("x_lo", [P, 2, P], F32R)
        f = sb("f", [P, 2, HD])
        gate = sb("gate", [P, 2, HD])
        q = sb("q", [P, 2, HD])
        k = sb("k", [P, 2, HD])
        v = sb("v", [P, 2, HD])
        sq_q = sb("sq_q", [P, HD])
        sq_k = sb("sq_k", [P, HD])
        sq_u = sb("sq_u", [P, HD])
        ssq = sb("ssq", [P, 2, H])
        ssk = sb("ssk", [P, 2, H])
        beta = sb("beta", [P, 2, H])
        coef = sb("coef", [P, 2, H])
        vb = sb("vb", [P, HD])
        kd = sb("kd", [P, HD])
        qT = sb("qT", [P, NP, P])
        kT = sb("kT", [P, NP, P])
        qdT = sb("qdT", [P, NP, P])
        pT = sb("pT", [P, H, P])
        u = sb("u", [P, HD])
        ssu = sb("ssu", [P, H])
        scale = sb("scale", [P, 2, H])
        og = sb("og", [P, HD])
        oT = sb("oT", [P, NP, P])

        pr_ps = [psum(f"pr_ps{r}") for r in range(2)]
        t_ps = [psum(f"t_ps{r}") for r in range(2)]
        o_ps = [psum(f"o_ps{r}") for r in range(2)]
        m_ps = psum("m_ps")
        s_ps = psum("s_ps")

        loaded = sem("loaded")
        names = ("rate_step rate_ready set_up decay_exp decay_ready w_out_ready stats_ready moments_ready rstd_step xn_ready x_turned "
                 "xt_ready xlo_ready beta_full beta_ready fb_ready gb_ready f_ready g_ready "
                 "qsq_ready ksq_ready usq_ready qsq_summed ksq_summed ssq_ready ssk_ready ssu_ready coef_step vb_ready kd_ready faded_ready qd_ready "
                 "o_full u_ready state_full state_ready ug_ready scale_step og_ready y_full x_ready").split()
        s = {n: sem(n) for n in names}
        pr_full, pr_read = bank_sems(sem, "pr_full", 2), bank_sems(sem, "pr_read", 2)
        t_full, t_read = bank_sems(sem, "t_full", 2), bank_sems(sem, "t_read", 2)

        def by_head(ap):
            return ap.rearrange("p (h d) -> p h d", d=D)

        def over_d(ap):
            return ap.unsqueeze(2).broadcast_to([P, H, D])

        def proj(tl, job):
            k_ = PROJ.index(job)
            return k_ % 2, tl.count(5, k_ // 2)

        def projected(eng, tl, kind, half):
            bank, before = proj(tl, (kind, half))
            eng.wait_ge(pr_read[bank], before + 1)

        def turn(tl, job):
            step = tl.later(1) if job[0] == "oT" else tl
            at = NTURN * step.off + TURN[job]
            absent = 2
            if isinstance(step.i, int) and step.m == 0 and TURN[job] < TURN["oT", 0]:
                absent = 0
            if isinstance(step.i, int) and step.m == B * NT:
                absent += TURN["oT", 0]
            return at % 2, NTURN * step.i + at // 2 - absent // 2

        with nc.Block() as block:
            @block.sync
            def _(eng):
                eng.dma_start(w_beta[:, :], io["wb"]).then_inc(loaded, 16)
                eng.dma_start(w_out[:, :, :], io["w_out"].rearrange("(r p) m -> p r m", p=P)).then_inc(loaded, 16)
                for half in range(2):
                    rows = slice(half * D, (half + 1) * D)
                    eng.dma_start(norm_w[rows, :], io["norm_w"].rearrange("(d o) -> d o", o=1)).then_inc(loaded, 16)
                    eng.dma_start(rate_col[rows, :], io["a_log_pairs"][half:half + 1, :].broadcast_to([D, NP])).then_inc(loaded, 16)
                for row, where, n_ in (("dt_bias", bias_f, HD), ("bg", bias_g, HD), ("a_log", rate, H)):
                    src = io[row].rearrange("(o n) -> o n", o=1).broadcast_to([P, n_])
                    eng.dma_start(where[:, :], src).then_inc(loaded, 16)

            @block.gpsimd
            def _(eng):
                eng.memset(mhalf[:, :], -0.5).then_inc(s["set_up"], 1)
                eng.memset(ones[:, :], 1.0).then_inc(s["set_up"], 1)
                eng.memset(eps[:, :], LN_EPS).then_inc(s["set_up"], 1)
                eng.memset(state[:, :, :, :], 0.0).then_inc(s["set_up"], 1)

            @block.vector
            def _(eng):
                eng.wait_ge(loaded, 16 * 9)
                eng.tensor_scalar(w_out[:, :, :], w_out[:, :, :], norm_w[:, 0:1], 4.0, ALU.mult, ALU.mult).then_inc(s["w_out_ready"], 1)
                eng.tensor_scalar(bias_f[:, :], bias_f[:, :], -1.0, None, ALU.mult).then_inc(s["w_out_ready"], 1)
                eng.wait_ge(s["rate_step"], 2)
                for r in (rate, rate_col):
                    eng.tensor_scalar(r[:, :], r[:, :], 1e30, -1.0, ALU.min, ALU.mult).then_inc(s["rate_ready"], 1)
                for h in range(H):
                    eng.wait_ge(s["decay_exp"], h + 1)
                    eng.tensor_tensor(decay[:, h, :], decay[:, h, :], const[:, C_STRICT:C_STRICT + P], ALU.mult).then_inc(s["decay_ready"], 1)

            @block.scalar
            def _(eng):
                eng.wait_ge(loaded, 16 * 9)
                for r in (rate, rate_col):
                    eng.activation(r[:, :], r[:, :], ACT.Exp).then_inc(s["rate_step"], 1)
                eng.wait_ge(s["rate_ready"], 2)
                for h in range(H):
                    eng.activation(decay[:, h, :], const[:, C_LAG:C_LAG + P], ACT.Exp, scale=rate[:, h:h + 1]).then_inc(s["decay_exp"], 1)
                for r in range(NP):
                    eng.activation(decay_q[:, r, :], const[:, C_TPOS:C_TPOS + P], ACT.Exp, scale=rate_col[:, r:r + 1]).then_inc(s["decay_exp"], 1)
                eng.activation(decay_k[:, :], rate[:, :], ACT.Exp, scale=const[:, C_LEFT:C_LEFT + 1]).then_inc(s["decay_exp"], 1)
                eng.activation(decay_s[:, :], rate_col[:, :], ACT.Exp, scale=float(P)).then_inc(s["decay_exp"], 1)

        LAST = B * NT - 1

        def run_steps(eng, step):
            step(Tile(0, 0), first=True)
            loops = (LAST - 2) // 2
            with eng.Fori(0, loops) as i:
                step(Tile(i, 1))
                step(Tile(i, 2))
            for m in range(2 * loops + 1, LAST + 1):
                step(Tile(0, m), ahead=m + 2 <= LAST, last=m == LAST)

        block = ctx.enter_context(nc.Block())

        @block.tensor
        def _(eng):
            def turn_x(tl):
                if not isinstance(tl.m, int) or tl.m >= 3:
                    eng.wait_ge(s["x_ready"], tl.count(1, -2))
                elif tl.m == 2:
                    eng.wait_ge(s["beta_ready"], 1)
                elif tl.m == 1:
                    eng.wait_ge(s["xt_ready"], 2)
                eng.wait_ge(s["xn_ready"], tl.count(1, 1))
                eng.transpose(m_ps[:, 0:P], xn[:, tl.b, :], ident).then_inc(s["x_turned"], 1)

            def project(tl, job):
                bank, before = proj(tl, job)
                if job == PROJ[0]:
                    eng.wait_ge(s["xlo_ready"], tl.count(1, 1))
                    eng.wait_ge(s["xt_ready"], tl.count(2, 2))
                eng.wait_ge(pr_read[bank], before)
                col = PROJ.index(job) * G
                hi, lo = w5_hi[:, col:col + G], w5_lo[:, col:col + G]
                eng.matmul(pr_ps[bank][:, :], x_hi[:, tl.b, :], hi, start=True, stop=False)
                eng.matmul(pr_ps[bank][:, :], x_hi[:, tl.b, :], lo, start=False, stop=False)
                eng.matmul(pr_ps[bank][:, :], x_lo[:, tl.b, :], hi, start=False, stop=True).then_inc(pr_full[bank], 1)

            def betas(tl, ahead):
                if ahead:
                    eng.wait_ge(s["xt_ready"], tl.count(2, 4))
                else:
                    eng.wait_ge(s["x_ready"], tl.count(1, -1))
                eng.matmul(m_ps[:, 0:H], xT[:, tl.b, :], w_beta[:, :], start=True, stop=True).then_inc(s["beta_full"], 1)

            def turning(tl, job):
                bank, before = turn(tl, job)
                eng.wait_ge(t_read[bank], before)
                return t_ps[bank], t_full[bank]

            def turned(tl, job):
                bank, before = turn(tl, job)
                eng.wait_ge(t_read[bank], before + 1)

            def turn_qk(tl, job):
                kind, half = job
                projected(eng, tl, kind[0], half)
                ps, full = turning(tl, job)
                src = (q if kind == "qT" else k)[:, tl.b, :]
                for r in range(4):
                    pair = 4 * half + r
                    mm = eng.transpose(ps[:, r * P:(r + 1) * P], src[:, pair * P:(pair + 1) * P], ident)
                mm.then_inc(full, 1)

            def scores(tl, n_):
                banks = [turning(tl, ("qk", 2 * n_ + odd)) for odd in range(2)]
                for r in range(4):
                    for odd, (ps, full) in enumerate(banks):
                        rows, pair = slice(odd * D, (odd + 1) * D), 4 * n_ + r
                        mm = eng.matmul(ps[:, r * P:(r + 1) * P], kT[rows, pair, :], qT[rows, pair, :], start=True, stop=True)
                        if r == 3:
                            mm.then_inc(full, 1)

            def update(tl, first):
                eng.wait_ge(s["kd_ready"], tl.count(1, 1))
                eng.wait_ge(s["vb_ready"], tl.count(1, 1))
                if not first:
                    eng.wait_ge(s["state_ready"], tl.count(2))
                for h in range(H):
                    rows, cols = slice((h % 2) * D, (h % 2 + 1) * D), slice(h * D, (h + 1) * D)
                    mm = eng.matmul(s_ps[rows, (h // 2) * D:(h // 2 + 1) * D], kd[:, cols], vb[:, cols], start=True, stop=True)
                mm.then_inc(s["state_full"], 1)

            def attend(tl, first):
                eng.wait_ge(s["qd_ready"], tl.count(1, 1))
                if not first:
                    eng.wait_ge(s["state_ready"], tl.count(2))
                for half in range(2):
                    if not first:
                        eng.wait_ge(s["u_ready"], tl.count(2, half - 1))
                    turned(tl, ("qk", 2 * half))
                    turned(tl, ("qk", 2 * half + 1))
                    for pair in range(4 * half, 4 * half + 4):
                        at = (pair % 4) * P
                        eng.matmul(o_ps[half][:, at:at + P], qdT[:, pair, :], state[:, tl.b, pair, :], start=True, stop=False,
                                   skip_group_check=True)
                        for h in (2 * pair, 2 * pair + 1):
                            at = (h % 8) * D
                            mm = eng.matmul(o_ps[half][:, at:at + D], pT[:, h, :], vb[:, h * D:(h + 1) * D], start=False, stop=True,
                                            skip_group_check=True)
                    mm.then_inc(s["o_full"], 1)

            def turn_o(tl, half):
                if half == 0:
                    eng.wait_ge(s["og_ready"], tl.count(1, 1))
                ps, full = turning(tl, ("oT", half))
                for r in range(4):
                    pair = 4 * half + r
                    mm = eng.transpose(ps[:, r * P:(r + 1) * P], og[:, pair * P:(pair + 1) * P], ident)
                mm.then_inc(full, 1)

            def project_out(tl):
                turned(tl, ("oT", 0))
                turned(tl, ("oT", 1))
                eng.wait_ge(s["x_ready"], tl.count(1, 1))
                eng.wait_ge(s["beta_ready"], min(tl.m + 3, LAST + 1) if isinstance(tl.m, int) else tl.count(1, 3))
                for pair in range(NP):
                    mm = eng.matmul(m_ps[:, 0:P], oT[:, pair, :], w_out[:, pair, :], start=(pair == 0), stop=(pair == NP - 1))
                mm.then_inc(s["y_full"], 1)

            def step(tl, first=False, ahead=True, last=False):
                nxt, prv = tl.later(1), tl.later(-1)
                own = [lambda j=j: turn_qk(tl, j) for j in (("qT", 0), ("kT", 0), ("qT", 1), ("kT", 1))]
                own += [lambda: scores(tl, 0), lambda: turn_x(tl.later(2)) if ahead else None, lambda: scores(tl, 1),
                        lambda: None if last else betas(nxt, ahead)]
                for n_, job in enumerate(PROJ):
                    if not last:
                        project(nxt, job)
                    if n_ < len(own):
                        own[n_]()
                if not first:
                    turn_o(prv, 0)
                    turn_o(prv, 1)
                attend(tl, first)
                if not first:
                    project_out(prv)
                update(tl, first)

            turn_x(Tile(0, 0))
            turn_x(Tile(0, 1))
            for job in PROJ:
                project(Tile(0, 0), job)
            betas(Tile(0, 0), True)
            run_steps(eng, step)
            turn_o(Tile(0, LAST), 0)
            turn_o(Tile(0, LAST), 1)
            project_out(Tile(0, LAST))

        @block.vector
        def _(eng):
            def layer_norm(tl):
                eng.bn_stats(stats[:, tl.b, :], X[:, bass.ds(tl.x, 1), :]).then_inc(s["stats_ready"], 1)
                eng.wait_ge(s["stats_ready"], tl.count(1, 1))
                eng.memset(held[:, :], 0.0)
                eng.bn_aggr(mv[:, tl.b, :], stats[:, tl.b, :]).then_inc(s["moments_ready"], 1)

            def normalize(tl):
                eng.wait_ge(s["rstd_step"], tl.count(2, 2))
                eng.tensor_scalar(xn[:, tl.b, :], X[:, bass.ds(tl.x, 1), :], mv[:, tl.b, 0:1], rstd[:, tl.b:tl.b + 1],
                                  ALU.subtract, ALU.mult).then_inc(s["xn_ready"], 1)

            def add_bias(tl, job):
                bank, before = proj(tl, job)
                eng.wait_ge(pr_full[bank], before + 1)
                kind, half = job
                where, bias, ready = (f, bias_f, s["fb_ready"]) if kind == "f" else (gate, bias_g, s["gb_ready"])
                part = slice(half * G, (half + 1) * G)
                if half == 0 and (not isinstance(tl.m, int) or tl.m >= 1):
                    if kind == "f":
                        eng.wait_ge(s["u_ready"], tl.count(2, -2))
                    else:
                        eng.wait_ge(s["ug_ready"], tl.count(1, -1))
                eng.tensor_tensor(where[:, tl.b, part], pr_ps[bank][:, :], bias[:, part], ALU.add).then_inc(pr_read[bank], 1)

            def decayed(tl, n_):
                bank, before = turn(tl, ("qk", n_))
                eng.wait_ge(t_full[bank], before + 1)
                if n_ == 0:
                    eng.wait_ge(s["o_full"], tl.count(2))
                heads = slice(8 * (n_ // 2) + n_ % 2, 8 * (n_ // 2) + 8, 2)
                eng.tensor_tensor(pT[:, heads, :], t_ps[bank][:, :].rearrange("p (h t) -> p h t", h=4),
                                  decay[:, heads, :], ALU.mult).then_inc(t_read[bank], 1)

            def gate_o(tl):
                for half in range(2):
                    part = slice(half * G, (half + 1) * G)
                    eng.wait_ge(s["o_full"], tl.count(2, half + 1))
                    eng.wait_ge(s["f_ready"], tl.count(1, 1))
                    eng.scalar_tensor_tensor(u[:, part], f[:, tl.b, part], 1.0, o_ps[half][:, :], ALU.add, ALU.mult).then_inc(s["u_ready"], 1)

            def new_state(tl):
                eng.wait_ge(s["state_full"], tl.count(1, 1))
                eng.wait_ge(s["faded_ready"], tl.count(1, 1))
                for half in range(2):
                    rows = slice(half * D, (half + 1) * D)
                    ps = s_ps[rows, :].rearrange("p (r e) -> p r e", r=NP)
                    cols = slice(half * D, (half + 1) * D)
                    eng.tensor_tensor(state[rows, tl.b, :, cols], ps, faded[rows, tl.b, :, cols], ALU.add).then_inc(s["state_ready"], 1)

            def sum_squares(tl, where, sq, ready, done):
                eng.wait_ge(s[ready], tl.count(1, 1))
                eng.tensor_reduce(where, by_head(sq[:, :]), AX.X, ALU.add).then_inc(s[done], 1)

            def guard(tl, where, summed, factor, ready):
                eng.wait_ge(s[summed], tl.count(1, 1))
                eng.tensor_scalar(where, where, L2_EPS ** 2, factor, ALU.max, ALU.mult).then_inc(s[ready], 1)

            def gate_u(tl):
                eng.wait_ge(s["g_ready"], tl.count(1, 1))
                eng.wait_ge(s["usq_ready"], tl.count(1, 1))
                eng.scalar_tensor_tensor(u[:, :], gate[:, tl.b, :], 1.0, u[:, :], ALU.add, ALU.mult).then_inc(s["ug_ready"], 1)

            def residual(tl):
                eng.wait_ge(s["y_full"], tl.count(1, 1))
                xs = X[:, bass.ds(tl.x, 1), :]
                eng.tensor_tensor(xs, m_ps[:, 0:P].rearrange("p (t c) -> p t c", t=1), xs, ALU.add).then_inc(s["x_ready"], 1)

            def step(tl, first=False, ahead=True, last=False):
                nxt, prv = tl.later(1), tl.later(-1)
                if not first:
                    gate_o(prv)
                if ahead:
                    layer_norm(tl.later(2))
                if not last:
                    add_bias(nxt, ("f", 0))
                if not first:
                    new_state(prv)
                if not last:
                    add_bias(nxt, ("f", 1))
                if not first:
                    sum_squares(prv, ssu[:, :], sq_u, "usq_ready", "ssu_ready")
                    gate_u(prv)
                if ahead:
                    normalize(tl.later(2))
                decayed(tl, 0)
                decayed(tl, 1)
                if not last:
                    add_bias(nxt, ("g", 0))
                    if not first:
                        eng.wait_ge(s["scale_step"], nxt.count(2, -3))
                    sum_squares(nxt, ssq[:, nxt.b, :], sq_q, "qsq_ready", "qsq_summed")
                decayed(tl, 2)
                if not last:
                    guard(nxt, ssq[:, nxt.b, :], "qsq_summed", 256 * RMS_EPS, "ssq_ready")
                decayed(tl, 3)
                if not last:
                    add_bias(nxt, ("g", 1))
                    sum_squares(nxt, ssk[:, nxt.b, :], sq_k, "ksq_ready", "ksq_summed")
                    guard(nxt, ssk[:, nxt.b, :], "ksq_summed", 4.0, "ssk_ready")
                if not first:
                    residual(prv)

            eng.sem_inc(s["x_ready"], 1)
            for m in range(2):
                layer_norm(Tile(0, m))
                normalize(Tile(0, m))
            for job in (("f", 0), ("f", 1), ("g", 0), ("g", 1)):
                add_bias(Tile(0, 0), job)
            sum_squares(Tile(0, 0), ssq[:, 0, :], sq_q, "qsq_ready", "qsq_summed")
            guard(Tile(0, 0), ssq[:, 0, :], "qsq_summed", 256 * RMS_EPS, "ssq_ready")
            sum_squares(Tile(0, 0), ssk[:, 0, :], sq_k, "ksq_ready", "ksq_summed")
            guard(Tile(0, 0), ssk[:, 0, :], "ksq_summed", 4.0, "ssk_ready")
            run_steps(eng, step)
            end = Tile(0, LAST)
            gate_o(end)
            new_state(end)
            sum_squares(end, ssu[:, :], sq_u, "usq_ready", "ssu_ready")
            gate_u(end)
            residual(end)

        @block.scalar
        def _(eng):
            def copy_x(tl):
                eng.wait_ge(s["x_turned"], tl.count(1, 1))
                eng.activation(xT[:, tl.b, :], m_ps[:, 0:P], ACT.Copy).then_inc(s["xt_ready"], 1)
                eng.activation(x_hi[:, tl.b, :], m_ps[:, 0:P], ACT.Copy).then_inc(s["xt_ready"], 1)

            def silu(tl, job):
                bank, before = proj(tl, job)
                kind, half = job
                eng.wait_ge(pr_full[bank], before + 1)
                where = {"q": q, "k": k, "v": v}[kind]
                eng.activation(where[:, tl.b, half * G:(half + 1) * G], pr_ps[bank][:, :], ACT.Silu).then_inc(pr_read[bank], 1)

            def tanh(tl, where, kind, ready):
                projected(eng, tl, kind, 1)
                eng.activation(where[:, tl.b, :], where[:, tl.b, :], ACT.Tanh, scale=0.5).then_inc(s[ready], 1)

            def copy_turned(tl, job, where):
                bank, before = turn(tl, job)
                half = job[1]
                eng.wait_ge(t_full[bank], before + 1)
                eng.activation(where[:, 4 * half:4 * half + 4, :], t_ps[bank][:, :].rearrange("p (r t) -> p r t", r=4),
                               ACT.Copy).then_inc(t_read[bank], 1)

            def beta_tanh(tl):
                eng.wait_ge(s["beta_full"], tl.count(1, 1))
                eng.activation(beta[:, tl.b, :], m_ps[:, 0:H], ACT.Tanh, scale=0.5).then_inc(s["beta_ready"], 1)

            def square_q(tl):
                projected(eng, tl, "q", 1)
                if not isinstance(tl.m, int) or tl.m >= 1:
                    eng.wait_ge(s["qsq_summed"], tl.count(1))
                eng.activation(sq_q[:, :], q[:, tl.b, :], ACT.Square).then_inc(s["qsq_ready"], 1)

            def square_k(tl):
                projected(eng, tl, "k", 1)
                if not isinstance(tl.m, int) or tl.m >= 1:
                    eng.wait_ge(s["ksq_summed"], tl.count(1))
                eng.activation(sq_k[:, :], k[:, tl.b, :], ACT.Square).then_inc(s["ksq_ready"], 1)

            def square_u(tl):
                eng.wait_ge(s["u_ready"], tl.count(2, 2))
                eng.activation(sq_u[:, :], u[:, :], ACT.Square).then_inc(s["usq_ready"], 1)

            def step(tl, first=False, ahead=True, last=False):
                nxt, prv = tl.later(1), tl.later(-1)
                if not last:
                    silu(nxt, ("q", 0))
                copy_turned(tl, ("qT", 0), qT)
                copy_turned(tl, ("kT", 0), kT)
                if not first:
                    square_u(prv)
                if not last:
                    silu(nxt, ("k", 0))
                copy_turned(tl, ("qT", 1), qT)
                copy_turned(tl, ("kT", 1), kT)
                if not last:
                    silu(nxt, ("q", 1))
                    square_q(nxt)
                    tanh(nxt, f, "f", "f_ready")
                if ahead:
                    copy_x(tl.later(2))
                if not last:
                    silu(nxt, ("k", 1))
                    square_k(nxt)
                    beta_tanh(nxt)
                    silu(nxt, ("v", 0))
                    tanh(nxt, gate, "g", "g_ready")
                    silu(nxt, ("v", 1))
                if not first:
                    copy_turned(prv, ("oT", 0), oT)
                    copy_turned(prv, ("oT", 1), oT)

            start = Tile(0, 0)
            copy_x(start)
            copy_x(Tile(0, 1))
            for job in PROJ:
                if job[0] in "qkv":
                    silu(start, job)
            tanh(start, f, "f", "f_ready")
            tanh(start, gate, "g", "g_ready")
            beta_tanh(start)
            square_q(start)
            square_k(start)
            run_steps(eng, step)
            end = Tile(0, LAST)
            square_u(end)
            copy_turned(end, ("oT", 0), oT)
            copy_turned(end, ("oT", 1), oT)

        @block.gpsimd
        def _(eng):
            def inverse_root(tl):
                eng.wait_ge(s["moments_ready"], tl.count(1, 1))
                eng.tensor_tensor(rstd[:, tl.b:tl.b + 1], mv[:, tl.b, 1:2], eps[:, :], ALU.add).then_inc(s["rstd_step"], 1)
                eng.wait_ge(s["rstd_step"], tl.count(2, 1))
                eng.tensor_tensor(rstd[:, tl.b:tl.b + 1], rstd[:, tl.b:tl.b + 1], mhalf[:, 0:1], ALU.pow).then_inc(s["rstd_step"], 1)

            def low_x(tl):
                eng.wait_ge(s["xt_ready"], tl.count(2, 2))
                eng.tensor_tensor(x_lo[:, tl.b, :], xT[:, tl.b, :], x_hi[:, tl.b, :].bitcast(F32), ALU.subtract).then_inc(s["xlo_ready"], 1)

            def coefficients(tl):
                b = tl.b
                eng.wait_ge(s["beta_ready"], tl.count(1, 1))
                eng.tensor_tensor(beta[:, b, :], beta[:, b, :], ones[:, :], ALU.add).then_inc(s["coef_step"], 1)
                eng.wait_ge(s["ssk_ready"], tl.count(1, 1))
                eng.tensor_tensor(coef[:, b, :], ssk[:, b, :], mhalf[:, :], ALU.pow).then_inc(s["coef_step"], 1)
                eng.wait_ge(s["coef_step"], tl.count(3, 2))
                eng.tensor_tensor(coef[:, b, :], coef[:, b, :], beta[:, b, :], ALU.mult).then_inc(s["coef_step"], 1)

            def weigh(tl, first):
                eng.wait_ge(s["coef_step"], tl.count(3, 3))
                projected(eng, tl, "v", 0)
                projected(eng, tl, "v", 1)
                if not first:
                    eng.wait_ge(s["state_full"], tl.count(1))
                eng.tensor_tensor(by_head(vb[:, :]), by_head(v[:, tl.b, :]), over_d(coef[:, tl.b, :]), ALU.mult).then_inc(s["vb_ready"], 1)
                eng.tensor_tensor(by_head(kd[:, :]), by_head(k[:, tl.b, :]), over_d(decay_k[:, :]), ALU.mult).then_inc(s["kd_ready"], 1)

            def fade(tl, first):
                if not first:
                    eng.wait_ge(s["state_ready"], tl.count(2))
                eng.tensor_tensor(faded[:, tl.b, :, :], state[:, tl.b, :, :], decay_s[:, :].unsqueeze(2).broadcast_to([P, NP, P]),
                                  ALU.mult).then_inc(s["faded_ready"], 1)

            def decay_queries(tl):
                bank, before = turn(tl, ("qT", 1))
                eng.wait_ge(t_read[bank], before + 1)
                eng.tensor_tensor(qdT[:, :, :], qT[:, :, :], decay_q[:, :, :], ALU.mult).then_inc(s["qd_ready"], 1)

            def scale_u(tl):
                b = tl.b
                eng.wait_ge(s["ssu_ready"], tl.count(1, 1))
                eng.tensor_tensor(scale[:, b, :], ssq[:, b, :], ssu[:, :], ALU.add).then_inc(s["scale_step"], 1)
                eng.wait_ge(s["scale_step"], tl.count(2, 1))
                eng.tensor_tensor(scale[:, b, :], scale[:, b, :], mhalf[:, :], ALU.pow).then_inc(s["scale_step"], 1)
                eng.wait_ge(s["scale_step"], tl.count(2, 2))
                eng.wait_ge(s["ug_ready"], tl.count(1, 1))
                eng.tensor_tensor(by_head(og[:, :]), by_head(u[:, :]), over_d(scale[:, b, :]), ALU.mult).then_inc(s["og_ready"], 1)

            def step(tl, first=False, ahead=True, last=False):
                nxt, prv = tl.later(1), tl.later(-1)
                if ahead:
                    inverse_root(tl.later(2))
                weigh(tl, first)
                if not first:
                    scale_u(prv)
                decay_queries(tl)
                if ahead:
                    low_x(tl.later(2))
                fade(tl, first)
                if not last:
                    coefficients(nxt)

            for m in range(2):
                inverse_root(Tile(0, m))
                low_x(Tile(0, m))
            coefficients(Tile(0, 0))
            run_steps(eng, step)
            scale_u(Tile(0, LAST))


def build(nc, io, out):
    ctx = ExitStack()
    with ctx:
        sb = lambda name, shape, dt=F32: ctx.enter_context(nc.sbuf_tensor(name, shape, dt))
        X = sb("X", [P, B * NT, C])
        const = sb("const", [P, C_WIDTH])
        w5_hi = sb("w5_hi", [P, 5 * HD], F32R)
        w5_lo = sb("w5_lo", [P, 5 * HD], F32R)
        with ExitStack() as attention:
            qk_hi = attention.enter_context(nc.sbuf_tensor("qk_hi", [P, 2 * B * T], F32R))
            qk_lo = attention.enter_context(nc.sbuf_tensor("qk_lo", [P, 2 * B * T], F32R))
            V = attention.enter_context(nc.sbuf_tensor("V", [P, B * NT, C], F32))
            qkv_phase(nc, io, X, const, qk_hi, qk_lo, V)
            attention_phase(nc, io, X, const, qk_hi, qk_lo, V, w5_hi, w5_lo)
        ffn_phase(nc, io, X, const, "f1_")
        linear_phase(nc, io, X, const, w5_hi, w5_lo)
        ffn_phase(nc, io, X, const, "f2_", out)


def constants():
    s = np.arange(P)[:, None]
    t = np.arange(P)[None, :]
    const = np.zeros((P, C_WIDTH), np.float32)
    const[:, C_IDENT:C_IDENT + P] = s == t
    const[:, C_LAG:C_LAG + P] = np.maximum(t - 1 - s, 0)
    const[:, C_STRICT:C_STRICT + P] = s < t
    const[:, C_NEG:C_NEG + P] = np.where(t > s, NEG, 0)
    const[:, C_TPOS:C_TPOS + P] = t
    const[:, C_LEFT] = P - 1 - np.arange(P)
    half = C // 2
    freqs = np.power(np.float32(ROTARY_BASE), -np.arange(half, dtype=np.float32) / np.float32(half)).astype(np.float32)
    radians = freqs[:, None] * np.arange(T, dtype=np.float32)[None, :]
    cos, sin = np.cos(radians), np.sin(radians)
    return const, np.concatenate([cos, cos]), np.concatenate([-sin, sin])


def kernel(**inputs):
    import concourse.bacc as bacc
    from concourse.bass_utils import run_bass_kernel_spmd

    a = {n: np.asarray(v) for n, v in inputs.items()}
    const, cos, sin = constants()

    def swapped(w):
        return np.concatenate([w[:, C // 2:], w[:, :C // 2]], axis=1)

    wq, wk, wv = (a["L0_attn_a_" + n][0] for n in ("wq", "wk", "wv"))
    big = {"f": a["L0_attn_b_Wf"], "q": a["L0_attn_b_Wq"], "g": a["L0_attn_b_Wg"], "k": a["L0_attn_b_Wk"], "v": a["L0_attn_b_Wv"]}
    arrays = {
        "x": a["L0_attn_a_x"],
        "const": const,
        "cos": cos,
        "sin": sin,
        "w_qkv": np.stack([wq, swapped(wq), wk, swapped(wk), wv], axis=1),
        "wo": a["L0_attn_a_wo"][0],
        "w_ffn": np.stack([a["L0_ffn_" + n].T for n in ("W_r", "W_k", "W_v")], axis=1),
        "mu": np.stack([a["L0_ffn_mu_r"], a["L0_ffn_mu_k"]], axis=1),
        "w5": np.concatenate([big[kind][:, half * G:(half + 1) * G] for kind, half in PROJ], axis=1),
        "wb": a["L0_attn_b_Wb"],
        "w_out": a["L0_attn_b_Wo"],
        "norm_w": a["L0_attn_b_norm_w"],
        "a_log": a["L0_attn_b_A_log"],
        "a_log_pairs": a["L0_attn_b_A_log"].reshape(NP, 2).T,
        "dt_bias": a["L0_attn_b_dt_bias"],
        "bg": a["L0_attn_b_bg"],
    }
    arrays = {n: np.ascontiguousarray(v) for n, v in arrays.items()}
    nc = bacc.Bacc("TRN2", target_bir_lowering=False, num_devices=1)
    io = {n: nc.dram_tensor("in_" + n, v.shape, mybir.dt.from_np(v.dtype), kind="ExternalInput").ap() for n, v in arrays.items()}
    out = nc.dram_tensor("out", (B, T, C), F32, kind="ExternalOutput").ap()
    build(nc, io, out)
    r = run_bass_kernel_spmd(nc, [{"in_" + n: v for n, v in arrays.items()}], core_ids=[0])
    return r.results[0]["out"]
```

```python
from contextlib import ExitStack

import numpy as np

import concourse.bass as bass
from concourse import mybir

F32 = mybir.dt.float32
F32R = mybir.dt.float32r
ALU = mybir.AluOpType
ACT = mybir.ActivationFunctionType
AX = mybir.AxisListType

P = 128
B, T, C = 2, 2048, 128
NT = T // P
GT = 4
G = GT * P
NG = T // G
H, D = 16, 64
HD = H * D
NP = H // 2
ROTARY_BASE = 10000.0
LN_EPS = 1e-5
RMS_EPS = 1e-5
L2_EPS = 1e-12
NEG = -1e30
HALVES = HD // G

C_IDENT, C_LAG, C_STRICT, C_NEG, C_TPOS = (k * P for k in range(5))
C_LEFT = 5 * P
C_WIDTH = 5 * P + 1


def bank_sems(sem, name, n):
    return [sem(f"{name}{k}") for k in range(n)]


def qkv_phase(nc, io, X, const, qk_hi, qk_lo, V):
    ctx = ExitStack()
    with ctx:
        sb = lambda name, shape, dt=F32: ctx.enter_context(nc.sbuf_tensor("qkv_" + name, shape, dt))
        sem = lambda name: ctx.enter_context(nc.semaphore("qkv_" + name))
        ident = const[:, C_IDENT:C_IDENT + P]
        cos = sb("cos", [P, T])
        sin = sb("sin", [P, T])
        w = sb("w", [P, 5, P])
        w_hi = sb("w_hi", [P, 4, P], F32R)
        w_lo = sb("w_lo", [P, 4, P], F32R)
        stats = sb("stats", [P, 2, GT, 6])
        mv = sb("mv", [P, 2, GT, 2])
        rstd = sb("rstd", [P, 2, GT])
        mhalf = sb("mhalf", [P, GT])
        eps = sb("eps", [P, GT])
        held = sb("held", [P, 1])
        xn = sb("xn", [P, 2, G])
        xT = sb("xT", [P, 2, G])
        x_hi = sb("x_hi", [P, 2, G], F32R)
        x_lo = sb("x_lo", [P, 2, G], F32R)
        by_cos = sb("by_cos", [P, 2, G])
        by_sin = sb("by_sin", [P, 2, G])
        rot = sb("rot", [P, 2, G])
        xt_ps = ctx.enter_context(nc.psum_tensor("qkv_xt_ps", [P, G], F32))
        pr_ps = [ctx.enter_context(nc.psum_tensor(f"qkv_pr_ps{k}", [P, G], F32)) for k in range(4)]
        v_ps = ctx.enter_context(nc.psum_tensor("qkv_v_ps", [P, G], F32))

        loaded_x, loaded_w, loaded_const, loaded_rope = (sem(n) for n in ("loaded_x", "loaded_w", "loaded_const", "loaded_rope"))
        weights_split = sem("weights_split")
        w_hi_ready = sem("w_hi_ready")
        mhalf_set = sem("mhalf_set")
        stats_ready, moments_ready, rstd_step, xn_ready = (sem(n) for n in ("stats_ready", "moments_ready", "rstd_step", "xn_ready"))
        xt_full, xt_copied, xlo_ready = (sem(n) for n in ("xt_full", "xt_copied", "xlo_ready"))
        pr_full = bank_sems(sem, "pr_full", 4)
        pr_read = bank_sems(sem, "pr_read", 4)
        rot_ready, rot_hi = bank_sems(sem, "rot_ready", 2), bank_sems(sem, "rot_hi", 2)
        rot_lo = sem("rot_lo")
        v_full, v_read = sem("v_full"), sem("v_read")

        block = ctx.enter_context(nc.Block())

        def tile_of(i, b, j):
            return b * NT + i * GT + j

        @block.sync
        def _(eng):
            eng.dma_start(const[:, :], io["const"]).then_inc(loaded_const, 16)
            for i in range(NG):
                for b in range(B):
                    src = io["x"][b, i * G:(i + 1) * G, :].rearrange("(t p) c -> p t c", p=P)
                    t0 = tile_of(i, b, 0)
                    eng.dma_start(X[:, t0:t0 + GT, :], src).then_inc(loaded_x, 16)
                    if i == 0 and b == 0:
                        eng.dma_start(w[:, :, :], io["w_qkv"]).then_inc(loaded_w, 16)
                        eng.dma_start(cos[:, :], io["cos"]).then_inc(loaded_rope, 16)
                        eng.dma_start(sin[:, :], io["sin"]).then_inc(loaded_rope, 16)
                    eng.wait_ge(loaded_x, 16 * (2 * i + b + 1))

        @block.gpsimd
        def _(eng):
            eng.memset(mhalf[:, :], -0.5).then_inc(mhalf_set, 1)
            eng.memset(eps[:, :], LN_EPS).then_inc(mhalf_set, 1)
            eng.wait_ge(loaded_w, 16)
            eng.wait_ge(w_hi_ready, 1)
            eng.tensor_tensor(w_lo[:, :, :], w[:, 0:4, :], w_hi[:, :, :].bitcast(F32), ALU.subtract).then_inc(weights_split, 1)
            eng.wait_ge(mhalf_set, 2)

            def rstds(g, b):
                eng.wait_ge(moments_ready, GT * (g + 1))
                eng.tensor_tensor(rstd[:, b, :], mv[:, b, :, 1], eps[:, :], ALU.add).then_inc(rstd_step, 1)
                eng.wait_ge(rstd_step, 2 * g + 1)
                eng.tensor_tensor(rstd[:, b, :], rstd[:, b, :], mhalf[:, :], ALU.pow).then_inc(rstd_step, 1)

            def rotated(i, b, r):
                g = 2 * i + b
                eng.wait_ge(pr_read[2 * r], g + 1)
                eng.wait_ge(pr_read[2 * r + 1], g + 1)
                eng.tensor_tensor(rot[:, r, :], by_cos[:, r, :], by_sin[:, r, :], ALU.add).then_inc(rot_ready[r], 1)
                eng.wait_ge(rot_hi[r], g + 1)
                at = (r * B + b) * T + i * G
                eng.tensor_tensor(qk_lo[:, bass.ds(at, G)], rot[:, r, :],
                                  qk_hi[:, bass.ds(at, G)].bitcast(F32), ALU.subtract).then_inc(rot_lo, 1)

            rstds(0, 0)
            with eng.Fori(0, NG - 1) as i:
                rstds(2 * i + 1, 1)
                rotated(i, 0, 0)
                rotated(i, 0, 1)
                rstds(2 * i + 2, 0)
                rotated(i, 1, 0)
                rotated(i, 1, 1)
            rstds(2 * NG - 1, 1)
            for b in range(B):
                for r in range(2):
                    rotated(NG - 1, b, r)

        @block.vector
        def _(eng):
            def moments(i, b):
                g = 2 * i + b
                eng.wait_ge(loaded_x, 16 * (g + 1))
                for j in range(GT):
                    eng.bn_stats(stats[:, b, j, :], X[:, bass.ds(tile_of(i, b, j), 1), :]).then_inc(stats_ready, 1)
                eng.wait_ge(stats_ready, GT * g + GT)
                eng.memset(held[:, :], 0.0)
                for j in range(GT):
                    eng.bn_aggr(mv[:, b, j, :], stats[:, b, j, :]).then_inc(moments_ready, 1)

            def normalize(i, b):
                g = 2 * i + b
                eng.wait_ge(rstd_step, 2 * g + 2)
                for j in range(GT):
                    eng.tensor_scalar(xn[:, b, j * P:(j + 1) * P], X[:, bass.ds(tile_of(i, b, j), 1), :],
                                      mv[:, b, j, 0:1], rstd[:, b, j:j + 1], ALU.subtract, ALU.mult).then_inc(xn_ready, 1)

            def low_x(g, b):
                eng.wait_ge(xt_copied, 2 * g + 2)
                eng.tensor_tensor(x_lo[:, b, :], xT[:, b, :], x_hi[:, b, :].bitcast(F32), ALU.subtract).then_inc(xlo_ready, 1)

            def products(i, b, r, first=False):
                g = 2 * i + b
                if not first:
                    eng.wait_ge(rot_ready[r], g)
                for k, (prod, table) in enumerate(((by_cos, cos), (by_sin, sin))):
                    eng.wait_ge(pr_full[2 * r + k], g + 1)
                    eng.tensor_tensor(prod[:, r, :], pr_ps[2 * r + k][:, :], table[:, bass.ds(i * G, G)],
                                      ALU.mult).then_inc(pr_read[2 * r + k], 1)

            moments(0, 0)
            normalize(0, 0)
            eng.wait_ge(loaded_rope, 32)

            def group(i, b, nxt, first=False):
                if nxt:
                    moments(*nxt)
                low_x(2 * i + b, b)
                products(i, b, 0, first)
                if nxt:
                    normalize(*nxt)
                products(i, b, 1, first)

            group(0, 0, (0, 1), first=True)
            group(0, 1, (1, 0))
            with eng.Fori(1, NG - 1) as i:
                group(i, 0, (i, 1))
                group(i, 1, (i + 1, 0))
            group(NG - 1, 0, (NG - 1, 1))
            group(NG - 1, 1, None)

        @block.scalar
        def _(eng):
            eng.wait_ge(loaded_w, 16)
            eng.activation(w_hi[:, :, :], w[:, 0:4, :], ACT.Copy).then_inc(w_hi_ready, 1)

            def copy_x(g, b):
                eng.wait_ge(xt_full, g + 1)
                eng.activation(xT[:, b, :], xt_ps[:, :], ACT.Copy).then_inc(xt_copied, 1)
                eng.activation(x_hi[:, b, :], xt_ps[:, :], ACT.Copy).then_inc(xt_copied, 1)

            def high_part(i, b, r):
                eng.wait_ge(rot_ready[r], 2 * i + b + 1)
                at = (r * B + b) * T + i * G
                eng.activation(qk_hi[:, bass.ds(at, G)], rot[:, r, :], ACT.Copy).then_inc(rot_hi[r], 1)

            def group(i, b, nxt):
                g = 2 * i + b
                eng.wait_ge(v_full, g + 1)
                eng.activation(V[:, bass.ds(tile_of(i, b, 0), GT), :], v_ps[:, :].rearrange("p (t c) -> p t c", t=GT),
                               ACT.Copy).then_inc(v_read, 1)
                high_part(i, b, 0)
                if nxt:
                    copy_x(*nxt)
                high_part(i, b, 1)

            copy_x(0, 0)
            with eng.Fori(0, NG - 1) as i:
                group(i, 0, (2 * i + 1, 1))
                group(i, 1, (2 * i + 2, 0))
            group(NG - 1, 0, (2 * NG - 1, 1))
            group(NG - 1, 1, None)

        @block.tensor
        def _(eng):
            eng.wait_ge(loaded_const, 16)

            def turn_x(g, b, first=False):
                if not first:
                    eng.wait_ge(xt_copied, 2 * g)
                for j in range(GT):
                    eng.wait_ge(xn_ready, GT * g + j + 1)
                    mm = eng.transpose(xt_ps[:, j * P:(j + 1) * P], xn[:, b, j * P:(j + 1) * P], ident)
                mm.then_inc(xt_full, 1)

            def values(g, b, first=False):
                eng.wait_ge(xt_copied, 2 * g + 2)
                if not first:
                    eng.wait_ge(v_read, g)
                for j in range(GT):
                    mm = eng.matmul(v_ps[:, j * P:(j + 1) * P], xT[:, b, j * P:(j + 1) * P], w[:, 4, :], start=True, stop=True)
                mm.then_inc(v_full, 1)

            def project(g, b, r, first=False):
                eng.wait_ge(xlo_ready, g + 1)
                for k in (2 * r, 2 * r + 1):
                    if not first:
                        eng.wait_ge(pr_read[k], g)
                    eng.matmul(pr_ps[k][:, :], w_hi[:, k, :], x_hi[:, b, :], start=True, stop=False)
                    eng.matmul(pr_ps[k][:, :], w_lo[:, k, :], x_hi[:, b, :], start=False, stop=False)
                    eng.matmul(pr_ps[k][:, :], w_hi[:, k, :], x_lo[:, b, :], start=False, stop=True).then_inc(pr_full[k], 1)

            def group(g, b, nxt, first=False):
                values(g, b, first)
                project(g, b, 0, first)
                if nxt:
                    turn_x(*nxt)
                project(g, b, 1, first)

            turn_x(0, 0, first=True)
            eng.wait_ge(w_hi_ready, 1)
            eng.wait_ge(weights_split, 1)
            group(0, 0, (1, 1), first=True)
            group(1, 1, (2, 0))
            with eng.Fori(1, NG - 1) as i:
                group(2 * i, 0, (2 * i + 1, 1))
                group(2 * i + 1, 1, (2 * i + 2, 0))
            group(2 * NG - 2, 0, (2 * NG - 1, 1))
            group(2 * NG - 1, 1, None)


def attention_phase(nc, io, X, const, qk_hi, qk_lo, V, w5_hi, w5_lo):
    ctx = ExitStack()
    with ctx:
        sb = lambda name, shape, dt=F32: ctx.enter_context(nc.sbuf_tensor("at_" + name, shape, dt))
        sem = lambda name: ctx.enter_context(nc.semaphore("at_" + name))
        ident = const[:, C_IDENT:C_IDENT + P]
        causal = const[:, C_NEG:C_NEG + P]
        wo = sb("wo", [P, P])
        w5_raw = sb("w5_raw", [P, 2, HD])
        q_hi = sb("q_hi", [P, 2, P], F32R)
        q_lo = sb("q_lo", [P, 2, P], F32R)
        top = sb("top", [P, 2, GT])
        ntop = sb("ntop", [P, 2, 2])
        probs = sb("probs", [P, 2, T])
        probsT = sb("probsT", [P, 2, G])
        psums = sb("psums", [P, 2, GT])
        total = sb("total", [P, 2, 2])
        o_n = sb("o_n", [P, 2, P])
        oT = sb("oT", [P, 2, P])
        s_ps = ctx.enter_context(nc.psum_tensor("at_s_ps", [P, T], F32))
        t_ps = [ctx.enter_context(nc.psum_tensor(f"at_t_ps{k}", [P, G], F32)) for k in range(2)]
        o_ps = [ctx.enter_context(nc.psum_tensor(f"at_o_ps{k}", [P, G], F32)) for k in range(2)]

        wo_loaded = sem("wo_loaded")
        w5_loaded = bank_sems(sem, "w5_loaded", 2)
        w5_hi_done, w5_lo_done = sem("w5_hi_done"), sem("w5_lo_done")
        q_here = sem("q_here")
        s_full = bank_sems(sem, "s_full", NG)
        masked, top_ready, ntop_step = sem("masked"), sem("top_ready"), sem("ntop_step")
        exp_ready = sem("exp_ready")
        t_full = bank_sems(sem, "t_full", 2)
        t_read = bank_sems(sem, "t_read", 2)
        pv_used = sem("pv_used")
        o_full, total_step, o_ready = sem("o_full"), sem("total_step"), sem("o_ready")
        x_ready = sem("x_ready")

        block = ctx.enter_context(nc.Block())

        def blocks(n):
            return n // GT + 1

        def scored(n):
            return [n // GT] + list(range(n // GT))

        BLK = [sum(blocks(m) for m in range(n)) for n in range(NT + 1)]
        BANK = [[sum(1 for m in range(n) if blocks(m) > k) for n in range(NT + 1)] for k in range(NG)]

        CREDIT = 1

        jobs = []
        for n in range(NT + 2):
            if n < NT:
                jobs += [("probs", n, j) for j in range(blocks(n))]
            if 1 <= n <= NT:
                jobs.append(("oT", n - 1, 0))
            if n >= 2:
                jobs.append(("wo", n - 2, 0))
        NJ = len(jobs)
        assert NJ % 2 == 0
        JOB = {job: k for k, job in enumerate(jobs)}

        def ring(b, job):
            k = JOB[job]
            return k % 2, b * (NJ // 2) + k // 2

        JOBS_OF = [(n, j) for n in range(NT) for j in range(blocks(n))]
        INNER = [sum(blocks(m) - 1 for m in range(n)) for n in range(NT + 1)]

        def copy_probs(eng, copy, b, n, j):
            k, before = ring(b, ("probs", n, j))
            eng.wait_ge(t_full[k], before + 1)
            width = min(G, (n + 1) * P - j * G)
            m = BLK[n] + j
            if m >= 2:
                pn, pj = JOBS_OF[m - 2]
                if pj == blocks(pn) - 1:
                    eng.wait_ge(o_full, b * NT + pn + 1 + CREDIT)
                else:
                    eng.wait_ge(pv_used, b * INNER[NT] + INNER[pn] + pj + 1)
            else:
                eng.wait_ge(o_full, b * NT + CREDIT)
            copy(probsT[:, m % 2, 0:width], t_ps[k][:, 0:width]).then_inc(t_read[k], 1)

        @block.sync
        def _(eng):
            eng.dma_start(wo[:, :], io["wo"]).then_inc(wo_loaded, 16)
            for k in range(5):
                if k >= 2:
                    eng.wait_ge(w5_lo_done, k - 1)
                eng.dma_start(w5_raw[:, k % 2, :], io["w5"][:, k * HD:(k + 1) * HD]).then_inc(w5_loaded[k % 2], 16)

        @block.gpsimd
        def _(eng):
            def bring_q(b, n):
                if n >= 2:
                    j = scored(n - 2)[-1]
                    eng.wait_ge(s_full[j], b * BANK[j][NT] + BANK[j][n - 2] + 1 + CREDIT)
                else:
                    j = scored(NT - 1)[-1]
                    eng.wait_ge(s_full[j], b * BANK[j][NT] + CREDIT)
                at = b * T + n * P
                eng.tensor_copy(q_hi[:, n % 2, :], qk_hi[:, bass.ds(at, P)]).then_inc(q_here, 1)
                eng.tensor_copy(q_lo[:, n % 2, :], qk_lo[:, bass.ds(at, P)]).then_inc(q_here, 1)

            def split_w5(k):
                eng.wait_ge(w5_loaded[k % 2], 16 * (k // 2 + 1))
                part = slice(k * HD, (k + 1) * HD)
                eng.tensor_copy(w5_hi[:, part], w5_raw[:, k % 2, :]).then_inc(w5_hi_done, 1)
                eng.wait_ge(w5_hi_done, k + 1)
                eng.tensor_tensor(w5_lo[:, part], w5_raw[:, k % 2, :], w5_hi[:, part].bitcast(F32),
                                  ALU.subtract).then_inc(w5_lo_done, 1)

            with eng.Fori(0, B) as b:
                for n in range(NT):
                    bring_q(b, n)
            for k in range(5):
                split_w5(k)

        @block.tensor
        def _(eng):
            eng.wait_ge(wo_loaded, 16)
            eng.sem_inc(o_full, CREDIT)
            for j in range(NG):
                eng.sem_inc(s_full[j], CREDIT)

            def scores(b, n):
                N = b * NT + n
                eng.wait_ge(q_here, 2 * N + 2)
                for j in scored(n):
                    used = BLK[n - 1] + j + 1 if n >= 1 and j < blocks(n - 1) else 0
                    eng.wait_ge(exp_ready, b * BLK[NT] + used + CREDIT)
                    width = G if j < n // GT else max(2 * P, (n % GT + 1) * P)
                    at = (B + b) * T + j * G
                    out = s_ps[:, j * G:j * G + width]
                    k_hi, k_lo = qk_hi[:, bass.ds(at, width)], qk_lo[:, bass.ds(at, width)]
                    eng.matmul(out, q_hi[:, n % 2, :], k_hi, start=True, stop=False)
                    eng.matmul(out, q_lo[:, n % 2, :], k_hi, start=False, stop=False)
                    eng.matmul(out, q_hi[:, n % 2, :], k_lo, start=False, stop=True).then_inc(s_full[j], 1)

            def wait_bank(b, job):
                k, before = ring(b, job)
                eng.wait_ge(t_read[k], before + CREDIT)
                return t_ps[k], t_full[k]

            def transposes(b, n, j):
                N = b * NT + n
                eng.wait_ge(exp_ready, b * BLK[NT] + BLK[n] + j + 1 + CREDIT)
                bank, full = wait_bank(b, ("probs", n, j))
                for t in range(min(GT, n + 1 - j * GT)):
                    mm = eng.transpose(bank[:, t * P:(t + 1) * P], probs[:, n % 2, (j * GT + t) * P:(j * GT + t + 1) * P], ident)
                mm.then_inc(full, 1)

            def values(b, n, j):
                N = b * NT + n
                k, before = ring(b, ("probs", n, j))
                eng.wait_ge(t_read[k], before + 1 + CREDIT)
                if j == 0:
                    if n >= 2:
                        eng.wait_ge(o_ready, N - 1 + CREDIT)
                    else:
                        eng.wait_ge(o_ready, b * NT + CREDIT)
                for t in range(min(GT, n + 1 - j * GT)):
                    kt = j * GT + t
                    mm = eng.matmul(o_ps[n % 2][:, 0:P], probsT[:, (BLK[n] + j) % 2, t * P:(t + 1) * P],
                                    V[:, bass.ds(b * NT + kt, 1), :], start=(kt == 0), stop=(kt == n))
                    if kt == n:
                        mm.then_inc(o_full, 1)
                    elif t == GT - 1:
                        mm.then_inc(pv_used, 1)

            def turn_o(b, n):
                eng.wait_ge(o_ready, b * NT + n + 1 + CREDIT)
                bank, full = wait_bank(b, ("oT", n, 0))
                eng.transpose(bank[:, 0:P], o_n[:, n % 2, :], ident).then_inc(full, 1)

            def project_o(b, n):
                k, before = ring(b, ("oT", n, 0))
                eng.wait_ge(t_read[k], before + 1 + CREDIT)
                bank, full = wait_bank(b, ("wo", n, 0))
                eng.matmul(bank[:, 0:P], oT[:, n % 2, :], wo[:, :], start=True, stop=True).then_inc(full, 1)

            with eng.Fori(0, B) as b:
                scores(b, 0)
                for n in range(NT + 2):
                    last = blocks(n) if n < NT else 0
                    for j in range(min(last, 2)):
                        transposes(b, n, j)
                    if n + 1 < NT:
                        scores(b, n + 1)
                    for j in range(last):
                        values(b, n, j)
                        if j + 2 < last:
                            transposes(b, n, j + 2)
                    if 1 <= n <= NT:
                        turn_o(b, n - 1)
                    if n >= 2:
                        project_o(b, n - 2)

        @block.vector
        def _(eng):
            def maxima(b, n):
                N = b * NT + n
                last = n // GT
                for j in scored(n):
                    eng.wait_ge(s_full[j], b * BANK[j][NT] + BANK[j][n] + 1 + CREDIT)
                    if j == last:
                        diag = s_ps[:, n * P:(n + 1) * P]
                        eng.tensor_tensor(diag, diag, causal, ALU.add).then_inc(masked, 1)
                        eng.wait_ge(masked, N + 1)
                    end = min((j + 1) * G, (n + 1) * P)
                    eng.tensor_reduce(top[:, n % 2, j:j + 1], s_ps[:, j * G:end], AX.X, ALU.max).then_inc(top_ready, 1)
                eng.wait_ge(top_ready, b * BLK[NT] + BLK[n + 1])
                eng.tensor_reduce(ntop[:, n % 2, 0:1], top[:, n % 2, 0:blocks(n)], AX.X, ALU.max, negate=True).then_inc(ntop_step, 1)
                eng.wait_ge(ntop_step, 2 * N + 1)
                eng.tensor_scalar(ntop[:, n % 2, 1:2], ntop[:, n % 2, 0:1], 1.0 / C, None, ALU.mult).then_inc(ntop_step, 1)

            def sum_rows(b, n):
                N = b * NT + n
                eng.wait_ge(exp_ready, b * BLK[NT] + BLK[n + 1] + CREDIT)
                eng.tensor_reduce(total[:, n % 2, 0:1], psums[:, n % 2, 0:blocks(n)], AX.X, ALU.add).then_inc(total_step, 1)
                eng.wait_ge(total_step, 2 * N + 1)
                eng.reciprocal(total[:, n % 2, 1:2], total[:, n % 2, 0:1]).then_inc(total_step, 1)

            def copy_oT(b, n):
                k, before = ring(b, ("oT", n, 0))
                eng.wait_ge(t_full[k], before + 1)
                eng.tensor_copy(oT[:, n % 2, :], t_ps[k][:, 0:P]).then_inc(t_read[k], 1)

            def residual(b, n):
                k, before = ring(b, ("wo", n, 0))
                eng.wait_ge(t_full[k], before + 1)
                xt = X[:, bass.ds(b * NT + n, 1), :]
                eng.tensor_tensor(xt, t_ps[k][:, 0:P].rearrange("p (t c) -> p t c", t=1), xt, ALU.add).then_inc(t_read[k], 1)

            for k in range(2):
                eng.sem_inc(t_read[k], CREDIT)
            with eng.Fori(0, B) as b:
                maxima(b, 0)
                for n in range(NT + 2):
                    last = blocks(n) if n < NT else 0
                    if n + 1 < NT:
                        maxima(b, n + 1)
                    if n < NT:
                        sum_rows(b, n)
                    for j in range(2, last):
                        copy_probs(eng, eng.tensor_copy, b, n, j)
                    if 1 <= n <= NT:
                        copy_oT(b, n - 1)
                    if n >= 2:
                        residual(b, n - 2)

        @block.scalar
        def _(eng):
            def exponentials(b, n):
                N = b * NT + n
                eng.wait_ge(ntop_step, 2 * N + 2)
                if n >= 2:
                    k, before = ring(b, ("probs", n - 2, blocks(n - 2) - 1))
                    eng.wait_ge(t_full[k], before + 1)
                else:
                    eng.wait_ge(o_full, b * NT + CREDIT)
                for j in range(blocks(n)):
                    end = min((j + 1) * G, (n + 1) * P)
                    eng.activation(probs[:, n % 2, j * G:end], s_ps[:, j * G:end], ACT.Exp, bias=ntop[:, n % 2, 1:2],
                                   scale=1.0 / C, accum_out=psums[:, n % 2, j:j + 1]).then_inc(exp_ready, 1)

            def scale_o(b, n):
                N = b * NT + n
                eng.wait_ge(o_full, N + 1 + CREDIT)
                eng.wait_ge(total_step, 2 * N + 2)
                eng.activation(o_n[:, n % 2, :], o_ps[n % 2][:, 0:P], ACT.Copy, scale=total[:, n % 2, 1:2]).then_inc(o_ready, 1)

            eng.sem_inc(exp_ready, CREDIT)
            eng.sem_inc(o_ready, CREDIT)
            with eng.Fori(0, B) as b:
                exponentials(b, 0)
                for n in range(NT):
                    for j in range(min(blocks(n), 2)):
                        copy_probs(eng, lambda o, i: eng.activation(o, i, ACT.Copy), b, n, j)
                    if n + 1 < NT:
                        exponentials(b, n + 1)
                    scale_o(b, n)


class Tile:

    def __init__(self, i, off):
        self.i, self.off = i, off
        self.m = 2 * i + off
        self.b = off % 2
        self.n = i + off // 2
        self.x = (off % 2) * NT + i + off // 2

    def later(self, k):
        return Tile(self.i, self.off + k)

    def count(self, per_tile, k=0):
        return 2 * per_tile * self.i + per_tile * self.off + k


def ffn_weights(nc, io, sb, sem):
    w = sb("fw_w", [P, 3, P])
    mu = sb("fw_mu", [P, 2])
    rest = sb("fw_rest", [P, 2])
    wr = sb("fw_wr", [P, 2, P])
    wk = sb("fw_wk", [P, 2, P])
    wk_hi = sb("fw_wk_hi", [P, 2, P], F32R)
    wk_lo = sb("fw_wk_lo", [P, 2, P], F32R)
    wv = sb("fw_wv", [P, P])
    loaded, rest_ready, scaled, wk_hi_ready, wk_lo_ready = (
        sem("fw_" + n) for n in ("loaded", "rest_ready", "scaled", "wk_hi_ready", "wk_lo_ready"))
    with nc.Block() as block:
        @block.sync
        def _(eng):
            eng.dma_start(w[:, :, :], io["w_ffn"]).then_inc(loaded, 16)
            eng.dma_start(mu[:, :], io["mu"]).then_inc(loaded, 16)

        @block.vector
        def _(eng):
            eng.wait_ge(loaded, 32)
            eng.tensor_scalar(rest[:, :], mu[:, :], -1.0, 1.0, ALU.mult, ALU.add).then_inc(rest_ready, 1)
            eng.tensor_scalar(wk[:, 0, :], w[:, 1, :], mu[:, 1:2], None, ALU.mult).then_inc(scaled, 1)
            eng.wait_ge(rest_ready, 1)
            eng.tensor_scalar(wk[:, 1, :], w[:, 1, :], rest[:, 1:2], None, ALU.mult).then_inc(scaled, 1)
            eng.tensor_scalar(wr[:, 0, :], w[:, 0, :], mu[:, 0:1], None, ALU.mult).then_inc(scaled, 1)
            eng.tensor_scalar(wr[:, 1, :], w[:, 0, :], rest[:, 0:1], None, ALU.mult).then_inc(scaled, 1)
            eng.tensor_scalar(wv[:, :], w[:, 2, :], 0.5, None, ALU.mult).then_inc(scaled, 1)

        @block.scalar
        def _(eng):
            eng.wait_ge(scaled, 2)
            eng.activation(wk_hi[:, :, :], wk[:, :, :], ACT.Copy).then_inc(wk_hi_ready, 1)

        @block.gpsimd
        def _(eng):
            eng.wait_ge(wk_hi_ready, 1)
            eng.tensor_tensor(wk_lo[:, :, :], wk[:, :, :], wk_hi[:, :, :].bitcast(F32), ALU.subtract).then_inc(wk_lo_ready, 1)
    return wr, wk_hi, wk_lo, wv


def ffn_phase(nc, X, const, weights, name, out=None):
    wr, wk_hi, wk_lo, wv = weights
    ctx = ExitStack()
    with ctx:
        sb = lambda what, shape, dt=F32: ctx.enter_context(nc.sbuf_tensor(name + what, shape, dt))
        sem = lambda what: ctx.enter_context(nc.semaphore(name + what))
        psum = lambda what: ctx.enter_context(nc.psum_tensor(name + what, [P, G], F32))
        ident = const[:, C_IDENT:C_IDENT + P]
        mhalf = sb("mhalf", [P, GT])
        eps = sb("eps", [P, GT])
        held = sb("held", [P, 1])
        stats = sb("stats", [P, 2, GT, 6])
        mv = sb("mv", [P, 2, GT, 2])
        rstd = sb("rstd", [P, 2, GT])
        xn = sb("xn", [P, 2, G])
        xT = sb("xT", [P, 2, 1 + G])
        x_hi = sb("x_hi", [P, 2, 1 + G], F32R)
        x_lo = sb("x_lo", [P, 2, 1 + G], F32R)
        k_pos = sb("k_pos", [P, 2, G])
        k_act = sb("k_act", [P, 2, G])
        r_tanh = sb("r_tanh", [P, 2, G])
        gated = sb("gated", [P, 2, G])
        xt_ps = [psum(f"xt_ps{b}") for b in range(2)]
        k_ps = [psum(f"k_ps{b}") for b in range(2)]
        r_ps = [psum(f"r_ps{b}") for b in range(2)]
        o_ps = [psum(f"o_ps{b}") for b in range(2)]

        (set_up, stats_ready, moments_ready, rstd_step, xn_ready, xt_full, carried, xt_ready, hi_ready, lo_ready, k_full,
         k_pos_ready, k_act_ready, r_full, r_ready, o_full, gated_ready, x_ready, stored) = (sem(n) for n in (
             "set_up", "stats_ready", "moments_ready", "rstd_step", "xn_ready", "xt_full", "carried", "xt_ready", "hi_ready",
             "lo_ready", "k_full", "k_pos_ready", "k_act_ready", "r_full", "r_ready", "o_full", "gated_ready", "x_ready", "stored"))
        GROUPS = B * NG

        def run_slots(eng, slot):
            whole = (GROUPS - 1 - 2) // 2
            for k in range(2):
                slot(Tile(0, k))
            with eng.Fori(1, 1 + whole) as i:
                slot(Tile(i, 0))
                slot(Tile(i, 1))
            for k in range(2 + 2 * whole, GROUPS + 2):
                slot(Tile(0, k))

        AHEAD = 2

        def exists(g):
            return not isinstance(g.m, int) or 0 <= g.m < GROUPS

        def late(g):
            return not isinstance(g.m, int) or g.m >= 2

        def tokens(g):
            return X[:, bass.ds(g.b * NT + g.n * GT, GT), :]

        block = ctx.enter_context(nc.Block())

        @block.sync
        def _(eng):
            if out is not None:
                for k in range(GROUPS):
                    g = Tile(0, k)
                    eng.wait_ge(x_ready, k + 1)
                    eng.dma_start(out[g.b, g.n * G:(g.n + 1) * G, :].rearrange("(t p) c -> p t c", p=P),
                                  X[:, g.b * NT + g.n * GT:g.b * NT + (g.n + 1) * GT, :]).then_inc(stored, 16)
                eng.wait_ge(stored, 16 * GROUPS)

        @block.gpsimd
        def _(eng):
            eng.memset(mhalf[:, :], -0.5).then_inc(set_up, 1)
            eng.memset(eps[:, :], LN_EPS).then_inc(set_up, 1)
            eng.memset(xT[:, :, 0:1], 0.0).then_inc(set_up, 1)
            eng.wait_ge(set_up, 3)

            def rstds(g):
                eng.wait_ge(moments_ready, g.count(1, 1))
                eng.tensor_tensor(rstd[:, g.b, :], mv[:, g.b, :, 1], eps[:, :], ALU.add).then_inc(rstd_step, 1)
                eng.wait_ge(rstd_step, g.count(2, 1))
                eng.tensor_tensor(rstd[:, g.b, :], rstd[:, g.b, :], mhalf[:, :], ALU.pow).then_inc(rstd_step, 1)

            def low_part(g):
                eng.wait_ge(hi_ready, g.count(1, 1))
                eng.tensor_tensor(x_lo[:, g.b, :], xT[:, g.b, :], x_hi[:, g.b, :].bitcast(F32), ALU.subtract).then_inc(lo_ready, 1)

            def slot(g):
                if exists(g.later(1)):
                    rstds(g.later(1))
                if exists(g):
                    low_part(g)

            rstds(Tile(0, 0))
            run_slots(eng, slot)

        @block.vector
        def _(eng):
            eng.sem_inc(gated_ready, AHEAD)

            def moments(g):
                for j in range(GT):
                    mm = eng.bn_stats(stats[:, g.b, j, :], X[:, bass.ds(g.b * NT + g.n * GT + j, 1), :])
                mm.then_inc(stats_ready, 1)
                eng.wait_ge(stats_ready, g.count(1, 1))
                eng.memset(held[:, :], 0.0)
                for j in range(GT):
                    mm = eng.bn_aggr(mv[:, g.b, j, :], stats[:, g.b, j, :])
                mm.then_inc(moments_ready, 1)

            def normalize(g):
                eng.wait_ge(rstd_step, g.count(2, 2))
                if late(g):
                    eng.wait_ge(xt_full, g.count(1, -1))
                for j in range(GT):
                    eng.tensor_scalar(xn[:, g.b, j * P:(j + 1) * P], X[:, bass.ds(g.b * NT + g.n * GT + j, 1), :],
                                      mv[:, g.b, j, 0:1], rstd[:, g.b, j:j + 1], ALU.subtract, ALU.mult).then_inc(xn_ready, 1)

            def output(g):
                eng.wait_ge(r_ready, g.count(1, AHEAD + 1))
                eng.wait_ge(o_full, g.count(1, AHEAD + 1))
                eng.scalar_tensor_tensor(gated[:, g.b, :], r_tanh[:, g.b, :], 1.0, o_ps[g.b][:, :], ALU.add, ALU.mult).then_inc(gated_ready, 1)
                eng.wait_ge(gated_ready, g.count(1, AHEAD + 1))
                eng.tensor_tensor(tokens(g), gated[:, g.b, :].rearrange("p (t c) -> p t c", t=GT), tokens(g), ALU.add).then_inc(x_ready, 1)

            def slot(g):
                if exists(g):
                    normalize(g)
                if exists(g.later(1)):
                    moments(g.later(1))
                if exists(g.later(-2)):
                    output(g.later(-2))

            moments(Tile(0, 0))
            run_slots(eng, slot)

        @block.scalar
        def _(eng):
            eng.sem_inc(r_ready, AHEAD)
            eng.sem_inc(k_pos_ready, AHEAD)
            eng.wait_ge(set_up, 3)

            def copy_x(g):
                eng.wait_ge(xt_full, g.count(1, 1))
                if late(g):
                    eng.wait_ge(k_full, g.count(1, -1))
                    eng.wait_ge(r_full, g.count(1, -1))
                    eng.activation(xT[:, g.b, 0:1], xT[:, g.b, G:G + 1], ACT.Copy).then_inc(carried, 1)
                    eng.wait_ge(carried, g.count(1, -1))
                eng.activation(xT[:, g.b, 1:1 + G], xt_ps[g.b][:, :], ACT.Copy).then_inc(xt_ready, 1)
                eng.wait_ge(xt_ready, g.count(1, 1))
                eng.activation(x_hi[:, g.b, :], xT[:, g.b, :], ACT.Copy).then_inc(hi_ready, 1)

            def tanh(g):
                eng.wait_ge(r_full, g.count(1, 1))
                eng.wait_ge(gated_ready, g.count(1, AHEAD - 1))
                eng.activation(r_tanh[:, g.b, :], r_ps[g.b][:, :], ACT.Tanh, scale=0.5).then_inc(r_ready, 1)

            def square(g):
                eng.wait_ge(k_full, g.count(1, 1))
                eng.activation(k_pos[:, g.b, :], k_ps[g.b][:, :], ACT.Relu).then_inc(k_pos_ready, 1)
                eng.wait_ge(k_pos_ready, g.count(1, AHEAD + 1))
                eng.wait_ge(o_full, g.count(1, AHEAD - 1))
                eng.activation(k_act[:, g.b, :], k_pos[:, g.b, :], ACT.Square).then_inc(k_act_ready, 1)

            def slot(g):
                if exists(g):
                    copy_x(g)
                if exists(g.later(-1)):
                    tanh(g.later(-1))
                    square(g.later(-1))

            run_slots(eng, slot)

        @block.tensor
        def _(eng):
            eng.sem_inc(o_full, AHEAD)

            def turn(g):
                if late(g):
                    eng.wait_ge(xt_ready, g.count(1, -1))
                for j in range(GT):
                    eng.wait_ge(xn_ready, g.count(GT, j + 1))
                    mm = eng.transpose(xt_ps[g.b][:, j * P:(j + 1) * P], xn[:, g.b, j * P:(j + 1) * P], ident)
                mm.then_inc(xt_full, 1)

            def keys(g):
                eng.wait_ge(lo_ready, g.count(1, 1))
                eng.wait_ge(k_pos_ready, g.count(1, AHEAD - 1))
                for shift in range(2):
                    hi, lo = x_hi[:, g.b, 1 - shift:1 - shift + G], x_lo[:, g.b, 1 - shift:1 - shift + G]
                    eng.matmul(k_ps[g.b][:, :], wk_hi[:, shift, :], hi, start=(shift == 0), stop=False)
                    eng.matmul(k_ps[g.b][:, :], wk_lo[:, shift, :], hi, start=False, stop=False)
                    mm = eng.matmul(k_ps[g.b][:, :], wk_hi[:, shift, :], lo, start=False, stop=(shift == 1))
                mm.then_inc(k_full, 1)

            def receptance(g):
                eng.wait_ge(xt_ready, g.count(1, 1))
                eng.wait_ge(r_ready, g.count(1, AHEAD - 1))
                for j in range(GT):
                    ps = r_ps[g.b][:, j * P:(j + 1) * P]
                    eng.matmul(ps, xT[:, g.b, 1 + j * P:1 + (j + 1) * P], wr[:, 0, :], start=True, stop=False)
                    mm = eng.matmul(ps, xT[:, g.b, j * P:(j + 1) * P], wr[:, 1, :], start=False, stop=True)
                mm.then_inc(r_full, 1)

            def values(g):
                eng.wait_ge(k_act_ready, g.count(1, 1))
                eng.wait_ge(gated_ready, g.count(1, AHEAD - 1))
                for j in range(GT):
                    mm = eng.matmul(o_ps[g.b][:, j * P:(j + 1) * P], k_act[:, g.b, j * P:(j + 1) * P], wv[:, :], start=True, stop=True)
                mm.then_inc(o_full, 1)

            def slot(g):
                if exists(g):
                    turn(g)
                if exists(g.later(-1)):
                    receptance(g.later(-1))
                if exists(g.later(-2)):
                    values(g.later(-2))
                if exists(g.later(-1)):
                    keys(g.later(-1))

            run_slots(eng, slot)


PROJ = [("q", 0), ("f", 0), ("k", 0), ("f", 1), ("q", 1), ("g", 0), ("k", 1), ("g", 1), ("v", 0), ("v", 1)]
TURN = {job: k for k, job in enumerate(
    [("qT", 0), ("kT", 0), ("qT", 1), ("kT", 1), ("qk", 0), ("qk", 1), ("qk", 2), ("qk", 3), ("oT", 0), ("oT", 1)])}
NTURN = len(TURN)


def linear_phase(nc, io, X, const, w5_hi, w5_lo):
    ctx = ExitStack()
    with ctx:
        sb = lambda what, shape, dt=F32: ctx.enter_context(nc.sbuf_tensor("la_" + what, shape, dt))
        sem = lambda what: ctx.enter_context(nc.semaphore("la_" + what))
        psum = lambda what: ctx.enter_context(nc.psum_tensor("la_" + what, [P, G], F32))
        ident = const[:, C_IDENT:C_IDENT + P]

        w_beta = sb("w_beta", [P, H])
        w_out = sb("w_out", [P, NP, P])
        norm_w = sb("norm_w", [P, 1])
        bias_f = sb("bias_f", [P, HD])
        bias_g = sb("bias_g", [P, HD])
        rate = sb("rate", [P, H])
        rate_col = sb("rate_col", [P, NP])
        decay = sb("decay", [P, H, P])
        decay_q = sb("decay_q", [P, NP, P])
        decay_k = sb("decay_k", [P, H])
        decay_s = sb("decay_s", [P, NP])
        mhalf = sb("mhalf", [P, H])
        ones = sb("ones", [P, H])
        eps = sb("eps", [P, 1])
        held = sb("held", [P, 1])
        state = sb("state", [P, 2, NP, P])
        faded = sb("faded", [P, NP, P])

        stats = sb("stats", [P, 2, 6])
        mv = sb("mv", [P, 2, 2])
        rstd = sb("rstd", [P, 2])
        xn = sb("xn", [P, 2, P])
        xT = sb("xT", [P, 2, P])
        x_hi = sb("x_hi", [P, 2, P], F32R)
        x_lo = sb("x_lo", [P, 2, P], F32R)
        f = sb("f", [P, 2, HD])
        gate = sb("gate", [P, 2, HD])
        q = sb("q", [P, 2, HD])
        k = sb("k", [P, 2, HD])
        v = sb("v", [P, 2, HD])
        sq_q = sb("sq_q", [P, HD])
        sq_k = sb("sq_k", [P, HD])
        sq_u = sb("sq_u", [P, HD])
        ssq = sb("ssq", [P, 2, H])
        ssk = sb("ssk", [P, 2, H])
        beta = sb("beta", [P, 2, H])
        coef = sb("coef", [P, 2, H])
        vb = sb("vb", [P, 2, HD])
        kd = sb("kd", [P, 2, HD])
        qT = sb("qT", [P, NP, P])
        kT = sb("kT", [P, NP, P])
        qdT = sb("qdT", [P, NP, P])
        pT = sb("pT", [P, H, P])
        u = sb("u", [P, HD])
        ssu = sb("ssu", [P, H])
        scale = sb("scale", [P, 2, H])
        og = sb("og", [P, HD])
        oT = sb("oT", [P, NP, P])

        pr_ps = [psum(f"pr_ps{r}") for r in range(2)]
        t_ps = [psum(f"t_ps{r}") for r in range(2)]
        o_ps = [psum(f"o_ps{r}") for r in range(2)]
        m_ps = psum("m_ps")
        s_ps = psum("s_ps")

        loaded = sem("loaded")
        names = ("rate_step rate_ready set_up decay_exp decay_ready w_out_ready stats_ready moments_ready rstd_step xn_ready x_turned "
                 "xt_ready xlo_ready beta_full beta_ready fb_ready gb_ready f_ready g_ready "
                 "qsq_ready ksq_ready usq_ready qsq_summed ksq_summed ssq_ready ssk_ready ssu_ready coef_step vb_ready kd_ready faded_ready qd_ready "
                 "o_full u_ready state_full state_ready ug_ready scale_step og_ready y_full x_ready").split()
        s = {n: sem(n) for n in names}
        pr_full, pr_read = bank_sems(sem, "pr_full", 2), bank_sems(sem, "pr_read", 2)
        t_full, t_read = bank_sems(sem, "t_full", 2), bank_sems(sem, "t_read", 2)

        def by_head(ap):
            return ap.rearrange("p (h d) -> p h d", d=D)

        def over_d(ap):
            return ap.unsqueeze(2).broadcast_to([P, H, D])

        def proj(tl, job):
            k_ = PROJ.index(job)
            return k_ % 2, tl.count(5, k_ // 2)

        def projected(eng, tl, kind, half):
            bank, before = proj(tl, (kind, half))
            eng.wait_ge(pr_read[bank], before + 1)

        def turn(tl, job):
            step = tl.later(1) if job[0] == "oT" else tl
            at = NTURN * step.off + TURN[job]
            absent = 2
            if isinstance(step.i, int) and step.m == 0 and TURN[job] < TURN["oT", 0]:
                absent = 0
            if isinstance(step.i, int) and step.m == B * NT:
                absent += TURN["oT", 0]
            return at % 2, NTURN * step.i + at // 2 - absent // 2

        with nc.Block() as block:
            @block.sync
            def _(eng):
                eng.dma_start(w_beta[:, :], io["wb"]).then_inc(loaded, 16)
                eng.dma_start(w_out[:, :, :], io["w_out"].rearrange("(r p) m -> p r m", p=P)).then_inc(loaded, 16)
                for half in range(2):
                    rows = slice(half * D, (half + 1) * D)
                    eng.dma_start(norm_w[rows, :], io["norm_w"].rearrange("(d o) -> d o", o=1)).then_inc(loaded, 16)
                    eng.dma_start(rate_col[rows, :], io["a_log_pairs"][half:half + 1, :].broadcast_to([D, NP])).then_inc(loaded, 16)
                for row, where, n_ in (("dt_bias", bias_f, HD), ("bg", bias_g, HD), ("a_log", rate, H)):
                    src = io[row].rearrange("(o n) -> o n", o=1).broadcast_to([P, n_])
                    eng.dma_start(where[:, :], src).then_inc(loaded, 16)

            @block.gpsimd
            def _(eng):
                eng.memset(mhalf[:, :], -0.5).then_inc(s["set_up"], 1)
                eng.memset(ones[:, :], 1.0).then_inc(s["set_up"], 1)
                eng.memset(eps[:, :], LN_EPS).then_inc(s["set_up"], 1)
                eng.memset(state[:, :, :, :], 0.0).then_inc(s["set_up"], 1)

            @block.vector
            def _(eng):
                eng.wait_ge(loaded, 16 * 9)
                eng.tensor_scalar(w_out[:, :, :], w_out[:, :, :], norm_w[:, 0:1], 4.0, ALU.mult, ALU.mult).then_inc(s["w_out_ready"], 1)
                eng.tensor_scalar(bias_f[:, :], bias_f[:, :], -1.0, None, ALU.mult).then_inc(s["w_out_ready"], 1)
                eng.wait_ge(s["rate_step"], 2)
                for r in (rate, rate_col):
                    eng.tensor_scalar(r[:, :], r[:, :], 1e30, -1.0, ALU.min, ALU.mult).then_inc(s["rate_ready"], 1)
                for h in range(H):
                    eng.wait_ge(s["decay_exp"], h + 1)
                    eng.tensor_tensor(decay[:, h, :], decay[:, h, :], const[:, C_STRICT:C_STRICT + P], ALU.mult).then_inc(s["decay_ready"], 1)

            @block.scalar
            def _(eng):
                eng.wait_ge(loaded, 16 * 9)
                for r in (rate, rate_col):
                    eng.activation(r[:, :], r[:, :], ACT.Exp).then_inc(s["rate_step"], 1)
                eng.wait_ge(s["rate_ready"], 2)
                for h in range(H):
                    eng.activation(decay[:, h, :], const[:, C_LAG:C_LAG + P], ACT.Exp, scale=rate[:, h:h + 1]).then_inc(s["decay_exp"], 1)
                for r in range(NP):
                    eng.activation(decay_q[:, r, :], const[:, C_TPOS:C_TPOS + P], ACT.Exp, scale=rate_col[:, r:r + 1]).then_inc(s["decay_exp"], 1)
                eng.activation(decay_k[:, :], rate[:, :], ACT.Exp, scale=const[:, C_LEFT:C_LEFT + 1]).then_inc(s["decay_exp"], 1)
                eng.activation(decay_s[:, :], rate_col[:, :], ACT.Exp, scale=float(P)).then_inc(s["decay_exp"], 1)

        LAST = B * NT - 1

        STATE_START = 2

        def exists(tl):
            return not isinstance(tl.m, int) or 0 <= tl.m <= LAST

        def run_steps(eng, step):
            step(Tile(0, 0))
            loops = (LAST - 3) // 2
            with eng.Fori(0, loops) as i:
                step(Tile(i, 1))
                step(Tile(i, 2))
            for m in range(2 * loops + 1, LAST + 1):
                step(Tile(0, m))

        block = ctx.enter_context(nc.Block())

        @block.tensor
        def _(eng):
            def turn_x(tl):
                if not isinstance(tl.m, int) or tl.m >= 3:
                    eng.wait_ge(s["x_ready"], tl.count(1, -2))
                elif tl.m == 2:
                    eng.wait_ge(s["beta_ready"], 1)
                elif tl.m == 1:
                    eng.wait_ge(s["xt_ready"], 2)
                eng.wait_ge(s["xn_ready"], tl.count(1, 1))
                eng.transpose(m_ps[:, 0:P], xn[:, tl.b, :], ident).then_inc(s["x_turned"], 1)

            def project(tl, job):
                bank, before = proj(tl, job)
                if job == PROJ[0]:
                    eng.wait_ge(s["xlo_ready"], tl.count(1, 1))
                    eng.wait_ge(s["xt_ready"], tl.count(2, 2))
                eng.wait_ge(pr_read[bank], before)
                col = PROJ.index(job) * G
                hi, lo = w5_hi[:, col:col + G], w5_lo[:, col:col + G]
                eng.matmul(pr_ps[bank][:, :], x_hi[:, tl.b, :], hi, start=True, stop=False)
                eng.matmul(pr_ps[bank][:, :], x_hi[:, tl.b, :], lo, start=False, stop=False)
                eng.matmul(pr_ps[bank][:, :], x_lo[:, tl.b, :], hi, start=False, stop=True).then_inc(pr_full[bank], 1)

            def betas(tl):
                if exists(tl.later(1)):
                    eng.wait_ge(s["xt_ready"], tl.count(2, 4))
                else:
                    eng.wait_ge(s["x_ready"], tl.count(1, -1))
                eng.matmul(m_ps[:, 0:H], xT[:, tl.b, :], w_beta[:, :], start=True, stop=True).then_inc(s["beta_full"], 1)

            def turning(tl, job):
                bank, before = turn(tl, job)
                eng.wait_ge(t_read[bank], before)
                return t_ps[bank], t_full[bank]

            def turned(tl, job):
                bank, before = turn(tl, job)
                eng.wait_ge(t_read[bank], before + 1)

            def turn_qk(tl, job):
                kind, half = job
                projected(eng, tl, kind[0], half)
                ps, full = turning(tl, job)
                src = (q if kind == "qT" else k)[:, tl.b, :]
                for r in range(4):
                    pair = 4 * half + r
                    mm = eng.transpose(ps[:, r * P:(r + 1) * P], src[:, pair * P:(pair + 1) * P], ident)
                mm.then_inc(full, 1)

            def scores(tl, n_):
                banks = [turning(tl, ("qk", 2 * n_ + odd)) for odd in range(2)]
                for r in range(4):
                    for odd, (ps, full) in enumerate(banks):
                        rows, pair = slice(odd * D, (odd + 1) * D), 4 * n_ + r
                        mm = eng.matmul(ps[:, r * P:(r + 1) * P], kT[rows, pair, :], qT[rows, pair, :], start=True, stop=True)
                        if r == 3:
                            mm.then_inc(full, 1)

            def update(tl):
                eng.wait_ge(s["kd_ready"], tl.count(1, 1))
                eng.wait_ge(s["vb_ready"], tl.count(1, 1))
                eng.wait_ge(s["state_ready"], tl.count(2, STATE_START))
                for h in range(H):
                    rows, cols = slice((h % 2) * D, (h % 2 + 1) * D), slice(h * D, (h + 1) * D)
                    mm = eng.matmul(s_ps[rows, (h // 2) * D:(h // 2 + 1) * D], kd[:, tl.b, cols], vb[:, tl.b, cols], start=True, stop=True)
                mm.then_inc(s["state_full"], 1)

            def attend(tl):
                eng.wait_ge(s["qd_ready"], tl.count(1, 1))
                eng.wait_ge(s["vb_ready"], tl.count(1, 1))
                eng.wait_ge(s["state_ready"], tl.count(2, STATE_START - 2))
                for half in range(2):
                    if exists(tl.later(-1)):
                        eng.wait_ge(s["u_ready"], tl.count(2, half - 1))
                    turned(tl, ("qk", 2 * half))
                    turned(tl, ("qk", 2 * half + 1))
                    for pair in range(4 * half, 4 * half + 4):
                        at = (pair % 4) * P
                        eng.matmul(o_ps[half][:, at:at + P], qdT[:, pair, :], state[:, tl.b, pair, :], start=True, stop=False,
                                   skip_group_check=True)
                        for h in (2 * pair, 2 * pair + 1):
                            at = (h % 8) * D
                            mm = eng.matmul(o_ps[half][:, at:at + D], pT[:, h, :], vb[:, tl.b, h * D:(h + 1) * D], start=False, stop=True,
                                            skip_group_check=True)
                    mm.then_inc(s["o_full"], 1)

            def turn_o(tl, half):
                if half == 0:
                    eng.wait_ge(s["og_ready"], tl.count(1, 1))
                ps, full = turning(tl, ("oT", half))
                for r in range(4):
                    pair = 4 * half + r
                    mm = eng.transpose(ps[:, r * P:(r + 1) * P], og[:, pair * P:(pair + 1) * P], ident)
                mm.then_inc(full, 1)

            def project_out(tl):
                turned(tl, ("oT", 0))
                turned(tl, ("oT", 1))
                eng.wait_ge(s["x_ready"], tl.count(1, 1))
                eng.wait_ge(s["beta_ready"], min(tl.m + 3, LAST + 1) if isinstance(tl.m, int) else tl.count(1, 3))
                for pair in range(NP):
                    mm = eng.matmul(m_ps[:, 0:P], oT[:, pair, :], w_out[:, pair, :], start=(pair == 0), stop=(pair == NP - 1))
                mm.then_inc(s["y_full"], 1)

            def step(tl):
                nxt, prv = tl.later(1), tl.later(-1)
                own = [lambda j=j: turn_qk(tl, j) for j in (("qT", 0), ("kT", 0), ("qT", 1), ("kT", 1))]
                own += [lambda: turn_x(tl.later(2)) if exists(tl.later(2)) else None, lambda: scores(tl, 0),
                        lambda: betas(nxt) if exists(nxt) else None, lambda: scores(tl, 1)]
                for n_, job in enumerate(PROJ):
                    if exists(nxt):
                        project(nxt, job)
                    if n_ < len(own):
                        own[n_]()
                if exists(prv):
                    turn_o(prv, 0)
                    turn_o(prv, 1)
                attend(tl)
                if exists(prv):
                    project_out(prv)
                update(tl)

            turn_x(Tile(0, 0))
            turn_x(Tile(0, 1))
            for job in PROJ:
                project(Tile(0, 0), job)
            betas(Tile(0, 0))
            run_steps(eng, step)
            turn_o(Tile(0, LAST), 0)
            turn_o(Tile(0, LAST), 1)
            project_out(Tile(0, LAST))

        @block.vector
        def _(eng):
            def layer_norm(tl):
                eng.bn_stats(stats[:, tl.b, :], X[:, bass.ds(tl.x, 1), :]).then_inc(s["stats_ready"], 1)
                eng.wait_ge(s["stats_ready"], tl.count(1, 1))
                eng.memset(held[:, :], 0.0)
                eng.bn_aggr(mv[:, tl.b, :], stats[:, tl.b, :]).then_inc(s["moments_ready"], 1)

            def normalize(tl):
                eng.wait_ge(s["rstd_step"], tl.count(2, 2))
                eng.tensor_scalar(xn[:, tl.b, :], X[:, bass.ds(tl.x, 1), :], mv[:, tl.b, 0:1], rstd[:, tl.b:tl.b + 1],
                                  ALU.subtract, ALU.mult).then_inc(s["xn_ready"], 1)

            def add_bias(tl, job):
                bank, before = proj(tl, job)
                eng.wait_ge(pr_full[bank], before + 1)
                kind, half = job
                where, bias, ready = (f, bias_f, s["fb_ready"]) if kind == "f" else (gate, bias_g, s["gb_ready"])
                part = slice(half * G, (half + 1) * G)
                if half == 0 and (not isinstance(tl.m, int) or tl.m >= 1):
                    if kind == "f":
                        eng.wait_ge(s["u_ready"], tl.count(2, -2))
                    else:
                        eng.wait_ge(s["ug_ready"], tl.count(1, -1))
                eng.tensor_tensor(where[:, tl.b, part], pr_ps[bank][:, :], bias[:, part], ALU.add).then_inc(pr_read[bank], 1)

            def decayed(tl, n_):
                bank, before = turn(tl, ("qk", n_))
                eng.wait_ge(t_full[bank], before + 1)
                if n_ == 0:
                    eng.wait_ge(s["o_full"], tl.count(2))
                heads = slice(8 * (n_ // 2) + n_ % 2, 8 * (n_ // 2) + 8, 2)
                eng.tensor_tensor(pT[:, heads, :], t_ps[bank][:, :].rearrange("p (h t) -> p h t", h=4),
                                  decay[:, heads, :], ALU.mult).then_inc(t_read[bank], 1)

            def gate_o(tl):
                for half in range(2):
                    part = slice(half * G, (half + 1) * G)
                    eng.wait_ge(s["o_full"], tl.count(2, half + 1))
                    eng.wait_ge(s["f_ready"], tl.count(1, 1))
                    eng.scalar_tensor_tensor(u[:, part], f[:, tl.b, part], 1.0, o_ps[half][:, :], ALU.add, ALU.mult).then_inc(s["u_ready"], 1)

            def new_state(tl):
                eng.wait_ge(s["state_full"], tl.count(1, 1))
                eng.wait_ge(s["faded_ready"], tl.count(1, 1))
                for half in range(2):
                    rows = slice(half * D, (half + 1) * D)
                    ps = s_ps[rows, :].rearrange("p (r e) -> p r e", r=NP)
                    cols = slice(half * D, (half + 1) * D)
                    eng.tensor_tensor(state[rows, tl.b, :, cols], ps, faded[rows, :, cols], ALU.add).then_inc(s["state_ready"], 1)

            def sum_squares(tl, where, sq, ready, done):
                eng.wait_ge(s[ready], tl.count(1, 1))
                eng.tensor_reduce(where, by_head(sq[:, :]), AX.X, ALU.add).then_inc(s[done], 1)

            def guard(tl, where, summed, factor, ready):
                eng.wait_ge(s[summed], tl.count(1, 1))
                eng.tensor_scalar(where, where, L2_EPS ** 2, factor, ALU.max, ALU.mult).then_inc(s[ready], 1)

            def gate_u(tl):
                eng.wait_ge(s["g_ready"], tl.count(1, 1))
                eng.wait_ge(s["usq_ready"], tl.count(1, 1))
                eng.scalar_tensor_tensor(u[:, :], gate[:, tl.b, :], 1.0, u[:, :], ALU.add, ALU.mult).then_inc(s["ug_ready"], 1)

            def residual(tl):
                eng.wait_ge(s["y_full"], tl.count(1, 1))
                xs = X[:, bass.ds(tl.x, 1), :]
                eng.tensor_tensor(xs, m_ps[:, 0:P].rearrange("p (t c) -> p t c", t=1), xs, ALU.add).then_inc(s["x_ready"], 1)

            def step(tl):
                nxt, prv = tl.later(1), tl.later(-1)
                if exists(nxt):
                    add_bias(nxt, ("f", 0))
                if exists(prv):
                    new_state(prv)
                if exists(nxt):
                    add_bias(nxt, ("f", 1))
                if exists(tl.later(2)):
                    normalize(tl.later(2))
                if exists(nxt):
                    add_bias(nxt, ("g", 0))
                decayed(tl, 0)
                decayed(tl, 1)
                if exists(nxt):
                    add_bias(nxt, ("g", 1))
                    sum_squares(nxt, ssk[:, nxt.b, :], sq_k, "ksq_ready", "ksq_summed")
                    guard(nxt, ssk[:, nxt.b, :], "ksq_summed", 4.0, "ssk_ready")
                decayed(tl, 2)
                decayed(tl, 3)
                if exists(nxt):
                    if exists(prv):
                        eng.wait_ge(s["scale_step"], nxt.count(2, -3))
                    sum_squares(nxt, ssq[:, nxt.b, :], sq_q, "qsq_ready", "qsq_summed")
                    guard(nxt, ssq[:, nxt.b, :], "qsq_summed", 256 * RMS_EPS, "ssq_ready")
                if exists(tl.later(3)):
                    layer_norm(tl.later(3))
                gate_o(tl)
                if exists(prv):
                    residual(prv)
                sum_squares(tl, ssu[:, :], sq_u, "usq_ready", "ssu_ready")
                gate_u(tl)

            eng.sem_inc(s["x_ready"], 1)
            eng.sem_inc(s["state_ready"], STATE_START)
            for m in range(3):
                layer_norm(Tile(0, m))
                if m < 2:
                    normalize(Tile(0, m))
            for job in (("f", 0), ("f", 1), ("g", 0), ("g", 1)):
                add_bias(Tile(0, 0), job)
            sum_squares(Tile(0, 0), ssk[:, 0, :], sq_k, "ksq_ready", "ksq_summed")
            guard(Tile(0, 0), ssk[:, 0, :], "ksq_summed", 4.0, "ssk_ready")
            sum_squares(Tile(0, 0), ssq[:, 0, :], sq_q, "qsq_ready", "qsq_summed")
            guard(Tile(0, 0), ssq[:, 0, :], "qsq_summed", 256 * RMS_EPS, "ssq_ready")
            run_steps(eng, step)
            end = Tile(0, LAST)
            new_state(end)
            residual(end)

        @block.scalar
        def _(eng):
            def copy_x(tl):
                eng.wait_ge(s["x_turned"], tl.count(1, 1))
                eng.activation(xT[:, tl.b, :], m_ps[:, 0:P], ACT.Copy).then_inc(s["xt_ready"], 1)
                eng.activation(x_hi[:, tl.b, :], m_ps[:, 0:P], ACT.Copy).then_inc(s["xt_ready"], 1)

            def silu(tl, job):
                bank, before = proj(tl, job)
                kind, half = job
                eng.wait_ge(pr_full[bank], before + 1)
                where = {"q": q, "k": k, "v": v}[kind]
                eng.activation(where[:, tl.b, half * G:(half + 1) * G], pr_ps[bank][:, :], ACT.Silu).then_inc(pr_read[bank], 1)

            def tanh(tl, where, kind, ready):
                projected(eng, tl, kind, 1)
                eng.activation(where[:, tl.b, :], where[:, tl.b, :], ACT.Tanh, scale=0.5).then_inc(s[ready], 1)

            def copy_turned(tl, job, where):
                bank, before = turn(tl, job)
                half = job[1]
                eng.wait_ge(t_full[bank], before + 1)
                eng.activation(where[:, 4 * half:4 * half + 4, :], t_ps[bank][:, :].rearrange("p (r t) -> p r t", r=4),
                               ACT.Copy).then_inc(t_read[bank], 1)

            def beta_tanh(tl):
                eng.wait_ge(s["beta_full"], tl.count(1, 1))
                eng.activation(beta[:, tl.b, :], m_ps[:, 0:H], ACT.Tanh, scale=0.5).then_inc(s["beta_ready"], 1)

            def square_q(tl):
                projected(eng, tl, "q", 1)
                if not isinstance(tl.m, int) or tl.m >= 1:
                    eng.wait_ge(s["qsq_summed"], tl.count(1))
                eng.activation(sq_q[:, :], q[:, tl.b, :], ACT.Square).then_inc(s["qsq_ready"], 1)

            def square_k(tl):
                projected(eng, tl, "k", 1)
                if not isinstance(tl.m, int) or tl.m >= 1:
                    eng.wait_ge(s["ksq_summed"], tl.count(1))
                eng.activation(sq_k[:, :], k[:, tl.b, :], ACT.Square).then_inc(s["ksq_ready"], 1)

            def square_u(tl):
                eng.wait_ge(s["u_ready"], tl.count(2, 2))
                eng.activation(sq_u[:, :], u[:, :], ACT.Square).then_inc(s["usq_ready"], 1)

            def step(tl):
                nxt, prv = tl.later(1), tl.later(-1)
                if exists(nxt):
                    silu(nxt, ("q", 0))
                copy_turned(tl, ("qT", 0), qT)
                copy_turned(tl, ("kT", 0), kT)
                if exists(nxt):
                    silu(nxt, ("k", 0))
                copy_turned(tl, ("qT", 1), qT)
                copy_turned(tl, ("kT", 1), kT)
                if exists(nxt):
                    silu(nxt, ("q", 1))
                if exists(tl.later(2)):
                    copy_x(tl.later(2))
                if exists(nxt):
                    tanh(nxt, f, "f", "f_ready")
                    silu(nxt, ("k", 1))
                    square_k(nxt)
                    square_q(nxt)
                    beta_tanh(nxt)
                    silu(nxt, ("v", 0))
                    tanh(nxt, gate, "g", "g_ready")
                    silu(nxt, ("v", 1))
                if exists(prv):
                    copy_turned(prv, ("oT", 0), oT)
                    copy_turned(prv, ("oT", 1), oT)
                square_u(tl)

            start = Tile(0, 0)
            copy_x(start)
            copy_x(Tile(0, 1))
            for job in PROJ:
                if job[0] in "qkv":
                    silu(start, job)
            tanh(start, f, "f", "f_ready")
            tanh(start, gate, "g", "g_ready")
            beta_tanh(start)
            square_k(start)
            square_q(start)
            run_steps(eng, step)
            end = Tile(0, LAST)
            copy_turned(end, ("oT", 0), oT)
            copy_turned(end, ("oT", 1), oT)

        @block.gpsimd
        def _(eng):
            def inverse_root(tl):
                eng.wait_ge(s["moments_ready"], tl.count(1, 1))
                eng.tensor_tensor(rstd[:, tl.b:tl.b + 1], mv[:, tl.b, 1:2], eps[:, :], ALU.add).then_inc(s["rstd_step"], 1)
                eng.wait_ge(s["rstd_step"], tl.count(2, 1))
                eng.tensor_tensor(rstd[:, tl.b:tl.b + 1], rstd[:, tl.b:tl.b + 1], mhalf[:, 0:1], ALU.pow).then_inc(s["rstd_step"], 1)

            def low_x(tl):
                eng.wait_ge(s["xt_ready"], tl.count(2, 2))
                eng.tensor_tensor(x_lo[:, tl.b, :], xT[:, tl.b, :], x_hi[:, tl.b, :].bitcast(F32), ALU.subtract).then_inc(s["xlo_ready"], 1)

            def coefficients(tl):
                b = tl.b
                eng.wait_ge(s["beta_ready"], tl.count(1, 1))
                eng.tensor_tensor(beta[:, b, :], beta[:, b, :], ones[:, :], ALU.add).then_inc(s["coef_step"], 1)
                eng.wait_ge(s["ssk_ready"], tl.count(1, 1))
                eng.tensor_tensor(coef[:, b, :], ssk[:, b, :], mhalf[:, :], ALU.pow).then_inc(s["coef_step"], 1)
                eng.wait_ge(s["coef_step"], tl.count(3, 2))
                eng.tensor_tensor(coef[:, b, :], coef[:, b, :], beta[:, b, :], ALU.mult).then_inc(s["coef_step"], 1)

            def weigh(tl):
                eng.wait_ge(s["coef_step"], tl.count(3, 3))
                projected(eng, tl, "v", 0)
                projected(eng, tl, "v", 1)
                if exists(tl.later(-2)):
                    eng.wait_ge(s["state_full"], tl.count(1, -1))
                eng.tensor_tensor(by_head(vb[:, tl.b, :]), by_head(v[:, tl.b, :]), over_d(coef[:, tl.b, :]), ALU.mult).then_inc(s["vb_ready"], 1)
                eng.tensor_tensor(by_head(kd[:, tl.b, :]), by_head(k[:, tl.b, :]), over_d(decay_k[:, :]), ALU.mult).then_inc(s["kd_ready"], 1)

            def fade(tl):
                eng.wait_ge(s["state_ready"], tl.count(2, STATE_START))
                eng.tensor_tensor(faded[:, :, :], state[:, tl.b, :, :], decay_s[:, :].unsqueeze(2).broadcast_to([P, NP, P]),
                                  ALU.mult).then_inc(s["faded_ready"], 1)

            def decay_queries(tl):
                bank, before = turn(tl, ("qT", 1))
                eng.wait_ge(t_read[bank], before + 1)
                eng.tensor_tensor(qdT[:, :, :], qT[:, :, :], decay_q[:, :, :], ALU.mult).then_inc(s["qd_ready"], 1)

            def scale_u(tl):
                b = tl.b
                eng.wait_ge(s["ssu_ready"], tl.count(1, 1))
                eng.tensor_tensor(scale[:, b, :], ssq[:, b, :], ssu[:, :], ALU.add).then_inc(s["scale_step"], 1)
                eng.wait_ge(s["scale_step"], tl.count(2, 1))
                eng.tensor_tensor(scale[:, b, :], scale[:, b, :], mhalf[:, :], ALU.pow).then_inc(s["scale_step"], 1)
                eng.wait_ge(s["scale_step"], tl.count(2, 2))
                eng.wait_ge(s["ug_ready"], tl.count(1, 1))
                eng.tensor_tensor(by_head(og[:, :]), by_head(u[:, :]), over_d(scale[:, b, :]), ALU.mult).then_inc(s["og_ready"], 1)

            def step(tl):
                nxt, prv = tl.later(1), tl.later(-1)
                if exists(prv):
                    scale_u(prv)
                decay_queries(tl)
                fade(tl)
                if exists(tl.later(2)):
                    low_x(tl.later(2))
                if exists(nxt):
                    coefficients(nxt)
                if exists(tl.later(3)):
                    inverse_root(tl.later(3))
                if exists(nxt):
                    weigh(nxt)

            for m in range(2):
                inverse_root(Tile(0, m))
                low_x(Tile(0, m))
            inverse_root(Tile(0, 2))
            coefficients(Tile(0, 0))
            weigh(Tile(0, 0))
            run_steps(eng, step)
            scale_u(Tile(0, LAST))


def build(nc, io, out):
    ctx = ExitStack()
    with ctx:
        sb = lambda name, shape, dt=F32: ctx.enter_context(nc.sbuf_tensor(name, shape, dt))
        X = sb("X", [P, B * NT, C])
        const = sb("const", [P, C_WIDTH])
        w5_hi = sb("w5_hi", [P, 5 * HD], F32R)
        w5_lo = sb("w5_lo", [P, 5 * HD], F32R)
        with ExitStack() as attention:
            qk_hi = attention.enter_context(nc.sbuf_tensor("qk_hi", [P, 2 * B * T], F32R))
            qk_lo = attention.enter_context(nc.sbuf_tensor("qk_lo", [P, 2 * B * T], F32R))
            V = attention.enter_context(nc.sbuf_tensor("V", [P, B * NT, C], F32))
            qkv_phase(nc, io, X, const, qk_hi, qk_lo, V)
            attention_phase(nc, io, X, const, qk_hi, qk_lo, V, w5_hi, w5_lo)
        weights = ffn_weights(nc, io, sb, lambda name: ctx.enter_context(nc.semaphore(name)))
        ffn_phase(nc, X, const, weights, "f1_")
        linear_phase(nc, io, X, const, w5_hi, w5_lo)
        ffn_phase(nc, X, const, weights, "f2_", out)


def constants():
    s = np.arange(P)[:, None]
    t = np.arange(P)[None, :]
    const = np.zeros((P, C_WIDTH), np.float32)
    const[:, C_IDENT:C_IDENT + P] = s == t
    const[:, C_LAG:C_LAG + P] = np.maximum(t - 1 - s, 0)
    const[:, C_STRICT:C_STRICT + P] = s < t
    const[:, C_NEG:C_NEG + P] = np.where(t > s, NEG, 0)
    const[:, C_TPOS:C_TPOS + P] = t
    const[:, C_LEFT] = P - 1 - np.arange(P)
    half = C // 2
    freqs = np.power(np.float32(ROTARY_BASE), -np.arange(half, dtype=np.float32) / np.float32(half)).astype(np.float32)
    radians = freqs[:, None] * np.arange(T, dtype=np.float32)[None, :]
    cos, sin = np.cos(radians), np.sin(radians)
    return const, np.concatenate([cos, cos]), np.concatenate([-sin, sin])


def kernel(**inputs):
    import concourse.bacc as bacc
    from concourse.bass_utils import run_bass_kernel_spmd

    a = {n: np.asarray(v) for n, v in inputs.items()}
    const, cos, sin = constants()

    def swapped(w):
        return np.concatenate([w[:, C // 2:], w[:, :C // 2]], axis=1)

    wq, wk, wv = (a["L0_attn_a_" + n][0] for n in ("wq", "wk", "wv"))
    big = {"f": a["L0_attn_b_Wf"], "q": a["L0_attn_b_Wq"], "g": a["L0_attn_b_Wg"], "k": a["L0_attn_b_Wk"], "v": a["L0_attn_b_Wv"]}
    arrays = {
        "x": a["L0_attn_a_x"],
        "const": const,
        "cos": cos,
        "sin": sin,
        "w_qkv": np.stack([wq, swapped(wq), wk, swapped(wk), wv], axis=1),
        "wo": a["L0_attn_a_wo"][0],
        "w_ffn": np.stack([a["L0_ffn_" + n].T for n in ("W_r", "W_k", "W_v")], axis=1),
        "mu": np.stack([a["L0_ffn_mu_r"], a["L0_ffn_mu_k"]], axis=1),
        "w5": np.concatenate([big[kind][:, half * G:(half + 1) * G] for kind, half in PROJ], axis=1),
        "wb": a["L0_attn_b_Wb"],
        "w_out": a["L0_attn_b_Wo"],
        "norm_w": a["L0_attn_b_norm_w"],
        "a_log": a["L0_attn_b_A_log"],
        "a_log_pairs": a["L0_attn_b_A_log"].reshape(NP, 2).T,
        "dt_bias": a["L0_attn_b_dt_bias"],
        "bg": a["L0_attn_b_bg"],
    }
    arrays = {n: np.ascontiguousarray(v) for n, v in arrays.items()}
    nc = bacc.Bacc("TRN2", target_bir_lowering=False, num_devices=1)
    io = {n: nc.dram_tensor("in_" + n, v.shape, mybir.dt.from_np(v.dtype), kind="ExternalInput").ap() for n, v in arrays.items()}
    out = nc.dram_tensor("out", (B, T, C), F32, kind="ExternalOutput").ap()
    build(nc, io, out)
    r = run_bass_kernel_spmd(nc, [{"in_" + n: v for n, v in arrays.items()}], core_ids=[0])
    return r.results[0]["out"]
```

```python
from contextlib import ExitStack

import numpy as np

import concourse.bass as bass
from concourse import mybir

F32 = mybir.dt.float32
F32R = mybir.dt.float32r
ALU = mybir.AluOpType
ACT = mybir.ActivationFunctionType
AX = mybir.AxisListType

P = 128
B, T, C = 2, 2048, 128
NT = T // P
GT = 4
G = GT * P
NG = T // G
H, D = 16, 64
HD = H * D
NP = H // 2
ROTARY_BASE = 10000.0
LN_EPS = 1e-5
RMS_EPS = 1e-5
L2_EPS = 1e-12
NEG = -1e30
HALVES = HD // G

C_IDENT, C_LAG, C_STRICT, C_NEG, C_TPOS = (k * P for k in range(5))
C_LEFT = 5 * P
C_WIDTH = 5 * P + 1


def bank_sems(sem, name, n):
    return [sem(f"{name}{k}") for k in range(n)]


class Tile:

    def __init__(self, i, off):
        self.i, self.off = i, off
        self.m = 2 * i + off
        self.b = off % 2
        self.n = i + off // 2
        self.x = (off % 2) * NT + i + off // 2

    def later(self, k):
        return Tile(self.i, self.off + k)

    def count(self, per_tile, k=0):
        return 2 * per_tile * self.i + per_tile * self.off + k


class Norm:

    def __init__(self, sb, sem, name, X, tiles, xn):
        self.X, self.tiles, self.xn = X, tiles, xn
        self.mhalf = sb(name + "mhalf", [P, tiles])
        self.eps = sb(name + "eps", [P, tiles])
        self.held = sb(name + "held", [P, 1])
        self.stats = sb(name + "stats", [P, 2, tiles, 6])
        self.mv = sb(name + "mv", [P, 2, tiles, 2])
        self.rstd = sb(name + "rstd", [P, 2, tiles])
        self.set_up, self.stats_ready, self.moments_ready, self.rstd_step, self.ready = (
            sem(name + n) for n in ("set_up", "stats_ready", "moments_ready", "rstd_step", "xn_ready"))

    def tile(self, g, j):
        return self.X[:, bass.ds(g.b * NT + g.n * self.tiles + j, 1), :]

    def prepare(self, eng):
        eng.memset(self.mhalf[:, :], -0.5).then_inc(self.set_up, 1)
        eng.memset(self.eps[:, :], LN_EPS).then_inc(self.set_up, 1)
        eng.wait_ge(self.set_up, 2)

    def moments(self, eng, g):
        for j in range(self.tiles):
            mm = eng.bn_stats(self.stats[:, g.b, j, :], self.tile(g, j))
        mm.then_inc(self.stats_ready, 1)
        eng.wait_ge(self.stats_ready, g.count(1, 1))
        eng.memset(self.held[:, :], 0.0)
        for j in range(self.tiles):
            mm = eng.bn_aggr(self.mv[:, g.b, j, :], self.stats[:, g.b, j, :])
        mm.then_inc(self.moments_ready, 1)

    def inverse_roots(self, eng, g):
        eng.wait_ge(self.moments_ready, g.count(1, 1))
        eng.tensor_tensor(self.rstd[:, g.b, :], self.mv[:, g.b, :, 1], self.eps[:, :], ALU.add).then_inc(self.rstd_step, 1)
        eng.wait_ge(self.rstd_step, g.count(2, 1))
        eng.tensor_tensor(self.rstd[:, g.b, :], self.rstd[:, g.b, :], self.mhalf[:, :], ALU.pow).then_inc(self.rstd_step, 1)

    def normalize(self, eng, g):
        eng.wait_ge(self.rstd_step, g.count(2, 2))
        for j in range(self.tiles):
            eng.tensor_scalar(self.xn[:, g.b, j * P:(j + 1) * P], self.tile(g, j), self.mv[:, g.b, j, 0:1],
                              self.rstd[:, g.b, j:j + 1], ALU.subtract, ALU.mult).then_inc(self.ready, 1)

    def first_vector(self, eng):
        for k in range(2):
            self.moments(eng, Tile(0, k))
        for k in range(2):
            self.normalize(eng, Tile(0, k))

    def first_gpsimd(self, eng):
        self.prepare(eng)
        for k in range(2):
            self.inverse_roots(eng, Tile(0, k))


def qkv_phase(nc, io, X, const, qk_hi, qk_lo, V):
    ctx = ExitStack()
    with ctx:
        sb = lambda name, shape, dt=F32: ctx.enter_context(nc.sbuf_tensor("qkv_" + name, shape, dt))
        sem = lambda name: ctx.enter_context(nc.semaphore("qkv_" + name))
        psum = lambda name: ctx.enter_context(nc.psum_tensor("qkv_" + name, [P, G], F32))
        ident = const[:, C_IDENT:C_IDENT + P]
        cos = sb("cos", [P, T])
        sin = sb("sin", [P, T])
        w = sb("w", [P, 5, P])
        w_hi = sb("w_hi", [P, 4, P], F32R)
        w_lo = sb("w_lo", [P, 4, P], F32R)
        stats = sb("stats", [P, 2, GT, 6])
        mv = sb("mv", [P, 2, GT, 2])
        rstd = sb("rstd", [P, 2, GT])
        shift = sb("shift", [P, 2, GT])
        mhalf = sb("mhalf", [P, GT])
        eps = sb("eps", [P, GT])
        held = sb("held", [P, 1])
        xn = sb("xn", [P, 2, G])
        xT = sb("xT", [P, 2, G])
        x_hi = sb("x_hi", [P, 2, G], F32R)
        x_lo = sb("x_lo", [P, 2, G], F32R)
        by_cos = sb("by_cos", [P, 2, G])
        by_sin = sb("by_sin", [P, 2, G])
        rot = sb("rot", [P, 2, 2, G])
        xt_ps = [psum(f"xt_ps{b}") for b in range(2)]
        pr_ps = [psum(f"pr_ps{k}") for k in range(4)]
        v_ps = [psum(f"v_ps{b}") for b in range(2)]

        (loaded_x, loaded_w, loaded_const, loaded_rope, set_up, w_hi_ready, w_lo_ready, stats_ready, moments_ready, rstd_step,
         shift_ready, xn_ready, xt_full, xt_copied, xlo_ready, v_full, v_read) = (sem(n) for n in (
             "loaded_x", "loaded_w", "loaded_const", "loaded_rope", "set_up", "w_hi_ready", "w_lo_ready", "stats_ready",
             "moments_ready", "rstd_step", "shift_ready", "xn_ready", "xt_full", "xt_copied", "xlo_ready", "v_full", "v_read"))
        pr_full, pr_read = bank_sems(sem, "pr_full", 4), bank_sems(sem, "pr_read", 4)
        rot_ready, rot_hi, rot_lo = (bank_sems(sem, n, 2) for n in ("rot_ready", "rot_hi", "rot_lo"))

        GROUPS = B * NG
        AHEAD = 2

        def run_slots(eng, slot):
            whole = (GROUPS - 2 - 2) // 2
            for k in range(2):
                slot(Tile(0, k))
            with eng.Fori(1, 1 + whole) as i:
                slot(Tile(i, 0))
                slot(Tile(i, 1))
            for k in range(2 + 2 * whole, GROUPS + 2):
                slot(Tile(0, k))

        def exists(g):
            return not isinstance(g.m, int) or 0 <= g.m < GROUPS

        def late(g, by=2):
            return not isinstance(g.m, int) or g.m >= by

        def place(g, r):
            return bass.ds((r * B + g.b) * T + g.n * G, G)

        block = ctx.enter_context(nc.Block())

        @block.sync
        def _(eng):
            for k in range(GROUPS):
                g = Tile(0, k)
                t0 = g.b * NT + g.n * GT
                src = io["x"][g.b, g.n * G:(g.n + 1) * G, :].rearrange("(t p) c -> p t c", p=P)
                eng.dma_start(X[:, t0:t0 + GT, :], src).then_inc(loaded_x, 16)
                if k == 0:
                    eng.dma_start(const[:, :], io["const"]).then_inc(loaded_const, 16)
                    eng.dma_start(w[:, :, :], io["w_qkv"]).then_inc(loaded_w, 16)
                eng.wait_ge(loaded_x, 16 * (k + 1))
                if k == 1:
                    eng.dma_start(cos[:, :], io["cos"]).then_inc(loaded_rope, 16)
                    eng.dma_start(sin[:, :], io["sin"]).then_inc(loaded_rope, 16)

        @block.gpsimd
        def _(eng):
            eng.memset(mhalf[:, :], -0.5).then_inc(set_up, 1)
            eng.memset(eps[:, :], LN_EPS).then_inc(set_up, 1)
            eng.wait_ge(set_up, 2)

            def rstds(g):
                eng.wait_ge(moments_ready, g.count(1, 1))
                if late(g):
                    eng.wait_ge(xn_ready, g.count(GT, -GT))
                eng.tensor_tensor(rstd[:, g.b, :], mv[:, g.b, :, 1], eps[:, :], ALU.add).then_inc(rstd_step, 1)
                eng.wait_ge(rstd_step, g.count(2, 1))
                eng.tensor_tensor(rstd[:, g.b, :], rstd[:, g.b, :], mhalf[:, :], ALU.pow).then_inc(rstd_step, 1)

            def low_x(g):
                eng.wait_ge(xt_copied, g.count(2, 2))
                if late(g):
                    eng.wait_ge(pr_full[3], g.count(1, -1))
                eng.tensor_tensor(x_lo[:, g.b, :], xT[:, g.b, :], x_hi[:, g.b, :].bitcast(F32), ALU.subtract).then_inc(xlo_ready, 1)

            def rotated(g, r):
                eng.wait_ge(pr_read[2 * r], g.count(1, 1))
                eng.wait_ge(pr_read[2 * r + 1], g.count(1, 1))
                eng.wait_ge(rot_hi[r], g.count(1, AHEAD - 1))
                eng.wait_ge(rot_lo[r], g.count(1, AHEAD - 1))
                eng.tensor_tensor(rot[:, g.b, r, :], by_cos[:, r, :], by_sin[:, r, :], ALU.add).then_inc(rot_ready[r], 1)

            def slot(g):
                if exists(g):
                    low_x(g)
                if exists(g.later(2)):
                    rstds(g.later(2))
                if exists(g.later(-1)):
                    rotated(g.later(-1), 0)
                    rotated(g.later(-1), 1)

            rstds(Tile(0, 0))
            rstds(Tile(0, 1))
            eng.wait_ge(w_hi_ready, 1)
            eng.tensor_tensor(w_lo[:, :, :], w[:, 0:4, :], w_hi[:, :, :].bitcast(F32), ALU.subtract).then_inc(w_lo_ready, 1)
            run_slots(eng, slot)

        @block.vector
        def _(eng):
            def moments(g):
                eng.wait_ge(loaded_x, g.count(16, 16))
                for j in range(GT):
                    mm = eng.bn_stats(stats[:, g.b, j, :], X[:, bass.ds(g.b * NT + g.n * GT + j, 1), :])
                mm.then_inc(stats_ready, 1)
                eng.wait_ge(stats_ready, g.count(1, 1))
                eng.memset(held[:, :], 0.0)
                for j in range(GT):
                    mm = eng.bn_aggr(mv[:, g.b, j, :], stats[:, g.b, j, :])
                mm.then_inc(moments_ready, 1)

            def shifts(g):
                eng.wait_ge(rstd_step, g.count(2, 2))
                eng.scalar_tensor_tensor(shift[:, g.b, :], mv[:, g.b, :, 0], -1.0, rstd[:, g.b, :], ALU.mult, ALU.mult).then_inc(shift_ready, 1)

            def products(g, r):
                if late(g, 1):
                    eng.wait_ge(rot_ready[r], g.count(1))
                for k, (prod, table) in enumerate(((by_cos, cos), (by_sin, sin))):
                    eng.wait_ge(pr_full[2 * r + k], g.count(1, 1))
                    eng.tensor_tensor(prod[:, r, :], pr_ps[2 * r + k][:, :], table[:, bass.ds(g.n * G, G)],
                                      ALU.mult).then_inc(pr_read[2 * r + k], 1)

            def low_part(g, r):
                eng.wait_ge(rot_hi[r], g.count(1, AHEAD + 1))
                eng.tensor_tensor(qk_lo[:, place(g, r)], rot[:, g.b, r, :], qk_hi[:, place(g, r)].bitcast(F32),
                                  ALU.subtract).then_inc(rot_lo[r], 1)

            def slot(g):
                if exists(g.later(1)):
                    shifts(g.later(1))
                if exists(g.later(-1)):
                    products(g.later(-1), 0)
                if exists(g.later(2)):
                    moments(g.later(2))
                if exists(g.later(-2)):
                    low_part(g.later(-2), 0)
                if exists(g.later(-1)):
                    products(g.later(-1), 1)
                if exists(g.later(-2)):
                    low_part(g.later(-2), 1)

            for r in range(2):
                eng.sem_inc(rot_lo[r], AHEAD)
            moments(Tile(0, 0))
            shifts(Tile(0, 0))
            moments(Tile(0, 1))
            eng.wait_ge(loaded_rope, 32)
            run_slots(eng, slot)

        @block.scalar
        def _(eng):
            def normalize(g):
                eng.wait_ge(shift_ready, g.count(1, 1))
                if late(g):
                    eng.wait_ge(xt_full, g.count(1, -1))
                for j in range(GT):
                    eng.activation(xn[:, g.b, j * P:(j + 1) * P], X[:, bass.ds(g.b * NT + g.n * GT + j, 1), :], ACT.Identity,
                                   bias=shift[:, g.b, j:j + 1], scale=rstd[:, g.b, j:j + 1]).then_inc(xn_ready, 1)

            def copy_x(g):
                eng.wait_ge(xt_full, g.count(1, 1))
                if late(g):
                    eng.wait_ge(v_full, g.count(1, -1))
                    eng.wait_ge(pr_full[3], g.count(1, -1))
                eng.activation(xT[:, g.b, :], xt_ps[g.b][:, :], ACT.Copy).then_inc(xt_copied, 1)
                eng.activation(x_hi[:, g.b, :], xt_ps[g.b][:, :], ACT.Copy).then_inc(xt_copied, 1)

            def copy_v(g):
                eng.wait_ge(v_full, g.count(1, 1))
                eng.activation(V[:, bass.ds(g.b * NT + g.n * GT, GT), :], v_ps[g.b][:, :].rearrange("p (t c) -> p t c", t=GT),
                               ACT.Copy).then_inc(v_read, 1)

            def high_part(g, r):
                eng.wait_ge(rot_ready[r], g.count(1, 1))
                eng.activation(qk_hi[:, place(g, r)], rot[:, g.b, r, :], ACT.Copy).then_inc(rot_hi[r], 1)

            def slot(g):
                if exists(g):
                    copy_x(g)
                if exists(g.later(1)):
                    normalize(g.later(1))
                if exists(g.later(-2)):
                    high_part(g.later(-2), 0)
                    high_part(g.later(-2), 1)
                if exists(g.later(-1)):
                    copy_v(g.later(-1))

            eng.sem_inc(v_read, AHEAD)
            for r in range(2):
                eng.sem_inc(rot_hi[r], AHEAD)
            normalize(Tile(0, 0))
            eng.wait_ge(loaded_w, 16)
            eng.activation(w_hi[:, :, :], w[:, 0:4, :], ACT.Copy).then_inc(w_hi_ready, 1)
            run_slots(eng, slot)

        @block.tensor
        def _(eng):
            eng.wait_ge(loaded_const, 16)
            eng.wait_ge(loaded_w, 16)

            def turn(g):
                if late(g):
                    eng.wait_ge(xt_copied, g.count(2, -2))
                for j in range(GT):
                    eng.wait_ge(xn_ready, g.count(GT, j + 1))
                    mm = eng.transpose(xt_ps[g.b][:, j * P:(j + 1) * P], xn[:, g.b, j * P:(j + 1) * P], ident)
                mm.then_inc(xt_full, 1)

            def values(g):
                eng.wait_ge(xt_copied, g.count(2, 2))
                eng.wait_ge(v_read, g.count(1, AHEAD - 1))
                for j in range(GT):
                    mm = eng.matmul(v_ps[g.b][:, j * P:(j + 1) * P], xT[:, g.b, j * P:(j + 1) * P], w[:, 4, :], start=True, stop=True)
                mm.then_inc(v_full, 1)

            def project(g, r):
                if not late(g, 1):
                    eng.wait_ge(w_lo_ready, 1)
                eng.wait_ge(xlo_ready, g.count(1, 1))
                for k in (2 * r, 2 * r + 1):
                    if late(g, 1):
                        eng.wait_ge(pr_read[k], g.count(1))
                    eng.matmul(pr_ps[k][:, :], w_hi[:, k, :], x_hi[:, g.b, :], start=True, stop=False)
                    eng.matmul(pr_ps[k][:, :], w_lo[:, k, :], x_hi[:, g.b, :], start=False, stop=False)
                    eng.matmul(pr_ps[k][:, :], w_hi[:, k, :], x_lo[:, g.b, :], start=False, stop=True).then_inc(pr_full[k], 1)

            def slot(g):
                if exists(g.later(-1)):
                    values(g.later(-1))
                if exists(g):
                    turn(g)
                if exists(g.later(-1)):
                    project(g.later(-1), 0)
                    project(g.later(-1), 1)

            run_slots(eng, slot)


def attention_phase(nc, io, X, const, qk_hi, qk_lo, V, w5_hi, w5_lo, ffn_weights, tables):
    ctx = ExitStack()
    with ctx:
        sb = lambda name, shape, dt=F32: ctx.enter_context(nc.sbuf_tensor("at_" + name, shape, dt))
        sem = lambda name: ctx.enter_context(nc.semaphore("at_" + name))
        ident = const[:, C_IDENT:C_IDENT + P]
        causal = const[:, C_NEG:C_NEG + P]
        wo = sb("wo", [P, P])
        PARTS = 4
        WIDTH = 5 * HD // (B * PARTS)
        w5_raw = sb("w5_raw", [P, 2, WIDTH])
        q_hi = sb("q_hi", [P, 2, P], F32R)
        q_lo = sb("q_lo", [P, 2, P], F32R)
        top = sb("top", [P, 2, GT])
        ntop = sb("ntop", [P, 2, 2])
        probs = sb("probs", [P, 2, T])
        probsT = sb("probsT", [P, 2, G])
        psums = sb("psums", [P, 2, GT])
        total = sb("total", [P, 2, 2])
        o_n = sb("o_n", [P, 2, P])
        oT = sb("oT", [P, 2, P])
        s_ps = ctx.enter_context(nc.psum_tensor("at_s_ps", [P, T], F32))
        t_ps = [ctx.enter_context(nc.psum_tensor(f"at_t_ps{k}", [P, G], F32)) for k in range(2)]
        o_ps = [ctx.enter_context(nc.psum_tensor(f"at_o_ps{k}", [P, G], F32)) for k in range(2)]

        wo_loaded = sem("wo_loaded")
        w5_loaded = bank_sems(sem, "w5_loaded", 2)
        w5_hi_done, w5_lo_done = sem("w5_hi_done"), sem("w5_lo_done")
        q_here = sem("q_here")
        s_full = bank_sems(sem, "s_full", NG)
        masked, top_ready, ntop_step = sem("masked"), sem("top_ready"), sem("ntop_step")
        exp_ready = sem("exp_ready")
        t_full = bank_sems(sem, "t_full", 2)
        t_read = bank_sems(sem, "t_read", 2)
        pv_used = sem("pv_used")
        o_full, total_step, o_ready = sem("o_full"), sem("total_step"), sem("o_ready")
        x_ready = sem("x_ready")

        block = ctx.enter_context(nc.Block())

        def blocks(n):
            return n // GT + 1

        def scored(n):
            return [n // GT] + list(range(n // GT))

        SMALL = 2 * GT

        def bank(n, j):
            return j + (NG // 2) * (n % 2) if n < SMALL else j

        def ahead(n):
            if n + 2 < SMALL:
                return n + 2
            return n + 1 if SMALL <= n + 1 < NT else None

        BLK = [sum(blocks(m) for m in range(n)) for n in range(NT + 1)]
        USES = [(bank(n, j), n, j) for n in range(NT) for j in range(blocks(n))]
        BANK = [[sum(1 for k_, m, _ in USES if k_ == k and m < n) for n in range(NT + 1)] for k in range(NG)]

        CREDIT = 1

        jobs = []
        for n in range(NT + 2):
            if n < NT:
                jobs += [("probs", n, j) for j in range(blocks(n))]
            if 1 <= n <= NT:
                jobs.append(("oT", n - 1, 0))
            if n >= 2:
                jobs.append(("wo", n - 2, 0))
        NJ = len(jobs)
        assert NJ % 2 == 0
        JOB = {job: k for k, job in enumerate(jobs)}

        def ring(b, job):
            k = JOB[job]
            return k % 2, b * (NJ // 2) + k // 2

        JOBS_OF = [(n, j) for n in range(NT) for j in range(blocks(n))]
        INNER = [sum(blocks(m) - 1 for m in range(n)) for n in range(NT + 1)]

        def copy_probs(eng, copy, b, n, j):
            k, before = ring(b, ("probs", n, j))
            eng.wait_ge(t_full[k], before + 1)
            width = min(G, (n + 1) * P - j * G)
            m = BLK[n] + j
            if m >= 2:
                pn, pj = JOBS_OF[m - 2]
                if pj == blocks(pn) - 1:
                    eng.wait_ge(o_full, b * NT + pn + 1 + CREDIT)
                else:
                    eng.wait_ge(pv_used, b * INNER[NT] + INNER[pn] + pj + 1)
            else:
                eng.wait_ge(o_full, b * NT + CREDIT)
            copy(probsT[:, m % 2, 0:width], t_ps[k][:, 0:width]).then_inc(t_read[k], 1)

        @block.sync
        def _(eng):
            eng.dma_start(wo[:, :], io["wo"]).then_inc(wo_loaded, 16)
            ffn_weights.sync(eng)
            tables.sync_rates(eng)
            for k in range(B * PARTS):
                if k >= 2:
                    eng.wait_ge(w5_lo_done, k - 1)
                eng.dma_start(w5_raw[:, k % 2, :], io["w5"][:, k * WIDTH:(k + 1) * WIDTH]).then_inc(w5_loaded[k % 2], 16)

        @block.gpsimd
        def _(eng):
            def bring_q(b, n):
                if n >= 2:
                    k = bank(n - 2, scored(n - 2)[-1])
                    eng.wait_ge(s_full[k], b * BANK[k][NT] + BANK[k][n - 2] + 1 + CREDIT)
                else:
                    k = bank(NT - 1, scored(NT - 1)[-1])
                    eng.wait_ge(s_full[k], b * BANK[k][NT] + CREDIT)
                at = b * T + n * P
                eng.tensor_copy(q_hi[:, n % 2, :], qk_hi[:, bass.ds(at, P)]).then_inc(q_here, 1)
                eng.tensor_copy(q_lo[:, n % 2, :], qk_lo[:, bass.ds(at, P)]).then_inc(q_here, 1)

            def split_w5(b, k):
                eng.wait_ge(w5_loaded[k % 2], 16 * (b * (PARTS // 2) + k // 2 + 1))
                part = bass.ds((b * PARTS + k) * WIDTH, WIDTH)
                eng.tensor_copy(w5_hi[:, part], w5_raw[:, k % 2, :]).then_inc(w5_hi_done, 1)
                eng.wait_ge(w5_hi_done, b * PARTS + k + 1)
                eng.tensor_tensor(w5_lo[:, part], w5_raw[:, k % 2, :], w5_hi[:, part].bitcast(F32),
                                  ALU.subtract).then_inc(w5_lo_done, 1)

            with eng.Fori(0, B) as b:
                for n in range(NT):
                    bring_q(b, n)
                    if n % 2 == 1 and n // 2 >= NT // 2 - PARTS:
                        split_w5(b, n // 2 - (NT // 2 - PARTS))
            ffn_weights.gpsimd(eng)
            tables.gpsimd_rates(eng)

        @block.tensor
        def _(eng):
            eng.sem_inc(o_full, CREDIT)
            for j in range(NG):
                eng.sem_inc(s_full[j], CREDIT)

            def scores(b, n):
                N = b * NT + n
                eng.wait_ge(q_here, 2 * N + 2)
                for j in scored(n):
                    k = bank(n, j)
                    used = max([BLK[m] + i + 1 for k_, m, i in USES if k_ == k and m < n], default=0)
                    eng.wait_ge(exp_ready, b * BLK[NT] + used + CREDIT)
                    width = G if j < n // GT else max(2 * P, (n % GT + 1) * P)
                    at = (B + b) * T + j * G
                    out = s_ps[:, k * G:k * G + width]
                    k_hi, k_lo = qk_hi[:, bass.ds(at, width)], qk_lo[:, bass.ds(at, width)]
                    eng.matmul(out, q_hi[:, n % 2, :], k_hi, start=True, stop=False)
                    eng.matmul(out, q_lo[:, n % 2, :], k_hi, start=False, stop=False)
                    eng.matmul(out, q_hi[:, n % 2, :], k_lo, start=False, stop=True).then_inc(s_full[k], 1)

            def wait_bank(b, job):
                k, before = ring(b, job)
                eng.wait_ge(t_read[k], before + CREDIT)
                return t_ps[k], t_full[k]

            def transposes(b, n, j):
                N = b * NT + n
                eng.wait_ge(exp_ready, b * BLK[NT] + BLK[n] + j + 1 + CREDIT)
                bank, full = wait_bank(b, ("probs", n, j))
                for t in range(min(GT, n + 1 - j * GT)):
                    mm = eng.transpose(bank[:, t * P:(t + 1) * P], probs[:, n % 2, (j * GT + t) * P:(j * GT + t + 1) * P], ident)
                mm.then_inc(full, 1)

            def values(b, n, j):
                N = b * NT + n
                k, before = ring(b, ("probs", n, j))
                eng.wait_ge(t_read[k], before + 1 + CREDIT)
                if j == 0:
                    if n >= 2:
                        eng.wait_ge(o_ready, N - 1 + CREDIT)
                    else:
                        eng.wait_ge(o_ready, b * NT + CREDIT)
                for t in range(min(GT, n + 1 - j * GT)):
                    kt = j * GT + t
                    mm = eng.matmul(o_ps[n % 2][:, 0:P], probsT[:, (BLK[n] + j) % 2, t * P:(t + 1) * P],
                                    V[:, bass.ds(b * NT + kt, 1), :], start=(kt == 0), stop=(kt == n))
                    if kt == n:
                        mm.then_inc(o_full, 1)
                    elif t == GT - 1:
                        mm.then_inc(pv_used, 1)

            def turn_o(b, n):
                eng.wait_ge(o_ready, b * NT + n + 1 + CREDIT)
                bank, full = wait_bank(b, ("oT", n, 0))
                eng.transpose(bank[:, 0:P], o_n[:, n % 2, :], ident).then_inc(full, 1)

            def project_o(b, n):
                k, before = ring(b, ("oT", n, 0))
                eng.wait_ge(t_read[k], before + 1 + CREDIT)
                bank, full = wait_bank(b, ("wo", n, 0))
                if n == 0:
                    eng.wait_ge(wo_loaded, 16)
                eng.matmul(bank[:, 0:P], oT[:, n % 2, :], wo[:, :], start=True, stop=True).then_inc(full, 1)

            with eng.Fori(0, B) as b:
                scores(b, 0)
                scores(b, 1)
                for n in range(NT + 2):
                    last = blocks(n) if n < NT else 0
                    for j in range(min(last, 2)):
                        transposes(b, n, j)
                    if ahead(n) is not None:
                        scores(b, ahead(n))
                    for j in range(last - 1):
                        values(b, n, j)
                        if j + 2 < last:
                            transposes(b, n, j + 2)
                    if 1 <= n <= NT:
                        turn_o(b, n - 1)
                    if n >= 2:
                        project_o(b, n - 2)
                    if n < NT:
                        values(b, n, last - 1)

        @block.vector
        def _(eng):
            def maxima(b, n):
                N = b * NT + n
                last = n // GT
                for j in scored(n):
                    k = bank(n, j)
                    eng.wait_ge(s_full[k], b * BANK[k][NT] + BANK[k][n] + 1 + CREDIT)
                    if j == last:
                        diag = s_ps[:, k * G + (n % GT) * P:k * G + (n % GT + 1) * P]
                        eng.tensor_tensor(diag, diag, causal, ALU.add).then_inc(masked, 1)
                        eng.wait_ge(masked, N + 1)
                    width = min(G, (n + 1) * P - j * G)
                    eng.tensor_reduce(top[:, n % 2, j:j + 1], s_ps[:, k * G:k * G + width], AX.X, ALU.max).then_inc(top_ready, 1)
                eng.wait_ge(top_ready, b * BLK[NT] + BLK[n + 1])
                eng.tensor_reduce(ntop[:, n % 2, 0:1], top[:, n % 2, 0:blocks(n)], AX.X, ALU.max, negate=True).then_inc(ntop_step, 1)
                eng.wait_ge(ntop_step, 2 * N + 1)
                eng.tensor_scalar(ntop[:, n % 2, 1:2], ntop[:, n % 2, 0:1], 1.0 / C, None, ALU.mult).then_inc(ntop_step, 1)

            def sum_rows(b, n):
                N = b * NT + n
                eng.wait_ge(exp_ready, b * BLK[NT] + BLK[n + 1] + CREDIT)
                eng.tensor_reduce(total[:, n % 2, 0:1], psums[:, n % 2, 0:blocks(n)], AX.X, ALU.add).then_inc(total_step, 1)
                eng.wait_ge(total_step, 2 * N + 1)
                eng.reciprocal(total[:, n % 2, 1:2], total[:, n % 2, 0:1]).then_inc(total_step, 1)

            def copy_oT(b, n):
                k, before = ring(b, ("oT", n, 0))
                eng.wait_ge(t_full[k], before + 1)
                eng.tensor_copy(oT[:, n % 2, :], t_ps[k][:, 0:P]).then_inc(t_read[k], 1)

            def residual(b, n):
                k, before = ring(b, ("wo", n, 0))
                eng.wait_ge(t_full[k], before + 1)
                xt = X[:, bass.ds(b * NT + n, 1), :]
                eng.tensor_tensor(xt, t_ps[k][:, 0:P].rearrange("p (t c) -> p t c", t=1), xt, ALU.add).then_inc(t_read[k], 1)

            for k in range(2):
                eng.sem_inc(t_read[k], CREDIT)
            ffn_weights.vector(eng)
            with eng.Fori(0, B) as b:
                maxima(b, 0)
                maxima(b, 1)
                for n in range(NT + 2):
                    last = blocks(n) if n < NT else 0
                    if ahead(n) == n + 2:
                        sum_rows(b, n)
                    if ahead(n) is not None:
                        maxima(b, ahead(n))
                    if n < NT and ahead(n) != n + 2:
                        sum_rows(b, n)
                    for j in range(2, last):
                        copy_probs(eng, eng.tensor_copy, b, n, j)
                    if 1 <= n <= NT:
                        copy_oT(b, n - 1)
                    if n >= 2:
                        residual(b, n - 2)

        @block.scalar
        def _(eng):
            def exponentials(b, n):
                N = b * NT + n
                eng.wait_ge(ntop_step, 2 * N + 2)
                if n >= 2:
                    k, before = ring(b, ("probs", n - 2, blocks(n - 2) - 1))
                    eng.wait_ge(t_full[k], before + 1)
                else:
                    eng.wait_ge(o_full, b * NT + CREDIT)
                for j in range(blocks(n)):
                    k, width = bank(n, j), min(G, (n + 1) * P - j * G)
                    eng.activation(probs[:, n % 2, j * G:j * G + width], s_ps[:, k * G:k * G + width], ACT.Exp, bias=ntop[:, n % 2, 1:2],
                                   scale=1.0 / C, accum_out=psums[:, n % 2, j:j + 1]).then_inc(exp_ready, 1)

            def scale_o(b, n):
                N = b * NT + n
                eng.wait_ge(o_full, N + 1 + CREDIT)
                eng.wait_ge(total_step, 2 * N + 2)
                eng.activation(o_n[:, n % 2, :], o_ps[n % 2][:, 0:P], ACT.Copy, scale=total[:, n % 2, 1:2]).then_inc(o_ready, 1)

            eng.sem_inc(exp_ready, CREDIT)
            eng.sem_inc(o_ready, CREDIT)
            ffn_weights.scalar(eng)
            with eng.Fori(0, B) as b:
                exponentials(b, 0)
                for n in range(NT):
                    for j in range(min(blocks(n), 2)):
                        copy_probs(eng, lambda o, i: eng.activation(o, i, ACT.Copy), b, n, j)
                    if n + 1 < NT:
                        exponentials(b, n + 1)
                    scale_o(b, n)
            tables.scalar_rates(eng)


class FfnWeights:

    def __init__(self, io, sb, sem):
        self.io = io
        self.w = sb("fw_w", [P, 3, P])
        self.mu = sb("fw_mu", [P, 2])
        self.rest = sb("fw_rest", [P, 2])
        self.wr = sb("fw_wr", [P, 2, P])
        self.wk = sb("fw_wk", [P, 2, P])
        self.wk_hi = sb("fw_wk_hi", [P, 2, P], F32R)
        self.wk_lo = sb("fw_wk_lo", [P, 2, P], F32R)
        self.wv = sb("fw_wv", [P, P])
        self.loaded, self.rest_ready, self.scaled, self.wk_hi_ready, self.wk_lo_ready = (
            sem("fw_" + n) for n in ("loaded", "rest_ready", "scaled", "wk_hi_ready", "wk_lo_ready"))

    def sync(self, eng):
        eng.dma_start(self.w[:, :, :], self.io["w_ffn"]).then_inc(self.loaded, 16)
        eng.dma_start(self.mu[:, :], self.io["mu"]).then_inc(self.loaded, 16)

    def vector(self, eng):
        w, mu, rest, wk, wr = self.w, self.mu, self.rest, self.wk, self.wr
        eng.wait_ge(self.loaded, 32)
        eng.tensor_scalar(rest[:, :], mu[:, :], -1.0, 1.0, ALU.mult, ALU.add).then_inc(self.rest_ready, 1)
        eng.tensor_scalar(wk[:, 0, :], w[:, 1, :], mu[:, 1:2], None, ALU.mult).then_inc(self.scaled, 1)
        eng.wait_ge(self.rest_ready, 1)
        eng.tensor_scalar(wk[:, 1, :], w[:, 1, :], rest[:, 1:2], None, ALU.mult).then_inc(self.scaled, 1)
        eng.tensor_scalar(wr[:, 0, :], w[:, 0, :], mu[:, 0:1], None, ALU.mult).then_inc(self.scaled, 1)
        eng.tensor_scalar(wr[:, 1, :], w[:, 0, :], rest[:, 0:1], None, ALU.mult).then_inc(self.scaled, 1)
        eng.tensor_scalar(self.wv[:, :], w[:, 2, :], 0.5, None, ALU.mult).then_inc(self.scaled, 1)

    def scalar(self, eng):
        eng.wait_ge(self.scaled, 2)
        eng.activation(self.wk_hi[:, :, :], self.wk[:, :, :], ACT.Copy).then_inc(self.wk_hi_ready, 1)

    def gpsimd(self, eng):
        eng.wait_ge(self.wk_hi_ready, 1)
        eng.tensor_tensor(self.wk_lo[:, :, :], self.wk[:, :, :], self.wk_hi[:, :, :].bitcast(F32),
                          ALU.subtract).then_inc(self.wk_lo_ready, 1)


def ffn_phase(nc, X, const, weights, norm, name, out=None, tables=None, next_norm=None):
    normed = 2 if out is not None else 0
    wr, wk_hi, wk_lo, wv = weights.wr, weights.wk_hi, weights.wk_lo, weights.wv
    ctx = ExitStack()
    with ctx:
        sb = lambda what, shape, dt=F32: ctx.enter_context(nc.sbuf_tensor(name + what, shape, dt))
        sem = lambda what: ctx.enter_context(nc.semaphore(name + what))
        psum = lambda what: ctx.enter_context(nc.psum_tensor(name + what, [P, G], F32))
        ident = const[:, C_IDENT:C_IDENT + P]
        xn = norm.xn
        xT = sb("xT", [P, 2, 1 + G])
        x_hi = sb("x_hi", [P, 2, 1 + G], F32R)
        x_lo = sb("x_lo", [P, 2, 1 + G], F32R)
        k_pos = sb("k_pos", [P, 2, G])
        k_act = sb("k_act", [P, 2, G])
        r_tanh = sb("r_tanh", [P, 2, G])
        gated = sb("gated", [P, 2, G])
        xt_ps = [psum(f"xt_ps{b}") for b in range(2)]
        k_ps = [psum(f"k_ps{b}") for b in range(2)]
        r_ps = [psum(f"r_ps{b}") for b in range(2)]
        o_ps = [psum(f"o_ps{b}") for b in range(2)]

        (set_up, xt_full, carried, xt_ready, hi_ready, lo_ready, k_full, k_pos_ready, k_act_ready, r_full, r_ready, o_full,
         gated_ready, x_ready, stored) = (sem(n) for n in (
             "set_up", "xt_full", "carried", "xt_ready", "hi_ready", "lo_ready", "k_full", "k_pos_ready", "k_act_ready",
             "r_full", "r_ready", "o_full", "gated_ready", "x_ready", "stored"))
        GROUPS = B * NG

        def run_slots(eng, slot):
            whole = (GROUPS - 2 - 2) // 2
            for k in range(2):
                slot(Tile(0, k))
            with eng.Fori(1, 1 + whole) as i:
                slot(Tile(i, 0))
                slot(Tile(i, 1))
            for k in range(2 + 2 * whole, GROUPS + 2):
                slot(Tile(0, k))

        AHEAD = 2

        def exists(g):
            return not isinstance(g.m, int) or 0 <= g.m < GROUPS

        def late(g):
            return not isinstance(g.m, int) or g.m >= 2

        def has_been_normed(g):
            return isinstance(g.m, int) and g.m < normed

        def tokens(g):
            return X[:, bass.ds(g.b * NT + g.n * GT, GT), :]

        block = ctx.enter_context(nc.Block())

        @block.sync
        def _(eng):
            if tables is not None:
                tables.sync(eng)
            if out is not None:
                for k in range(GROUPS):
                    g = Tile(0, k)
                    eng.wait_ge(x_ready, k + 1)
                    eng.dma_start(out[g.b, g.n * G:(g.n + 1) * G, :].rearrange("(t p) c -> p t c", p=P),
                                  X[:, g.b * NT + g.n * GT:g.b * NT + (g.n + 1) * GT, :]).then_inc(stored, 16)
                eng.wait_ge(stored, 16 * GROUPS)

        @block.gpsimd
        def _(eng):
            if not normed:
                norm.prepare(eng)
            eng.memset(xT[:, :, 0:1], 0.0).then_inc(set_up, 1)

            def low_part(g):
                eng.wait_ge(hi_ready, g.count(1, 1))
                eng.tensor_tensor(x_lo[:, g.b, :], xT[:, g.b, :], x_hi[:, g.b, :].bitcast(F32), ALU.subtract).then_inc(lo_ready, 1)

            def slot(g):
                if exists(g):
                    low_part(g)
                if exists(g.later(2)):
                    norm.inverse_roots(eng, g.later(2))
                if tables is not None and g.off == GROUPS - 1:
                    tables.gpsimd_strict(eng)
                if next_norm is not None and g.off == GROUPS:
                    next_norm.first_gpsimd(eng)

            if not normed:
                norm.inverse_roots(eng, Tile(0, 0))
                norm.inverse_roots(eng, Tile(0, 1))
            run_slots(eng, slot)

        @block.vector
        def _(eng):
            eng.sem_inc(gated_ready, AHEAD)

            def normalize(g):
                if late(g):
                    eng.wait_ge(xt_full, g.count(1, -1))
                norm.normalize(eng, g)

            def output(g):
                eng.wait_ge(r_ready, g.count(1, AHEAD + 1))
                eng.wait_ge(o_full, g.count(1, AHEAD + 1))
                eng.scalar_tensor_tensor(gated[:, g.b, :], r_tanh[:, g.b, :], 1.0, o_ps[g.b][:, :], ALU.add, ALU.mult).then_inc(gated_ready, 1)
                eng.wait_ge(gated_ready, g.count(1, AHEAD + 1))
                eng.tensor_tensor(tokens(g), gated[:, g.b, :].rearrange("p (t c) -> p t c", t=GT), tokens(g), ALU.add).then_inc(x_ready, 1)

            def slot(g):
                if tables is not None and g.off == GROUPS:
                    tables.vector(eng)
                if next_norm is not None and g.off == GROUPS:
                    next_norm.first_vector(eng)
                if exists(g.later(1)) and not has_been_normed(g.later(1)):
                    normalize(g.later(1))
                if exists(g.later(2)):
                    norm.moments(eng, g.later(2))
                if exists(g.later(-2)):
                    output(g.later(-2))

            if not normed:
                norm.moments(eng, Tile(0, 0))
                norm.moments(eng, Tile(0, 1))
                normalize(Tile(0, 0))
            run_slots(eng, slot)

        @block.scalar
        def _(eng):
            eng.sem_inc(r_ready, AHEAD)
            eng.sem_inc(k_pos_ready, AHEAD)
            eng.wait_ge(set_up, 1)
            def copy_x(g):
                eng.wait_ge(xt_full, g.count(1, 1))
                if late(g):
                    eng.wait_ge(k_full, g.count(1, -1))
                    eng.wait_ge(r_full, g.count(1, -1))
                    eng.activation(xT[:, g.b, 0:1], xT[:, g.b, G:G + 1], ACT.Copy).then_inc(carried, 1)
                    eng.wait_ge(carried, g.count(1, -1))
                eng.activation(xT[:, g.b, 1:1 + G], xt_ps[g.b][:, :], ACT.Copy).then_inc(xt_ready, 1)
                eng.wait_ge(xt_ready, g.count(1, 1))
                eng.activation(x_hi[:, g.b, :], xT[:, g.b, :], ACT.Copy).then_inc(hi_ready, 1)

            def tanh(g):
                eng.wait_ge(r_full, g.count(1, 1))
                eng.wait_ge(gated_ready, g.count(1, AHEAD - 1))
                eng.activation(r_tanh[:, g.b, :], r_ps[g.b][:, :], ACT.Tanh, scale=0.5).then_inc(r_ready, 1)

            def square(g):
                eng.wait_ge(k_full, g.count(1, 1))
                eng.activation(k_pos[:, g.b, :], k_ps[g.b][:, :], ACT.Relu).then_inc(k_pos_ready, 1)
                eng.wait_ge(k_pos_ready, g.count(1, AHEAD + 1))
                eng.wait_ge(o_full, g.count(1, AHEAD - 1))
                eng.activation(k_act[:, g.b, :], k_pos[:, g.b, :], ACT.Square).then_inc(k_act_ready, 1)

            def slot(g):
                if exists(g):
                    copy_x(g)
                if exists(g.later(-1)):
                    tanh(g.later(-1))
                    square(g.later(-1))
                if tables is not None and isinstance(g.m, int):
                    if g.m < 2:
                        tables.scalar_heads(eng, range(g.m * H // 2, (g.m + 1) * H // 2))
                    elif GROUPS - 2 <= g.m < GROUPS:
                        half = g.m - (GROUPS - 2)
                        tables.scalar_pairs(eng, range(half * NP // 2, (half + 1) * NP // 2))
                    elif g.m == GROUPS:
                        tables.scalar_rest(eng)

            run_slots(eng, slot)

        @block.tensor
        def _(eng):
            eng.sem_inc(o_full, AHEAD)

            def turn(g):
                if late(g):
                    eng.wait_ge(xt_ready, g.count(1, -1))
                for j in range(GT):
                    eng.wait_ge(norm.ready, g.count(GT, j + 1))
                    mm = eng.transpose(xt_ps[g.b][:, j * P:(j + 1) * P], xn[:, g.b, j * P:(j + 1) * P], ident)
                mm.then_inc(xt_full, 1)

            def keys(g):
                eng.wait_ge(lo_ready, g.count(1, 1))
                eng.wait_ge(k_pos_ready, g.count(1, AHEAD - 1))
                for shift in range(2):
                    hi, lo = x_hi[:, g.b, 1 - shift:1 - shift + G], x_lo[:, g.b, 1 - shift:1 - shift + G]
                    eng.matmul(k_ps[g.b][:, :], wk_hi[:, shift, :], hi, start=(shift == 0), stop=False)
                    eng.matmul(k_ps[g.b][:, :], wk_lo[:, shift, :], hi, start=False, stop=False)
                    mm = eng.matmul(k_ps[g.b][:, :], wk_hi[:, shift, :], lo, start=False, stop=(shift == 1))
                mm.then_inc(k_full, 1)

            def receptance(g):
                eng.wait_ge(xt_ready, g.count(1, 1))
                eng.wait_ge(r_ready, g.count(1, AHEAD - 1))
                for j in range(GT):
                    ps = r_ps[g.b][:, j * P:(j + 1) * P]
                    eng.matmul(ps, xT[:, g.b, 1 + j * P:1 + (j + 1) * P], wr[:, 0, :], start=True, stop=False)
                    mm = eng.matmul(ps, xT[:, g.b, j * P:(j + 1) * P], wr[:, 1, :], start=False, stop=True)
                mm.then_inc(r_full, 1)

            def values(g):
                eng.wait_ge(k_act_ready, g.count(1, 1))
                eng.wait_ge(gated_ready, g.count(1, AHEAD - 1))
                for j in range(GT):
                    mm = eng.matmul(o_ps[g.b][:, j * P:(j + 1) * P], k_act[:, g.b, j * P:(j + 1) * P], wv[:, :], start=True, stop=True)
                mm.then_inc(o_full, 1)

            def slot(g):
                if exists(g):
                    turn(g)
                if exists(g.later(-1)):
                    receptance(g.later(-1))
                if exists(g.later(-2)):
                    values(g.later(-2))
                if exists(g.later(-1)):
                    keys(g.later(-1))

            run_slots(eng, slot)


PROJ = [("q", 0), ("f", 0), ("k", 0), ("f", 1), ("q", 1), ("g", 0), ("k", 1), ("g", 1), ("v", 0), ("v", 1)]
TURN = {job: k for k, job in enumerate(
    [("qT", 0), ("kT", 0), ("qT", 1), ("kT", 1), ("qk", 0), ("qk", 1), ("qk", 2), ("qk", 3), ("oT", 0), ("oT", 1)])}
NTURN = len(TURN)


class LinearTables:

    def __init__(self, io, const, sb, sem):
        self.io, self.const = io, const
        self.rate = sb("lt_rate", [P, H])
        self.rate_col = sb("lt_rate_col", [P, NP])
        self.rates_loaded, self.loaded, self.rate_step, self.rate_ready, self.decay_exp, self.decay_ready, self.w_ready = (
            sem("lt_" + n) for n in ("rates_loaded", "loaded", "rate_step", "rate_ready", "decay_exp", "decay_ready", "w_ready"))

    def make_room(self, sb):
        self.w_beta = sb("lt_w_beta", [P, H])
        self.w_out = sb("lt_w_out", [P, NP, P])
        self.norm_w = sb("lt_norm_w", [P, 1])
        self.bias_f = sb("lt_bias_f", [P, HD])
        self.bias_g = sb("lt_bias_g", [P, HD])
        self.decay = sb("lt_decay", [P, H, P])
        self.decay_q = sb("lt_decay_q", [P, NP, P])
        self.decay_k = sb("lt_decay_k", [P, H])
        self.decay_s = sb("lt_decay_s", [P, NP])

    def sync_rates(self, eng):
        src = self.io["a_log"].rearrange("(o n) -> o n", o=1).broadcast_to([P, H])
        eng.dma_start(self.rate[:, :], src).then_inc(self.rates_loaded, 16)
        for half in range(2):
            src = self.io["a_log_pairs"][half:half + 1, :].broadcast_to([D, NP])
            eng.dma_start(self.rate_col[half * D:(half + 1) * D, :], src).then_inc(self.rates_loaded, 16)

    def sync(self, eng):
        io, loaded = self.io, self.loaded
        for row, where in (("dt_bias", self.bias_f), ("bg", self.bias_g)):
            src = io[row].rearrange("(o n) -> o n", o=1).broadcast_to([P, HD])
            eng.dma_start(where[:, :], src).then_inc(loaded, 16)
        for half in range(2):
            src = io["norm_w"].rearrange("(d o) -> d o", o=1)
            eng.dma_start(self.norm_w[half * D:(half + 1) * D, :], src).then_inc(loaded, 16)
        eng.dma_start(self.w_beta[:, :], io["wb"]).then_inc(loaded, 16)
        eng.dma_start(self.w_out[:, :, :], io["w_out"].rearrange("(r p) m -> p r m", p=P)).then_inc(loaded, 16)

    def scalar_rates(self, eng):
        eng.wait_ge(self.rates_loaded, 16 * 3)
        for r in (self.rate, self.rate_col):
            eng.activation(r[:, :], r[:, :], ACT.Exp).then_inc(self.rate_step, 1)

    def gpsimd_rates(self, eng):
        eng.wait_ge(self.rate_step, 2)
        for r in (self.rate, self.rate_col):
            eng.tensor_scalar(r[:, :], r[:, :], 1e30, -1.0, ALU.min, ALU.mult).then_inc(self.rate_ready, 1)

    def scalar_heads(self, eng, heads):
        for h in heads:
            eng.activation(self.decay[:, h, :], self.const[:, C_LAG:C_LAG + P], ACT.Exp,
                           scale=self.rate[:, h:h + 1]).then_inc(self.decay_exp, 1)

    def scalar_pairs(self, eng, pairs):
        for r in pairs:
            eng.activation(self.decay_q[:, r, :], self.const[:, C_TPOS:C_TPOS + P], ACT.Exp,
                           scale=self.rate_col[:, r:r + 1]).then_inc(self.decay_exp, 1)

    def scalar_rest(self, eng):
        eng.activation(self.decay_k[:, :], self.rate[:, :], ACT.Exp, scale=self.const[:, C_LEFT:C_LEFT + 1]).then_inc(self.decay_exp, 1)
        eng.activation(self.decay_s[:, :], self.rate_col[:, :], ACT.Exp, scale=float(P)).then_inc(self.decay_exp, 1)

    def gpsimd_strict(self, eng):
        eng.wait_ge(self.decay_exp, H)
        strict = self.const[:, C_STRICT:C_STRICT + P].unsqueeze(1).broadcast_to([P, H, P])
        eng.tensor_tensor(self.decay[:, :, :], self.decay[:, :, :], strict, ALU.mult).then_inc(self.decay_ready, 1)

    def vector(self, eng):
        eng.wait_ge(self.loaded, 16 * 6)
        eng.tensor_scalar(self.w_out[:, :, :], self.w_out[:, :, :], self.norm_w[:, 0:1], 4.0, ALU.mult, ALU.mult).then_inc(self.w_ready, 1)
        eng.tensor_scalar(self.bias_f[:, :], self.bias_f[:, :], -1.0, None, ALU.mult).then_inc(self.w_ready, 1)


def linear_phase(nc, X, const, w5_hi, w5_lo, tables, norm, next_norm):
    ctx = ExitStack()
    with ctx:
        sb = lambda what, shape, dt=F32: ctx.enter_context(nc.sbuf_tensor("la_" + what, shape, dt))
        sem = lambda what: ctx.enter_context(nc.semaphore("la_" + what))
        psum = lambda what: ctx.enter_context(nc.psum_tensor("la_" + what, [P, G], F32))
        w_beta, w_out, bias_f, bias_g = tables.w_beta, tables.w_out, tables.bias_f, tables.bias_g
        decay, decay_q, decay_k, decay_s = tables.decay, tables.decay_q, tables.decay_k, tables.decay_s
        ident = const[:, C_IDENT:C_IDENT + P]

        mhalf = sb("mhalf", [P, H])
        ones = sb("ones", [P, H])
        state = sb("state", [P, 2, NP, P])
        faded = sb("faded", [P, NP, P])

        xn = norm.xn
        xT = sb("xT", [P, 2, P])
        x_hi = sb("x_hi", [P, 2, P], F32R)
        x_lo = sb("x_lo", [P, 2, P], F32R)
        f = sb("f", [P, 2, HD])
        gate = sb("gate", [P, 2, HD])
        q = sb("q", [P, 2, HD])
        k = sb("k", [P, 2, HD])
        v = sb("v", [P, 2, HD])
        sq_q = sb("sq_q", [P, HD])
        sq_k = sb("sq_k", [P, HD])
        sq_u = next_norm.xn[:, :, :].rearrange("p b g -> p (b g)")
        ssq = sb("ssq", [P, 2, H])
        ssk = sb("ssk", [P, 2, H])
        beta = sb("beta", [P, 2, H])
        coef = sb("coef", [P, 2, H])
        vb = sb("vb", [P, 2, HD])
        kd = sb("kd", [P, 2, HD])
        qT = sb("qT", [P, NP, P])
        kT = sb("kT", [P, NP, P])
        qdT = sb("qdT", [P, NP, P])
        pT = sb("pT", [P, H, P])
        u = sb("u", [P, HD])
        ssu = sb("ssu", [P, H])
        scale = sb("scale", [P, 2, H])
        og = sb("og", [P, HD])
        oT = sb("oT", [P, NP, P])

        pr_ps = [psum(f"pr_ps{r}") for r in range(2)]
        t_ps = [psum(f"t_ps{r}") for r in range(2)]
        o_ps = [psum(f"o_ps{r}") for r in range(2)]
        m_ps = psum("m_ps")
        s_ps = psum("s_ps")

        names = ("set_up x_turned "
                 "xt_ready xlo_ready beta_full beta_ready fb_ready gb_ready f_ready g_ready "
                 "qsq_ready ksq_ready usq_ready qsq_summed ksq_summed ssq_ready ssk_ready ssu_ready coef_step vb_ready kd_ready faded_ready qd_ready "
                 "o_full u_ready state_full state_ready ug_ready scale_step og_ready y_full x_ready").split()
        s = {n: sem(n) for n in names}
        pr_full, pr_read = bank_sems(sem, "pr_full", 2), bank_sems(sem, "pr_read", 2)
        t_full, t_read = bank_sems(sem, "t_full", 2), bank_sems(sem, "t_read", 2)

        def by_head(ap):
            return ap.rearrange("p (h d) -> p h d", d=D)

        def over_d(ap):
            return ap.unsqueeze(2).broadcast_to([P, H, D])

        def proj(tl, job):
            k_ = PROJ.index(job)
            return k_ % 2, tl.count(5, k_ // 2)

        def projected(eng, tl, kind, half):
            bank, before = proj(tl, (kind, half))
            eng.wait_ge(pr_read[bank], before + 1)

        def turn(tl, job):
            step = tl.later(1) if job[0] == "oT" else tl
            at = NTURN * step.off + TURN[job]
            absent = 2
            if isinstance(step.i, int) and step.m == 0 and TURN[job] < TURN["oT", 0]:
                absent = 0
            if isinstance(step.i, int) and step.m == B * NT:
                absent += TURN["oT", 0]
            return at % 2, NTURN * step.i + at // 2 - absent // 2

        LAST = B * NT - 1

        STATE_START = 2

        def exists(tl):
            return not isinstance(tl.m, int) or 0 <= tl.m <= LAST

        def carries(tl):
            return exists(tl.later(2))

        def run_steps(eng, step):
            step(Tile(0, 0))
            loops = (LAST - 3) // 2
            with eng.Fori(0, loops) as i:
                step(Tile(i, 1))
                step(Tile(i, 2))
            for m in range(2 * loops + 1, LAST + 1):
                step(Tile(0, m))

        block = ctx.enter_context(nc.Block())

        @block.tensor
        def _(eng):
            def turn_x(tl):
                if not isinstance(tl.m, int) or tl.m >= 3:
                    eng.wait_ge(s["x_ready"], tl.count(1, -2))
                elif tl.m == 2:
                    eng.wait_ge(s["beta_ready"], 1)
                elif tl.m == 1:
                    eng.wait_ge(s["xt_ready"], 2)
                eng.wait_ge(norm.ready, tl.count(1, 1))
                eng.transpose(m_ps[:, 0:P], xn[:, tl.b, :], ident).then_inc(s["x_turned"], 1)

            def project(tl, job):
                bank, before = proj(tl, job)
                if job == PROJ[0]:
                    eng.wait_ge(s["xlo_ready"], tl.count(1, 1))
                    eng.wait_ge(s["xt_ready"], tl.count(2, 2))
                eng.wait_ge(pr_read[bank], before)
                col = PROJ.index(job) * G
                hi, lo = w5_hi[:, col:col + G], w5_lo[:, col:col + G]
                eng.matmul(pr_ps[bank][:, :], x_hi[:, tl.b, :], hi, start=True, stop=False)
                eng.matmul(pr_ps[bank][:, :], x_hi[:, tl.b, :], lo, start=False, stop=False)
                eng.matmul(pr_ps[bank][:, :], x_lo[:, tl.b, :], hi, start=False, stop=True).then_inc(pr_full[bank], 1)

            def betas(tl):
                if exists(tl.later(1)):
                    eng.wait_ge(s["xt_ready"], tl.count(2, 4))
                else:
                    eng.wait_ge(s["x_ready"], tl.count(1, -1))
                eng.matmul(m_ps[:, 0:H], xT[:, tl.b, :], w_beta[:, :], start=True, stop=True).then_inc(s["beta_full"], 1)

            def turning(tl, job):
                bank, before = turn(tl, job)
                eng.wait_ge(t_read[bank], before)
                return t_ps[bank], t_full[bank]

            def turned(tl, job):
                bank, before = turn(tl, job)
                eng.wait_ge(t_read[bank], before + 1)

            def turn_qk(tl, job):
                kind, half = job
                projected(eng, tl, kind[0], half)
                ps, full = turning(tl, job)
                src = (q if kind == "qT" else k)[:, tl.b, :]
                for r in range(4):
                    pair = 4 * half + r
                    mm = eng.transpose(ps[:, r * P:(r + 1) * P], src[:, pair * P:(pair + 1) * P], ident)
                mm.then_inc(full, 1)

            def scores(tl, n_):
                banks = [turning(tl, ("qk", 2 * n_ + odd)) for odd in range(2)]
                for r in range(4):
                    for odd, (ps, full) in enumerate(banks):
                        rows, pair = slice(odd * D, (odd + 1) * D), 4 * n_ + r
                        mm = eng.matmul(ps[:, r * P:(r + 1) * P], kT[rows, pair, :], qT[rows, pair, :], start=True, stop=True)
                        if r == 3:
                            mm.then_inc(full, 1)

            def update(tl):
                eng.wait_ge(s["kd_ready"], tl.count(1, 1))
                eng.wait_ge(s["vb_ready"], tl.count(1, 1))
                eng.wait_ge(s["state_ready"], tl.count(2, STATE_START))
                for h in range(H):
                    rows, cols = slice((h % 2) * D, (h % 2 + 1) * D), slice(h * D, (h + 1) * D)
                    mm = eng.matmul(s_ps[rows, (h // 2) * D:(h // 2 + 1) * D], kd[:, tl.b, cols], vb[:, tl.b, cols], start=True, stop=True)
                mm.then_inc(s["state_full"], 1)

            def attend(tl):
                eng.wait_ge(s["qd_ready"], tl.count(1, 1))
                eng.wait_ge(s["vb_ready"], tl.count(1, 1))
                eng.wait_ge(s["state_ready"], tl.count(2, STATE_START - 2))
                for half in range(2):
                    if exists(tl.later(-1)):
                        eng.wait_ge(s["u_ready"], tl.count(2, half - 1))
                    turned(tl, ("qk", 2 * half))
                    turned(tl, ("qk", 2 * half + 1))
                    for pair in range(4 * half, 4 * half + 4):
                        at = (pair % 4) * P
                        eng.matmul(o_ps[half][:, at:at + P], qdT[:, pair, :], state[:, tl.b, pair, :], start=True, stop=False,
                                   skip_group_check=True)
                        for h in (2 * pair, 2 * pair + 1):
                            at = (h % 8) * D
                            mm = eng.matmul(o_ps[half][:, at:at + D], pT[:, h, :], vb[:, tl.b, h * D:(h + 1) * D], start=False, stop=True,
                                            skip_group_check=True)
                    mm.then_inc(s["o_full"], 1)

            def turn_o(tl, half):
                if half == 0:
                    eng.wait_ge(s["og_ready"], tl.count(1, 1))
                ps, full = turning(tl, ("oT", half))
                for r in range(4):
                    pair = 4 * half + r
                    mm = eng.transpose(ps[:, r * P:(r + 1) * P], og[:, pair * P:(pair + 1) * P], ident)
                mm.then_inc(full, 1)

            def project_out(tl):
                turned(tl, ("oT", 0))
                turned(tl, ("oT", 1))
                eng.wait_ge(s["x_ready"], tl.count(1, 1))
                eng.wait_ge(s["beta_ready"], min(tl.m + 3, LAST + 1) if isinstance(tl.m, int) else tl.count(1, 3))
                for pair in range(NP):
                    mm = eng.matmul(m_ps[:, 0:P], oT[:, pair, :], w_out[:, pair, :], start=(pair == 0), stop=(pair == NP - 1))
                mm.then_inc(s["y_full"], 1)

            def step(tl):
                nxt, prv = tl.later(1), tl.later(-1)
                own = [lambda j=j: turn_qk(tl, j) for j in (("qT", 0), ("kT", 0), ("qT", 1), ("kT", 1))]
                own += [lambda: None, lambda: scores(tl, 0), lambda: turn_x(tl.later(2)) if exists(tl.later(2)) else None,
                        lambda: scores(tl, 1), lambda: betas(nxt) if exists(nxt) else None]
                for n_, job in enumerate(PROJ):
                    if exists(nxt):
                        project(nxt, job)
                    if n_ < len(own):
                        own[n_]()
                if exists(prv):
                    turn_o(prv, 0)
                    turn_o(prv, 1)
                attend(tl)
                if exists(prv):
                    project_out(prv)
                if carries(tl):
                    update(tl)

            turn_x(Tile(0, 0))
            turn_x(Tile(0, 1))
            for job in PROJ:
                project(Tile(0, 0), job)
            betas(Tile(0, 0))
            run_steps(eng, step)
            turn_o(Tile(0, LAST), 0)
            turn_o(Tile(0, LAST), 1)
            project_out(Tile(0, LAST))

        @block.vector
        def _(eng):
            def add_bias(tl, job):
                bank, before = proj(tl, job)
                eng.wait_ge(pr_full[bank], before + 1)
                kind, half = job
                where, bias, ready = (f, bias_f, s["fb_ready"]) if kind == "f" else (gate, bias_g, s["gb_ready"])
                part = slice(half * G, (half + 1) * G)
                if half == 0 and (not isinstance(tl.m, int) or tl.m >= 1):
                    if kind == "f":
                        eng.wait_ge(s["u_ready"], tl.count(2, -2))
                    else:
                        eng.wait_ge(s["ug_ready"], tl.count(1, -1))
                eng.tensor_tensor(where[:, tl.b, part], pr_ps[bank][:, :], bias[:, part], ALU.add).then_inc(pr_read[bank], 1)

            def decayed(tl, n_):
                bank, before = turn(tl, ("qk", n_))
                eng.wait_ge(t_full[bank], before + 1)
                if n_ == 0:
                    eng.wait_ge(s["o_full"], tl.count(2))
                heads = slice(8 * (n_ // 2) + n_ % 2, 8 * (n_ // 2) + 8, 2)
                eng.tensor_tensor(pT[:, heads, :], t_ps[bank][:, :].rearrange("p (h t) -> p h t", h=4),
                                  decay[:, heads, :], ALU.mult).then_inc(t_read[bank], 1)

            def gate_o(tl):
                for half in range(2):
                    part = slice(half * G, (half + 1) * G)
                    eng.wait_ge(s["o_full"], tl.count(2, half + 1))
                    eng.wait_ge(s["f_ready"], tl.count(1, 1))
                    eng.scalar_tensor_tensor(u[:, part], f[:, tl.b, part], 1.0, o_ps[half][:, :], ALU.add, ALU.mult).then_inc(s["u_ready"], 1)

            def new_state(tl):
                eng.wait_ge(s["state_full"], tl.count(1, 1))
                eng.wait_ge(s["faded_ready"], tl.count(1, 1))
                for half in range(2):
                    rows = slice(half * D, (half + 1) * D)
                    ps = s_ps[rows, :].rearrange("p (r e) -> p r e", r=NP)
                    cols = slice(half * D, (half + 1) * D)
                    eng.tensor_tensor(state[rows, tl.b, :, cols], ps, faded[rows, :, cols], ALU.add).then_inc(s["state_ready"], 1)

            def sum_squares(tl, where, sq, ready, done):
                eng.wait_ge(s[ready], tl.count(1, 1))
                eng.tensor_reduce(where, by_head(sq[:, :]), AX.X, ALU.add).then_inc(s[done], 1)

            def guard(tl, where, summed, factor, ready):
                eng.wait_ge(s[summed], tl.count(1, 1))
                eng.tensor_scalar(where, where, L2_EPS ** 2, factor, ALU.max, ALU.mult).then_inc(s[ready], 1)

            def gate_u(tl):
                eng.wait_ge(s["g_ready"], tl.count(1, 1))
                eng.wait_ge(s["usq_ready"], tl.count(1, 1))
                eng.scalar_tensor_tensor(u[:, :], gate[:, tl.b, :], 1.0, u[:, :], ALU.add, ALU.mult).then_inc(s["ug_ready"], 1)

            def residual(tl):
                eng.wait_ge(s["y_full"], tl.count(1, 1))
                xs = X[:, bass.ds(tl.x, 1), :]
                eng.tensor_tensor(xs, m_ps[:, 0:P].rearrange("p (t c) -> p t c", t=1), xs, ALU.add).then_inc(s["x_ready"], 1)

            def step(tl):
                nxt, prv = tl.later(1), tl.later(-1)
                if exists(nxt):
                    add_bias(nxt, ("f", 0))
                if exists(prv) and carries(prv):
                    new_state(prv)
                if exists(nxt):
                    add_bias(nxt, ("f", 1))
                if exists(tl.later(2)):
                    norm.normalize(eng, tl.later(2))
                if exists(nxt):
                    add_bias(nxt, ("g", 0))
                decayed(tl, 0)
                decayed(tl, 1)
                if exists(nxt):
                    add_bias(nxt, ("g", 1))
                decayed(tl, 2)
                decayed(tl, 3)
                if exists(nxt):
                    sum_squares(nxt, ssk[:, nxt.b, :], sq_k, "ksq_ready", "ksq_summed")
                    guard(nxt, ssk[:, nxt.b, :], "ksq_summed", 4.0, "ssk_ready")
                    if exists(prv):
                        eng.wait_ge(s["scale_step"], nxt.count(2, -3))
                    sum_squares(nxt, ssq[:, nxt.b, :], sq_q, "qsq_ready", "qsq_summed")
                    guard(nxt, ssq[:, nxt.b, :], "qsq_summed", 256 * RMS_EPS, "ssq_ready")
                if exists(tl.later(3)):
                    norm.moments(eng, tl.later(3))
                gate_o(tl)
                if exists(prv):
                    residual(prv)
                sum_squares(tl, ssu[:, :], sq_u, "usq_ready", "ssu_ready")
                gate_u(tl)

            eng.sem_inc(s["x_ready"], 1)
            eng.sem_inc(s["state_ready"], STATE_START)
            norm.moments(eng, Tile(0, 2))
            for job in (("f", 0), ("f", 1), ("g", 0), ("g", 1)):
                add_bias(Tile(0, 0), job)
            sum_squares(Tile(0, 0), ssk[:, 0, :], sq_k, "ksq_ready", "ksq_summed")
            guard(Tile(0, 0), ssk[:, 0, :], "ksq_summed", 4.0, "ssk_ready")
            sum_squares(Tile(0, 0), ssq[:, 0, :], sq_q, "qsq_ready", "qsq_summed")
            guard(Tile(0, 0), ssq[:, 0, :], "qsq_summed", 256 * RMS_EPS, "ssq_ready")
            run_steps(eng, step)
            next_norm.first_vector(eng)
            residual(Tile(0, LAST))

        @block.scalar
        def _(eng):
            def copy_x(tl):
                eng.wait_ge(s["x_turned"], tl.count(1, 1))
                eng.activation(xT[:, tl.b, :], m_ps[:, 0:P], ACT.Copy).then_inc(s["xt_ready"], 1)
                eng.activation(x_hi[:, tl.b, :], m_ps[:, 0:P], ACT.Copy).then_inc(s["xt_ready"], 1)

            def silu(tl, job):
                bank, before = proj(tl, job)
                kind, half = job
                eng.wait_ge(pr_full[bank], before + 1)
                where = {"q": q, "k": k, "v": v}[kind]
                eng.activation(where[:, tl.b, half * G:(half + 1) * G], pr_ps[bank][:, :], ACT.Silu).then_inc(pr_read[bank], 1)

            def tanh(tl, where, kind, ready):
                projected(eng, tl, kind, 1)
                eng.activation(where[:, tl.b, :], where[:, tl.b, :], ACT.Tanh, scale=0.5).then_inc(s[ready], 1)

            def copy_turned(tl, job, where):
                bank, before = turn(tl, job)
                half = job[1]
                eng.wait_ge(t_full[bank], before + 1)
                eng.activation(where[:, 4 * half:4 * half + 4, :], t_ps[bank][:, :].rearrange("p (r t) -> p r t", r=4),
                               ACT.Copy).then_inc(t_read[bank], 1)

            def beta_tanh(tl):
                eng.wait_ge(s["beta_full"], tl.count(1, 1))
                eng.activation(beta[:, tl.b, :], m_ps[:, 0:H], ACT.Tanh, scale=0.5).then_inc(s["beta_ready"], 1)

            def square_q(tl):
                projected(eng, tl, "q", 1)
                if not isinstance(tl.m, int) or tl.m >= 1:
                    eng.wait_ge(s["qsq_summed"], tl.count(1))
                eng.activation(sq_q[:, :], q[:, tl.b, :], ACT.Square).then_inc(s["qsq_ready"], 1)

            def square_k(tl):
                projected(eng, tl, "k", 1)
                if not isinstance(tl.m, int) or tl.m >= 1:
                    eng.wait_ge(s["ksq_summed"], tl.count(1))
                eng.activation(sq_k[:, :], k[:, tl.b, :], ACT.Square).then_inc(s["ksq_ready"], 1)

            def square_u(tl):
                eng.wait_ge(s["u_ready"], tl.count(2, 2))
                eng.activation(sq_u, u[:, :], ACT.Square).then_inc(s["usq_ready"], 1)

            def step(tl):
                nxt, prv = tl.later(1), tl.later(-1)
                if exists(nxt):
                    silu(nxt, ("q", 0))
                copy_turned(tl, ("qT", 0), qT)
                copy_turned(tl, ("kT", 0), kT)
                if exists(nxt):
                    silu(nxt, ("k", 0))
                copy_turned(tl, ("qT", 1), qT)
                copy_turned(tl, ("kT", 1), kT)
                if exists(nxt):
                    silu(nxt, ("q", 1))
                if exists(nxt):
                    tanh(nxt, f, "f", "f_ready")
                    silu(nxt, ("k", 1))
                if exists(tl.later(2)):
                    copy_x(tl.later(2))
                if exists(nxt):
                    square_k(nxt)
                    square_q(nxt)
                    silu(nxt, ("v", 0))
                    beta_tanh(nxt)
                    tanh(nxt, gate, "g", "g_ready")
                    silu(nxt, ("v", 1))
                if exists(prv):
                    copy_turned(prv, ("oT", 0), oT)
                    copy_turned(prv, ("oT", 1), oT)
                square_u(tl)

            start = Tile(0, 0)
            copy_x(start)
            copy_x(Tile(0, 1))
            silu(start, ("q", 0))
            silu(start, ("k", 0))
            silu(start, ("q", 1))
            tanh(start, f, "f", "f_ready")
            silu(start, ("k", 1))
            square_k(start)
            silu(start, ("v", 0))
            square_q(start)
            silu(start, ("v", 1))
            beta_tanh(start)
            tanh(start, gate, "g", "g_ready")
            run_steps(eng, step)
            end = Tile(0, LAST)
            copy_turned(end, ("oT", 0), oT)
            copy_turned(end, ("oT", 1), oT)

        @block.gpsimd
        def _(eng):
            eng.memset(mhalf[:, :], -0.5).then_inc(s["set_up"], 1)
            eng.memset(ones[:, :], 1.0).then_inc(s["set_up"], 1)
            eng.memset(state[:, :, :, :], 0.0).then_inc(s["set_up"], 1)
            eng.wait_ge(s["set_up"], 3)

            def low_x(tl):
                eng.wait_ge(s["xt_ready"], tl.count(2, 2))
                eng.tensor_tensor(x_lo[:, tl.b, :], xT[:, tl.b, :], x_hi[:, tl.b, :].bitcast(F32), ALU.subtract).then_inc(s["xlo_ready"], 1)

            def coefficients(tl):
                b = tl.b
                eng.wait_ge(s["beta_ready"], tl.count(1, 1))
                eng.tensor_tensor(beta[:, b, :], beta[:, b, :], ones[:, :], ALU.add).then_inc(s["coef_step"], 1)
                eng.wait_ge(s["ssk_ready"], tl.count(1, 1))
                eng.tensor_tensor(coef[:, b, :], ssk[:, b, :], mhalf[:, :], ALU.pow).then_inc(s["coef_step"], 1)
                eng.wait_ge(s["coef_step"], tl.count(3, 2))
                eng.tensor_tensor(coef[:, b, :], coef[:, b, :], beta[:, b, :], ALU.mult).then_inc(s["coef_step"], 1)

            def weigh(tl):
                eng.wait_ge(s["coef_step"], tl.count(3, 3))
                projected(eng, tl, "v", 0)
                projected(eng, tl, "v", 1)
                if exists(tl.later(-2)):
                    eng.wait_ge(s["state_full"], tl.count(1, -1))
                eng.tensor_tensor(by_head(vb[:, tl.b, :]), by_head(v[:, tl.b, :]), over_d(coef[:, tl.b, :]), ALU.mult).then_inc(s["vb_ready"], 1)
                eng.tensor_tensor(by_head(kd[:, tl.b, :]), by_head(k[:, tl.b, :]), over_d(decay_k[:, :]), ALU.mult).then_inc(s["kd_ready"], 1)

            def fade(tl):
                eng.wait_ge(s["state_ready"], tl.count(2, STATE_START))
                eng.tensor_tensor(faded[:, :, :], state[:, tl.b, :, :], decay_s[:, :].unsqueeze(2).broadcast_to([P, NP, P]),
                                  ALU.mult).then_inc(s["faded_ready"], 1)

            def decay_queries(tl):
                bank, before = turn(tl, ("qT", 1))
                eng.wait_ge(t_read[bank], before + 1)
                eng.tensor_tensor(qdT[:, :, :], qT[:, :, :], decay_q[:, :, :], ALU.mult).then_inc(s["qd_ready"], 1)

            def scale_u(tl):
                b = tl.b
                eng.wait_ge(s["ssu_ready"], tl.count(1, 1))
                eng.tensor_tensor(scale[:, b, :], ssq[:, b, :], ssu[:, :], ALU.add).then_inc(s["scale_step"], 1)
                eng.wait_ge(s["scale_step"], tl.count(2, 1))
                eng.tensor_tensor(scale[:, b, :], scale[:, b, :], mhalf[:, :], ALU.pow).then_inc(s["scale_step"], 1)
                eng.wait_ge(s["scale_step"], tl.count(2, 2))
                eng.wait_ge(s["ug_ready"], tl.count(1, 1))
                eng.tensor_tensor(by_head(og[:, :]), by_head(u[:, :]), over_d(scale[:, b, :]), ALU.mult).then_inc(s["og_ready"], 1)

            def step(tl):
                nxt, prv = tl.later(1), tl.later(-1)
                if exists(prv):
                    scale_u(prv)
                decay_queries(tl)
                if carries(tl):
                    fade(tl)
                if exists(tl.later(2)):
                    low_x(tl.later(2))
                if exists(nxt):
                    coefficients(nxt)
                if exists(tl.later(3)):
                    norm.inverse_roots(eng, tl.later(3))
                if exists(nxt):
                    weigh(nxt)

            for m in range(2):
                low_x(Tile(0, m))
            norm.inverse_roots(eng, Tile(0, 2))
            coefficients(Tile(0, 0))
            weigh(Tile(0, 0))
            run_steps(eng, step)
            scale_u(Tile(0, LAST))
            next_norm.first_gpsimd(eng)


def build(nc, io, out):
    ctx = ExitStack()
    with ctx:
        sb = lambda name, shape, dt=F32: ctx.enter_context(nc.sbuf_tensor(name, shape, dt))
        X = sb("X", [P, B * NT, C])
        const = sb("const", [P, C_WIDTH])
        w5_hi = sb("w5_hi", [P, 5 * HD], F32R)
        w5_lo = sb("w5_lo", [P, 5 * HD], F32R)
        sem = lambda name: ctx.enter_context(nc.semaphore(name))
        weights = FfnWeights(io, sb, sem)
        tables = LinearTables(io, const, sb, sem)
        with ExitStack() as attention:
            qk_hi = attention.enter_context(nc.sbuf_tensor("qk_hi", [P, 2 * B * T], F32R))
            qk_lo = attention.enter_context(nc.sbuf_tensor("qk_lo", [P, 2 * B * T], F32R))
            V = attention.enter_context(nc.sbuf_tensor("V", [P, B * NT, C], F32))
            qkv_phase(nc, io, X, const, qk_hi, qk_lo, V)
            attention_phase(nc, io, X, const, qk_hi, qk_lo, V, w5_hi, w5_lo, weights, tables)
        tables.make_room(sb)
        norm_1 = Norm(sb, sem, "n1_", X, GT, sb("n1_xn", [P, 2, G]))
        norm_2 = Norm(sb, sem, "n2_", X, 1, sb("n2_xn", [P, 2, P]))
        norm_3 = Norm(sb, sem, "n3_", X, GT, norm_1.xn)
        ffn_phase(nc, X, const, weights, norm_1, "f1_", tables=tables, next_norm=norm_2)
        linear_phase(nc, X, const, w5_hi, w5_lo, tables, norm_2, norm_3)
        ffn_phase(nc, X, const, weights, norm_3, "f2_", out)


def constants():
    s = np.arange(P)[:, None]
    t = np.arange(P)[None, :]
    const = np.zeros((P, C_WIDTH), np.float32)
    const[:, C_IDENT:C_IDENT + P] = s == t
    const[:, C_LAG:C_LAG + P] = np.maximum(t - 1 - s, 0)
    const[:, C_STRICT:C_STRICT + P] = s < t
    const[:, C_NEG:C_NEG + P] = np.where(t > s, NEG, 0)
    const[:, C_TPOS:C_TPOS + P] = t
    const[:, C_LEFT] = P - 1 - np.arange(P)
    half = C // 2
    freqs = np.power(np.float32(ROTARY_BASE), -np.arange(half, dtype=np.float32) / np.float32(half)).astype(np.float32)
    radians = freqs[:, None] * np.arange(T, dtype=np.float32)[None, :]
    cos, sin = np.cos(radians), np.sin(radians)
    return const, np.concatenate([cos, cos]), np.concatenate([-sin, sin])


def kernel(**inputs):
    import concourse.bacc as bacc
    from concourse.bass_utils import run_bass_kernel_spmd

    a = {n: np.asarray(v) for n, v in inputs.items()}
    const, cos, sin = constants()

    def swapped(w):
        return np.concatenate([w[:, C // 2:], w[:, :C // 2]], axis=1)

    wq, wk, wv = (a["L0_attn_a_" + n][0] for n in ("wq", "wk", "wv"))
    big = {"f": a["L0_attn_b_Wf"], "q": a["L0_attn_b_Wq"], "g": a["L0_attn_b_Wg"], "k": a["L0_attn_b_Wk"], "v": a["L0_attn_b_Wv"]}
    arrays = {
        "x": a["L0_attn_a_x"],
        "const": const,
        "cos": cos,
        "sin": sin,
        "w_qkv": np.stack([wq, swapped(wq), wk, swapped(wk), wv], axis=1),
        "wo": a["L0_attn_a_wo"][0],
        "w_ffn": np.stack([a["L0_ffn_" + n].T for n in ("W_r", "W_k", "W_v")], axis=1),
        "mu": np.stack([a["L0_ffn_mu_r"], a["L0_ffn_mu_k"]], axis=1),
        "w5": np.concatenate([big[kind][:, half * G:(half + 1) * G] for kind, half in PROJ], axis=1),
        "wb": a["L0_attn_b_Wb"],
        "w_out": a["L0_attn_b_Wo"],
        "norm_w": a["L0_attn_b_norm_w"],
        "a_log": a["L0_attn_b_A_log"],
        "a_log_pairs": a["L0_attn_b_A_log"].reshape(NP, 2).T,
        "dt_bias": a["L0_attn_b_dt_bias"],
        "bg": a["L0_attn_b_bg"],
    }
    arrays = {n: np.ascontiguousarray(v) for n, v in arrays.items()}
    nc = bacc.Bacc("TRN2", target_bir_lowering=False, num_devices=1)
    io = {n: nc.dram_tensor("in_" + n, v.shape, mybir.dt.from_np(v.dtype), kind="ExternalInput").ap() for n, v in arrays.items()}
    out = nc.dram_tensor("out", (B, T, C), F32, kind="ExternalOutput").ap()
    build(nc, io, out)
    r = run_bass_kernel_spmd(nc, [{"in_" + n: v for n, v in arrays.items()}], core_ids=[0])
    return r.results[0]["out"]
```
